# Optimizing a Trainium2 kernel written in Bass

```python
import numpy as np
import jax
import jax.numpy as jnp

def _softmax(x, axis=-1):
    return jax.nn.softmax(x, axis=axis)

def _gelu(x):
    return jax.nn.gelu(x, approximate=True)

def _silu(x):
    return jax.nn.silu(x)

def _sigmoid(x):
    return jax.nn.sigmoid(x)

def _layernorm(x, axis=-1, eps=1e-05):
    m = jnp.mean(x, axis=axis, keepdims=True)
    v = jnp.var(x, axis=axis, keepdims=True)
    return (x - m) / jnp.sqrt(v + eps)

def _scatter_add(tgt, idx, src, axis=0):
    return tgt.at[idx].add(src)

def _segment_sum(src, seg, n):
    return jax.ops.segment_sum(src, seg, n)
kernel_name = 'mk_xattn_ffn_d4_seqx_r8_1b02da'

def setup_inputs(seed: int=0):
    np.random.seed(seed)
    _w = jnp.asarray

    def _rec_inputs():
        import jax
        import jax.numpy as jnp
        _rk = jax.random.key(seed)
        x = 7.22e-05 + 1 * jax.random.normal(jax.random.fold_in(_rk, 1), (4, 512, 128), jnp.float32)
        _lenS = 512 - jax.random.randint(jax.random.fold_in(_rk, 7), (4,), 0, max(1, 512 // 4) + 1, jnp.int32)
        _lenS2 = 154 - jax.random.randint(jax.random.fold_in(_rk, 8), (4,), 0, max(1, 154 // 4) + 1, jnp.int32)
        _ctx_1024P = jax.random.normal(jax.random.fold_in(_rk, 11), (4, 16, 128), jnp.float32)
        _ctx_1024c = jax.random.dirichlet(jax.random.fold_in(_rk, 511), 0.3 * jnp.ones((16,), jnp.float32), (4, 154))
        _ctx_1024t = jnp.einsum('bsk,bkd->bsd', _ctx_1024c, _ctx_1024P)
        _ctx_1024t = _ctx_1024t * jax.lax.rsqrt(jnp.mean(jnp.square(_ctx_1024t)) + 1e-12) * 0.953939
        ctx_1024 = -0.000514642 + 1.00011 * (_ctx_1024t + 0.3 * jax.random.normal(jax.random.fold_in(_rk, 611), (4, 154, 128), jnp.float32))
        itok_BxS_0_511 = jax.random.randint(jax.random.fold_in(_rk, 12), (4, 512), 0, 64, jnp.int32)
        return (x, ctx_1024, itok_BxS_0_511)
    x, ctx_1024, itok_BxS_0_511 = _rec_inputs()

    def _L0_xattn_setup():
        import jax, jax.numpy as jnp
        import numpy as np
        Q_DIM, KV_DIM = (128, 128)
        H, HD, KVC, QC, R = (16, 64, 32, 48, 64)
        LOOKBACK = 2
        B, LQ, LK = (4, 256, 64)

        def _rope(x, pos):
            r = x.shape[-1]
            half = r // 2
            inv = 1.0 / 10000.0 ** (jnp.arange(half, dtype=jnp.float32) / half)
            ang = pos[..., None].astype(jnp.float32) * inv
            cos, sin = (jnp.cos(ang), jnp.sin(ang))
            x1, x2 = (x[..., :half], x[..., half:])
            return jnp.concatenate([x1 * cos - x2 * sin, x1 * sin + x2 * cos], axis=-1)
        key = jax.random.key(seed)
        ks = jax.random.split(key, 11)
        w = lambda k, shape: jax.random.normal(k, shape, jnp.float32) / np.sqrt(shape[0]).astype(np.float32)
        return {'q': jax.random.normal(ks[0], (B, LQ, Q_DIM), jnp.float32), 'kv': jax.random.normal(ks[1], (B, LK, KV_DIM), jnp.float32), 'seg_id': jnp.sort(jax.random.randint(ks[2], (B, LQ), 0, LK), axis=-1), 'w_kv_comp': w(ks[3], (KV_DIM, KVC)), 'w_q_down': w(ks[4], (Q_DIM, QC)), 'w_q_up': w(ks[5], (QC, H * HD)), 'w_q_rope': w(ks[6], (QC, H * R)), 'w_k_up': w(ks[7], (KVC, H * HD)), 'w_k_rope': w(ks[8], (KVC, R)), 'w_v_up': w(ks[9], (KVC, H * HD)), 'w_out': w(ks[10], (H * HD, Q_DIM))}
    _L0_xattn_all = _L0_xattn_setup()
    _L0_xattn_in = {k: v for k, v in _L0_xattn_all.items() if k in ('w_kv_comp', 'w_q_down', 'w_q_up', 'w_q_rope', 'w_k_up', 'w_k_rope', 'w_v_up', 'w_out')}
    del _L0_xattn_all

    def _L0_ffn_setup():
        import jax, jax.numpy as jnp
        import numpy as np
        EPS = 1e-05

        def _layernorm(x, w, b):
            mu = jnp.mean(x, axis=-1, keepdims=True)
            var = jnp.mean((x - mu) ** 2, axis=-1, keepdims=True)
            return (x - mu) * jax.lax.rsqrt(var + EPS) * w + b

        def _rope_tables(T, D, base=10000.0):
            inv_freq = 1.0 / base ** (jnp.arange(0, D, 2, dtype=jnp.float32) / D)
            t = jnp.arange(T, dtype=jnp.float32)
            freqs = jnp.einsum('i,j->ij', t, inv_freq)
            emb = jnp.concatenate([freqs, freqs], axis=-1)
            return (jnp.cos(emb), jnp.sin(emb))

        def _rotate_half(x):
            x1, x2 = (x[..., :x.shape[-1] // 2], x[..., x.shape[-1] // 2:])
            return jnp.concatenate([-x2, x1], axis=-1)

        def _attn(x, ln_w, ln_b, conv_w, attn_w, proj_w, n_head):
            B, T, C = x.shape
            D = C // n_head
            h = _layernorm(x, ln_w, ln_b)
            hc = jnp.transpose(h, (0, 2, 1))
            hc = jnp.pad(hc, ((0, 0), (0, 0), (2, 0)))
            hc = jax.lax.conv_general_dilated(hc, conv_w, window_strides=(1,), padding='VALID', dimension_numbers=('NCH', 'OIH', 'NCH'), feature_group_count=C)
            h = jnp.transpose(hc, (0, 2, 1))
            qkv = h @ attn_w
            q, k, v = jnp.split(qkv, 3, axis=-1)
            q = q.reshape(B, T, n_head, D)
            k = k.reshape(B, T, n_head, D)
            v = v.reshape(B, T, n_head, D)
            cos, sin = _rope_tables(T, D)
            cos = cos[None, :, None, :]
            sin = sin[None, :, None, :]
            q = q * cos + _rotate_half(q) * sin
            k = k * cos + _rotate_half(k) * sin
            scores = jnp.einsum('bqhd,bkhd->bhqk', q, k) / jnp.sqrt(jnp.float32(D))
            causal = jnp.tril(jnp.ones((T, T), dtype=bool))
            scores = jnp.where(causal, scores, jnp.float32(-1e+30))
            p = jax.nn.softmax(scores, axis=-1)
            y = jnp.einsum('bhqk,bkhd->bqhd', p, v).reshape(B, T, C)
            return y @ proj_w

        def _moe(x, ln_w, ln_b, router_w, expert_wv, expert_proj):
            h = _layernorm(x, ln_w, ln_b)
            logits = h @ router_w
            expert_idx = jnp.argmax(logits, axis=-1)
            E = router_w.shape[-1]
            out = jnp.zeros_like(x)
            for e in range(E):
                gv = h @ expert_wv[e]
                gate_raw, value = jnp.split(gv, 2, axis=-1)
                y = gate_raw * jax.nn.sigmoid(gate_raw) * value @ expert_proj[e]
                out = out + jnp.where((expert_idx == e)[..., None], y, 0.0)
            return out
        C, H, E, B, T = (128, 16, 4, 4, 128)
        Dff = 4 * C
        key = jax.random.key(seed)
        ks = jax.random.split(key, 8)
        s = 0.02
        return {'x': jax.random.normal(ks[0], (B, T, C), dtype=jnp.float32), 'ln1_w': jnp.ones((C,), jnp.float32), 'ln1_b': jnp.zeros((C,), jnp.float32), 'ln2_w': jnp.ones((C,), jnp.float32), 'ln2_b': jnp.zeros((C,), jnp.float32), 'conv_w': jax.random.normal(ks[1], (C, 1, 3), dtype=jnp.float32) * 0.1, 'attn_w': jax.random.normal(ks[2], (C, 3 * C), dtype=jnp.float32) * s, 'proj_w': jax.random.normal(ks[3], (C, C), dtype=jnp.float32) * s, 'router_w': jax.random.normal(ks[4], (C, E), dtype=jnp.float32) * s, 'expert_wv': jax.random.normal(ks[5], (E, C, 2 * Dff), dtype=jnp.float32) * s, 'expert_proj': jax.random.normal(ks[6], (E, Dff, C), dtype=jnp.float32) * s}
    _L0_ffn_all = _L0_ffn_setup()
    _L0_ffn_in = {k: v for k, v in _L0_ffn_all.items() if k in ('ln1_w', 'ln1_b', 'ln2_w', 'ln2_b', 'conv_w', 'attn_w', 'proj_w', 'router_w', 'expert_wv', 'expert_proj')}
    del _L0_ffn_all

    def _L1_xattn_setup():
        import jax, jax.numpy as jnp
        import numpy as np
        D_MODEL = 128
        NUM_HEADS = 16
        D_K = D_MODEL // NUM_HEADS
        B, N = (2, 256)
        key = jax.random.key(seed)
        ks = jax.random.split(key, 11)
        s = 1.0 / np.sqrt(D_MODEL)
        inp = {'query': jax.random.normal(ks[0], (B, N, D_MODEL), jnp.float32), 'key': jax.random.normal(ks[1], (B, N, D_MODEL), jnp.float32), 'value': jax.random.normal(ks[2], (B, N, D_MODEL), jnp.float32), 'w_q': jax.random.normal(ks[3], (D_MODEL, D_MODEL), jnp.float32) * s, 'b_q': jax.random.normal(ks[4], (D_MODEL,), jnp.float32) * s, 'w_k': jax.random.normal(ks[5], (D_MODEL, D_MODEL), jnp.float32) * s, 'b_k': jax.random.normal(ks[6], (D_MODEL,), jnp.float32) * s, 'w_v': jax.random.normal(ks[7], (D_MODEL, D_MODEL), jnp.float32) * s, 'b_v': jax.random.normal(ks[8], (D_MODEL,), jnp.float32) * s, 'w_o': jax.random.normal(ks[9], (D_MODEL, D_MODEL), jnp.float32) * s, 'b_o': jax.random.normal(ks[10], (D_MODEL,), jnp.float32) * s}
        return inp
    _L1_xattn_all = _L1_xattn_setup()
    _L1_xattn_in = {k: v for k, v in _L1_xattn_all.items() if k in ('w_q', 'b_q', 'w_k', 'b_k', 'w_v', 'b_v', 'w_o', 'b_o')}
    del _L1_xattn_all

    def _L1_ffn_setup():
        import jax, jax.numpy as jnp
        import numpy as np
        D_MODEL = 128
        DEPTH = 8
        M = 2 ** DEPTH
        N_INTERNAL = M - 1
        B, T = (8, 512)

        def _leaf_probs(gate):
            BT = gate.shape[0]
            lp = jnp.ones((BT, M), dtype=gate.dtype)
            for level in range(DEPTH):
                n = 2 ** level
                half = M // (2 * n)
                g = gate[:, n - 1:2 * n - 1]
                f = jnp.stack([1.0 - g, g], axis=-1)
                f = jnp.broadcast_to(f[..., None], (BT, n, 2, half))
                lp = lp * f.reshape(BT, M)
            return lp
        key = jax.random.key(seed)
        ks = jax.random.split(key, 7)
        x = jax.random.normal(ks[0], (B, T, D_MODEL), dtype=jnp.float32)
        Wq = jax.random.normal(ks[1], (D_MODEL, D_MODEL), dtype=jnp.float32) * 0.02
        routers = jax.random.normal(ks[2], (N_INTERNAL, D_MODEL), dtype=jnp.float32) * 0.02
        leaf_keys = jax.random.normal(ks[3], (M, D_MODEL), dtype=jnp.float32) * 0.02
        leaf_values = jax.random.normal(ks[4], (M, D_MODEL), dtype=jnp.float32) * 0.02
        Wout_w = jax.random.normal(ks[5], (D_MODEL, D_MODEL), dtype=jnp.float32) * 0.02
        Wout_b = jax.random.normal(ks[6], (D_MODEL,), dtype=jnp.float32) * 0.02
        return {'x': x, 'Wq': Wq, 'routers': routers, 'leaf_keys': leaf_keys, 'leaf_values': leaf_values, 'Wout_w': Wout_w, 'Wout_b': Wout_b}
    _L1_ffn_all = _L1_ffn_setup()
    _L1_ffn_in = {k: v for k, v in _L1_ffn_all.items() if k in ('Wq', 'routers', 'leaf_keys', 'leaf_values', 'Wout_w', 'Wout_b')}
    del _L1_ffn_all

    def _L2_xattn_setup():
        import jax, jax.numpy as jnp
        import numpy as np
        B, S, D_MODEL, H = (4, 256, 128, 16)
        D_K = D_MODEL // H

        def _split_heads(x):
            b, s, d = x.shape
            return x.reshape(b, s, H, D_K).transpose(0, 2, 1, 3)
        key = jax.random.key(seed)
        ks = jax.random.split(key, 11)
        scale_in = 1.0 / np.sqrt(D_K)
        scale_o = 1.0 / np.sqrt(D_MODEL)
        return {'Q': jax.random.normal(ks[0], (B, S, D_MODEL), jnp.float32), 'K': jax.random.normal(ks[1], (B, S, D_MODEL), jnp.float32), 'V': jax.random.normal(ks[2], (B, S, D_MODEL), jnp.float32), 'Wq': jax.random.normal(ks[3], (H, D_K, D_K), jnp.float32) * scale_in, 'bq': jnp.zeros((H, D_K), jnp.float32), 'Wk': jax.random.normal(ks[4], (H, D_K, D_K), jnp.float32) * scale_in, 'bk': jnp.zeros((H, D_K), jnp.float32), 'Wv': jax.random.normal(ks[5], (H, D_K, D_K), jnp.float32) * scale_in, 'bv': jnp.zeros((H, D_K), jnp.float32), 'Wo': jax.random.normal(ks[6], (D_MODEL, D_MODEL), jnp.float32) * scale_o, 'bo': jnp.zeros((D_MODEL,), jnp.float32)}
    _L2_xattn_all = _L2_xattn_setup()
    _L2_xattn_in = {k: v for k, v in _L2_xattn_all.items() if k in ('Wq', 'bq', 'Wk', 'bk', 'Wv', 'bv', 'Wo', 'bo')}
    del _L2_xattn_all

    def _L2_ffn_setup():
        import jax, jax.numpy as jnp
        import numpy as np
        B, T, C = (2, 256, 128)
        H, D = (16, 64)
        CR = 8
        R = C // CR
        ROPE = D // 2
        NOPE = D - ROPE
        E, K, I, S = (8, 2, 64, 1)
        THETA = 100000.0
        EPS = 1e-05

        def _rmsnorm(x, w):
            rms = jnp.sqrt(jnp.mean(x * x, axis=-1, keepdims=True) + EPS)
            return w * (x / rms)

        def _rope(xh):
            d = xh.shape[-1]
            t = jnp.arange(xh.shape[2], dtype=jnp.float32)
            freqs = 1.0 / THETA ** (jnp.arange(0, d, 2, dtype=jnp.float32) / d)
            ang = jnp.outer(t, freqs)
            cos, sin = (jnp.cos(ang), jnp.sin(ang))
            xr = xh.reshape(xh.shape[:-1] + (d // 2, 2))
            x0, x1 = (xr[..., 0], xr[..., 1])
            rot = jnp.stack([x0 * cos - x1 * sin, x0 * sin + x1 * cos], axis=-1)
            return rot.reshape(xh.shape)

        def _attention(x, Wq, Wkva, Wkvb, Wo):
            b, t, _ = x.shape
            q = (x @ Wq).reshape(b, t, H, D).transpose(0, 2, 1, 3)
            ckv = x @ Wkva
            kv_latent, k_rope = (ckv[:, :, :R], ckv[:, :, R:])
            kv = (kv_latent @ Wkvb).reshape(b, t, H, NOPE).transpose(0, 2, 1, 3)
            k_rope = jnp.broadcast_to(k_rope[:, None, :, :], (b, H, t, ROPE))
            q_nope, q_rope = (q[..., :NOPE], q[..., NOPE:])
            q = jnp.concatenate([q_nope, _rope(q_rope)], axis=-1)
            k = jnp.concatenate([kv, _rope(k_rope)], axis=-1)
            v = jnp.concatenate([kv, jnp.zeros_like(k_rope)], axis=-1)
            att = jnp.einsum('bhqd,bhkd->bhqk', q, k) / jnp.sqrt(jnp.float32(D))
            mask = jnp.tril(jnp.ones((t, t), dtype=bool))
            att = jnp.where(mask, att, jnp.float32(-jnp.inf))
            att = jax.nn.softmax(att, axis=-1)
            y = jnp.einsum('bhqk,bhkd->bhqd', att, v)
            y = y.transpose(0, 2, 1, 3).reshape(b, t, H * D)
            return y @ Wo

        def _experts(x_flat, Wg, Wu, Wd):
            g = jax.nn.silu(jnp.einsum('nc,eci->nei', x_flat, Wg))
            u = jnp.einsum('nc,eci->nei', x_flat, Wu)
            return jnp.einsum('nei,eic->nec', g * u, Wd)

        def _moe(x, Wgate, expert_bias, Wg, Wu, Wd, sWg, sWu, sWd):
            b, t, c = x.shape
            xf = x.reshape(-1, c)
            shared = jnp.mean(_experts(xf, sWg, sWu, sWd), axis=1)
            logits = xf @ Wgate + expert_bias
            probs = jax.nn.softmax(logits, axis=-1)
            topk_p, topk_i = jax.lax.top_k(probs, K)
            topk_p = topk_p / jnp.sum(topk_p, axis=-1, keepdims=True)
            comb = jnp.sum(jax.nn.one_hot(topk_i, E, dtype=xf.dtype) * topk_p[..., None], axis=1)
            routed = jnp.einsum('ne,nec->nc', comb, _experts(xf, Wg, Wu, Wd))
            return (shared + routed).reshape(b, t, c)
        key = jax.random.key(seed)
        ks = jax.random.split(key, 16)
        w = lambda k, shp: jax.random.normal(k, shp, dtype=jnp.float32) * 0.02
        return {'x': jax.random.normal(ks[0], (B, T, C), dtype=jnp.float32), 'w_ln1': jnp.ones((C,), jnp.float32), 'Wq': w(ks[1], (C, H * D)), 'Wkva': w(ks[2], (C, R + ROPE)), 'Wkvb': w(ks[3], (R, H * NOPE)), 'Wo': w(ks[4], (H * D, C)), 'w_ln2': jnp.ones((C,), jnp.float32), 'Wgate': w(ks[5], (C, E)), 'expert_bias': jnp.zeros((E,), jnp.float32), 'Wg': w(ks[6], (E, C, I)), 'Wu': w(ks[7], (E, C, I)), 'Wd': w(ks[8], (E, I, C)), 'sWg': w(ks[9], (S, C, I)), 'sWu': w(ks[10], (S, C, I)), 'sWd': w(ks[11], (S, I, C))}
    _L2_ffn_all = _L2_ffn_setup()
    _L2_ffn_in = {k: v for k, v in _L2_ffn_all.items() if k in ('w_ln1', 'Wq', 'Wkva', 'Wkvb', 'Wo', 'w_ln2', 'Wgate', 'expert_bias', 'Wg', 'Wu', 'Wd', 'sWg', 'sWu', 'sWd')}
    del _L2_ffn_all

    def _L3_xattn_setup():
        import jax, jax.numpy as jnp
        import numpy as np
        B, S, D = (2, 256, 128)
        H = 16
        DK = D // H
        key = jax.random.key(seed)
        ks = jax.random.split(key, 7)
        scale = 1.0 / np.sqrt(D)
        return {'Query': jax.random.normal(ks[0], (B, S, D), dtype=jnp.float32), 'Key': jax.random.normal(ks[1], (B, S, D), dtype=jnp.float32), 'Value': jax.random.normal(ks[2], (B, S, D), dtype=jnp.float32), 'Wq': jax.random.normal(ks[3], (D, D), dtype=jnp.float32) * scale, 'Wk': jax.random.normal(ks[4], (D, D), dtype=jnp.float32) * scale, 'Wv': jax.random.normal(ks[5], (D, D), dtype=jnp.float32) * scale, 'Wo': jax.random.normal(ks[6], (D, D), dtype=jnp.float32) * scale}
    _L3_xattn_all = _L3_xattn_setup()
    _L3_xattn_in = {k: v for k, v in _L3_xattn_all.items() if k in ('Wq', 'Wk', 'Wv', 'Wo')}
    del _L3_xattn_all

    def _L3_ffn_setup():
        import jax, jax.numpy as jnp
        import numpy as np
        INT8_MAX = 127.0

        def _absmax_scale(x, axes):
            amax = jnp.max(jnp.abs(x), axis=axes, keepdims=True)
            return jnp.maximum(amax, 1e-12) / INT8_MAX
        key = jax.random.key(seed)
        k1, k2 = jax.random.split(key)
        lhs = jax.random.normal(k1, (4, 1024, 128), dtype=jnp.float32)
        rhs = jax.random.normal(k2, (128, 128), dtype=jnp.float32)
        return {'lhs': lhs, 'rhs': rhs}
    _L3_ffn_all = _L3_ffn_setup()
    _L3_ffn_in = {k: v for k, v in _L3_ffn_all.items() if k in ('rhs',)}
    del _L3_ffn_all
    return {'x': x, 'ctx_1024': ctx_1024, 'itok_BxS_0_511': itok_BxS_0_511, 'L0_xattn_w_kv_comp': _L0_xattn_in['w_kv_comp'], 'L0_xattn_w_q_down': _L0_xattn_in['w_q_down'], 'L0_xattn_w_q_up': _L0_xattn_in['w_q_up'], 'L0_xattn_w_q_rope': _L0_xattn_in['w_q_rope'], 'L0_xattn_w_k_up': _L0_xattn_in['w_k_up'], 'L0_xattn_w_k_rope': _L0_xattn_in['w_k_rope'], 'L0_xattn_w_v_up': _L0_xattn_in['w_v_up'], 'L0_xattn_w_out': _L0_xattn_in['w_out'], 'L0_ffn_ln1_w': _L0_ffn_in['ln1_w'], 'L0_ffn_ln1_b': _L0_ffn_in['ln1_b'], 'L0_ffn_ln2_w': _L0_ffn_in['ln2_w'], 'L0_ffn_ln2_b': _L0_ffn_in['ln2_b'], 'L0_ffn_conv_w': _L0_ffn_in['conv_w'], 'L0_ffn_attn_w': _L0_ffn_in['attn_w'], 'L0_ffn_proj_w': _L0_ffn_in['proj_w'], 'L0_ffn_router_w': _L0_ffn_in['router_w'], 'L0_ffn_expert_wv': _L0_ffn_in['expert_wv'], 'L0_ffn_expert_proj': _L0_ffn_in['expert_proj'], 'L1_xattn_w_q': _L1_xattn_in['w_q'], 'L1_xattn_b_q': _L1_xattn_in['b_q'], 'L1_xattn_w_k': _L1_xattn_in['w_k'], 'L1_xattn_b_k': _L1_xattn_in['b_k'], 'L1_xattn_w_v': _L1_xattn_in['w_v'], 'L1_xattn_b_v': _L1_xattn_in['b_v'], 'L1_xattn_w_o': _L1_xattn_in['w_o'], 'L1_xattn_b_o': _L1_xattn_in['b_o'], 'L1_ffn_Wq': _L1_ffn_in['Wq'], 'L1_ffn_routers': _L1_ffn_in['routers'], 'L1_ffn_leaf_keys': _L1_ffn_in['leaf_keys'], 'L1_ffn_leaf_values': _L1_ffn_in['leaf_values'], 'L1_ffn_Wout_w': _L1_ffn_in['Wout_w'], 'L1_ffn_Wout_b': _L1_ffn_in['Wout_b'], 'L2_xattn_Wq': _L2_xattn_in['Wq'], 'L2_xattn_bq': _L2_xattn_in['bq'], 'L2_xattn_Wk': _L2_xattn_in['Wk'], 'L2_xattn_bk': _L2_xattn_in['bk'], 'L2_xattn_Wv': _L2_xattn_in['Wv'], 'L2_xattn_bv': _L2_xattn_in['bv'], 'L2_xattn_Wo': _L2_xattn_in['Wo'], 'L2_xattn_bo': _L2_xattn_in['bo'], 'L2_ffn_w_ln1': _L2_ffn_in['w_ln1'], 'L2_ffn_Wq': _L2_ffn_in['Wq'], 'L2_ffn_Wkva': _L2_ffn_in['Wkva'], 'L2_ffn_Wkvb': _L2_ffn_in['Wkvb'], 'L2_ffn_Wo': _L2_ffn_in['Wo'], 'L2_ffn_w_ln2': _L2_ffn_in['w_ln2'], 'L2_ffn_Wgate': _L2_ffn_in['Wgate'], 'L2_ffn_expert_bias': _L2_ffn_in['expert_bias'], 'L2_ffn_Wg': _L2_ffn_in['Wg'], 'L2_ffn_Wu': _L2_ffn_in['Wu'], 'L2_ffn_Wd': _L2_ffn_in['Wd'], 'L2_ffn_sWg': _L2_ffn_in['sWg'], 'L2_ffn_sWu': _L2_ffn_in['sWu'], 'L2_ffn_sWd': _L2_ffn_in['sWd'], 'L3_xattn_Wq': _L3_xattn_in['Wq'], 'L3_xattn_Wk': _L3_xattn_in['Wk'], 'L3_xattn_Wv': _L3_xattn_in['Wv'], 'L3_xattn_Wo': _L3_xattn_in['Wo'], 'L3_ffn_rhs': _L3_ffn_in['rhs']}

def reference(x, ctx_1024, itok_BxS_0_511, L0_xattn_w_kv_comp, L0_xattn_w_q_down, L0_xattn_w_q_up, L0_xattn_w_q_rope, L0_xattn_w_k_up, L0_xattn_w_k_rope, L0_xattn_w_v_up, L0_xattn_w_out, L0_ffn_ln1_w, L0_ffn_ln1_b, L0_ffn_ln2_w, L0_ffn_ln2_b, L0_ffn_conv_w, L0_ffn_attn_w, L0_ffn_proj_w, L0_ffn_router_w, L0_ffn_expert_wv, L0_ffn_expert_proj, L1_xattn_w_q, L1_xattn_b_q, L1_xattn_w_k, L1_xattn_b_k, L1_xattn_w_v, L1_xattn_b_v, L1_xattn_w_o, L1_xattn_b_o, L1_ffn_Wq, L1_ffn_routers, L1_ffn_leaf_keys, L1_ffn_leaf_values, L1_ffn_Wout_w, L1_ffn_Wout_b, L2_xattn_Wq, L2_xattn_bq, L2_xattn_Wk, L2_xattn_bk, L2_xattn_Wv, L2_xattn_bv, L2_xattn_Wo, L2_xattn_bo, L2_ffn_w_ln1, L2_ffn_Wq, L2_ffn_Wkva, L2_ffn_Wkvb, L2_ffn_Wo, L2_ffn_w_ln2, L2_ffn_Wgate, L2_ffn_expert_bias, L2_ffn_Wg, L2_ffn_Wu, L2_ffn_Wd, L2_ffn_sWg, L2_ffn_sWu, L2_ffn_sWd, L3_xattn_Wq, L3_xattn_Wk, L3_xattn_Wv, L3_xattn_Wo, L3_ffn_rhs):
    import jax
    import jax.numpy as jnp

    def _L0_xattn_ref(q, kv, seg_id, w_kv_comp, w_q_down, w_q_up, w_q_rope, w_k_up, w_k_rope, w_v_up, w_out):
        import jax, jax.numpy as jnp
        import numpy as np
        Q_DIM, KV_DIM = (128, 128)
        H, HD, KVC, QC, R = (16, 64, 32, 48, 64)
        LOOKBACK = 2
        B, LQ, LK = (4, 256, 64)

        def _rope(x, pos):
            r = x.shape[-1]
            half = r // 2
            inv = 1.0 / 10000.0 ** (jnp.arange(half, dtype=jnp.float32) / half)
            ang = pos[..., None].astype(jnp.float32) * inv
            cos, sin = (jnp.cos(ang), jnp.sin(ang))
            x1, x2 = (x[..., :half], x[..., half:])
            return jnp.concatenate([x1 * cos - x2 * sin, x1 * sin + x2 * cos], axis=-1)
        b, lq, _ = q.shape
        lk = kv.shape[1]
        kv_c = kv @ w_kv_comp
        qc = q @ w_q_down
        q_nope = (qc @ w_q_up).reshape(b, lq, H, HD)
        q_rope = (qc @ w_q_rope).reshape(b, lq, H, R)
        q_rope = _rope(q_rope, jnp.arange(lq)[None, :, None])
        k_nope = (kv_c @ w_k_up).reshape(b, lk, H, HD)
        k_rope = _rope(kv_c @ w_k_rope, jnp.arange(lk)[None, :])
        v = (kv_c @ w_v_up).reshape(b, lk, H, HD)
        scale = 1.0 / np.sqrt(HD + R).astype(np.float32)
        scores = (jnp.einsum('bqhd,bkhd->bhqk', q_nope, k_nope) + jnp.einsum('bqhr,bkr->bhqk', q_rope, k_rope)) * scale
        k_idx = jnp.arange(lk)[None, None, :]
        q_seg = seg_id[:, :, None]
        good = (k_idx <= q_seg) & (k_idx >= q_seg - LOOKBACK)
        neg = jnp.finfo(scores.dtype).min
        scores = jnp.where(good[:, None, :, :], scores, neg)
        attn = jax.nn.softmax(scores, axis=-1)
        out = jnp.einsum('bhqk,bkhd->bqhd', attn, v).reshape(b, lq, H * HD)
        return out @ w_out

    def _L0_ffn_ref(x, ln1_w, ln1_b, ln2_w, ln2_b, conv_w, attn_w, proj_w, router_w, expert_wv, expert_proj):
        import jax, jax.numpy as jnp
        import numpy as np
        EPS = 1e-05

        def _layernorm(x, w, b):
            mu = jnp.mean(x, axis=-1, keepdims=True)
            var = jnp.mean((x - mu) ** 2, axis=-1, keepdims=True)
            return (x - mu) * jax.lax.rsqrt(var + EPS) * w + b

        def _rope_tables(T, D, base=10000.0):
            inv_freq = 1.0 / base ** (jnp.arange(0, D, 2, dtype=jnp.float32) / D)
            t = jnp.arange(T, dtype=jnp.float32)
            freqs = jnp.einsum('i,j->ij', t, inv_freq)
            emb = jnp.concatenate([freqs, freqs], axis=-1)
            return (jnp.cos(emb), jnp.sin(emb))

        def _rotate_half(x):
            x1, x2 = (x[..., :x.shape[-1] // 2], x[..., x.shape[-1] // 2:])
            return jnp.concatenate([-x2, x1], axis=-1)

        def _attn(x, ln_w, ln_b, conv_w, attn_w, proj_w, n_head):
            B, T, C = x.shape
            D = C // n_head
            h = _layernorm(x, ln_w, ln_b)
            hc = jnp.transpose(h, (0, 2, 1))
            hc = jnp.pad(hc, ((0, 0), (0, 0), (2, 0)))
            hc = jax.lax.conv_general_dilated(hc, conv_w, window_strides=(1,), padding='VALID', dimension_numbers=('NCH', 'OIH', 'NCH'), feature_group_count=C)
            h = jnp.transpose(hc, (0, 2, 1))
            qkv = h @ attn_w
            q, k, v = jnp.split(qkv, 3, axis=-1)
            q = q.reshape(B, T, n_head, D)
            k = k.reshape(B, T, n_head, D)
            v = v.reshape(B, T, n_head, D)
            cos, sin = _rope_tables(T, D)
            cos = cos[None, :, None, :]
            sin = sin[None, :, None, :]
            q = q * cos + _rotate_half(q) * sin
            k = k * cos + _rotate_half(k) * sin
            scores = jnp.einsum('bqhd,bkhd->bhqk', q, k) / jnp.sqrt(jnp.float32(D))
            causal = jnp.tril(jnp.ones((T, T), dtype=bool))
            scores = jnp.where(causal, scores, jnp.float32(-1e+30))
            p = jax.nn.softmax(scores, axis=-1)
            y = jnp.einsum('bhqk,bkhd->bqhd', p, v).reshape(B, T, C)
            return y @ proj_w

        def _moe(x, ln_w, ln_b, router_w, expert_wv, expert_proj):
            h = _layernorm(x, ln_w, ln_b)
            logits = h @ router_w
            expert_idx = jnp.argmax(logits, axis=-1)
            E = router_w.shape[-1]
            out = jnp.zeros_like(x)
            for e in range(E):
                gv = h @ expert_wv[e]
                gate_raw, value = jnp.split(gv, 2, axis=-1)
                y = gate_raw * jax.nn.sigmoid(gate_raw) * value @ expert_proj[e]
                out = out + jnp.where((expert_idx == e)[..., None], y, 0.0)
            return out
        n_head = 16
        x = x + _attn(x, ln1_w, ln1_b, conv_w, attn_w, proj_w, n_head)
        x = x + _moe(x, ln2_w, ln2_b, router_w, expert_wv, expert_proj)
        return x

    def _L1_xattn_ref(query, key, value, w_q, b_q, w_k, b_k, w_v, b_v, w_o, b_o):
        import jax, jax.numpy as jnp
        import numpy as np
        D_MODEL = 128
        NUM_HEADS = 16
        D_K = D_MODEL // NUM_HEADS
        B, N = (2, 256)
        Bq, Nq, _ = query.shape
        Q = (query @ w_q.T + b_q).reshape(Bq, Nq, NUM_HEADS, D_K).transpose(0, 2, 1, 3)
        K = (key @ w_k.T + b_k).reshape(Bq, -1, NUM_HEADS, D_K).transpose(0, 2, 1, 3)
        V = (value @ w_v.T + b_v).reshape(Bq, -1, NUM_HEADS, D_K).transpose(0, 2, 1, 3)
        scores = jnp.einsum('bhqd,bhkd->bhqk', Q, K) / np.sqrt(D_K).astype(np.float32)
        attn = jax.nn.softmax(scores, axis=-1)
        ctx = jnp.einsum('bhqk,bhkd->bhqd', attn, V)
        ctx = ctx.transpose(0, 2, 1, 3).reshape(Bq, Nq, D_MODEL)
        return ctx @ w_o.T + b_o

    def _L1_ffn_ref(x, Wq, routers, leaf_keys, leaf_values, Wout_w, Wout_b):
        import jax, jax.numpy as jnp
        import numpy as np
        D_MODEL = 128
        DEPTH = 8
        M = 2 ** DEPTH
        N_INTERNAL = M - 1
        B, T = (8, 512)

        def _leaf_probs(gate):
            BT = gate.shape[0]
            lp = jnp.ones((BT, M), dtype=gate.dtype)
            for level in range(DEPTH):
                n = 2 ** level
                half = M // (2 * n)
                g = gate[:, n - 1:2 * n - 1]
                f = jnp.stack([1.0 - g, g], axis=-1)
                f = jnp.broadcast_to(f[..., None], (BT, n, 2, half))
                lp = lp * f.reshape(BT, M)
            return lp
        Bv, Tv, d = x.shape
        q = jnp.einsum('btd,ed->bte', x, Wq)
        q_flat = q.reshape(Bv * Tv, d)
        gate = jax.nn.sigmoid(q_flat @ routers.T)
        leaf_prob = _leaf_probs(gate)
        ret = (leaf_prob @ leaf_values).reshape(Bv, Tv, d)
        return jnp.einsum('btd,ed->bte', ret, Wout_w) + Wout_b

    def _L2_xattn_ref(Q, K, V, Wq, bq, Wk, bk, Wv, bv, Wo, bo):
        import jax, jax.numpy as jnp
        import numpy as np
        B, S, D_MODEL, H = (4, 256, 128, 16)
        D_K = D_MODEL // H

        def _split_heads(x):
            b, s, d = x.shape
            return x.reshape(b, s, H, D_K).transpose(0, 2, 1, 3)
        q = jnp.einsum('bhsd,hde->bhse', _split_heads(Q), Wq) + bq[None, :, None, :]
        k = jnp.einsum('bhsd,hde->bhse', _split_heads(K), Wk) + bk[None, :, None, :]
        v = jnp.einsum('bhsd,hde->bhse', _split_heads(V), Wv) + bv[None, :, None, :]
        scores = jnp.einsum('bhqd,bhkd->bhqk', q, k) / jnp.sqrt(jnp.float32(D_K))
        attn = jax.nn.softmax(scores, axis=-1)
        ctx = jnp.einsum('bhqk,bhkd->bhqd', attn, v)
        ctx = ctx.transpose(0, 2, 1, 3).reshape(Q.shape[0], Q.shape[1], D_MODEL)
        return ctx @ Wo + bo

    def _L2_ffn_ref(x, w_ln1, Wq, Wkva, Wkvb, Wo, w_ln2, Wgate, expert_bias, Wg, Wu, Wd, sWg, sWu, sWd):
        import jax, jax.numpy as jnp
        import numpy as np
        B, T, C = (2, 256, 128)
        H, D = (16, 64)
        CR = 8
        R = C // CR
        ROPE = D // 2
        NOPE = D - ROPE
        E, K, I, S = (8, 2, 64, 1)
        THETA = 100000.0
        EPS = 1e-05

        def _rmsnorm(x, w):
            rms = jnp.sqrt(jnp.mean(x * x, axis=-1, keepdims=True) + EPS)
            return w * (x / rms)

        def _rope(xh):
            d = xh.shape[-1]
            t = jnp.arange(xh.shape[2], dtype=jnp.float32)
            freqs = 1.0 / THETA ** (jnp.arange(0, d, 2, dtype=jnp.float32) / d)
            ang = jnp.outer(t, freqs)
            cos, sin = (jnp.cos(ang), jnp.sin(ang))
            xr = xh.reshape(xh.shape[:-1] + (d // 2, 2))
            x0, x1 = (xr[..., 0], xr[..., 1])
            rot = jnp.stack([x0 * cos - x1 * sin, x0 * sin + x1 * cos], axis=-1)
            return rot.reshape(xh.shape)

        def _attention(x, Wq, Wkva, Wkvb, Wo):
            b, t, _ = x.shape
            q = (x @ Wq).reshape(b, t, H, D).transpose(0, 2, 1, 3)
            ckv = x @ Wkva
            kv_latent, k_rope = (ckv[:, :, :R], ckv[:, :, R:])
            kv = (kv_latent @ Wkvb).reshape(b, t, H, NOPE).transpose(0, 2, 1, 3)
            k_rope = jnp.broadcast_to(k_rope[:, None, :, :], (b, H, t, ROPE))
            q_nope, q_rope = (q[..., :NOPE], q[..., NOPE:])
            q = jnp.concatenate([q_nope, _rope(q_rope)], axis=-1)
            k = jnp.concatenate([kv, _rope(k_rope)], axis=-1)
            v = jnp.concatenate([kv, jnp.zeros_like(k_rope)], axis=-1)
            att = jnp.einsum('bhqd,bhkd->bhqk', q, k) / jnp.sqrt(jnp.float32(D))
            mask = jnp.tril(jnp.ones((t, t), dtype=bool))
            att = jnp.where(mask, att, jnp.float32(-jnp.inf))
            att = jax.nn.softmax(att, axis=-1)
            y = jnp.einsum('bhqk,bhkd->bhqd', att, v)
            y = y.transpose(0, 2, 1, 3).reshape(b, t, H * D)
            return y @ Wo

        def _experts(x_flat, Wg, Wu, Wd):
            g = jax.nn.silu(jnp.einsum('nc,eci->nei', x_flat, Wg))
            u = jnp.einsum('nc,eci->nei', x_flat, Wu)
            return jnp.einsum('nei,eic->nec', g * u, Wd)

        def _moe(x, Wgate, expert_bias, Wg, Wu, Wd, sWg, sWu, sWd):
            b, t, c = x.shape
            xf = x.reshape(-1, c)
            shared = jnp.mean(_experts(xf, sWg, sWu, sWd), axis=1)
            logits = xf @ Wgate + expert_bias
            probs = jax.nn.softmax(logits, axis=-1)
            topk_p, topk_i = jax.lax.top_k(probs, K)
            topk_p = topk_p / jnp.sum(topk_p, axis=-1, keepdims=True)
            comb = jnp.sum(jax.nn.one_hot(topk_i, E, dtype=xf.dtype) * topk_p[..., None], axis=1)
            routed = jnp.einsum('ne,nec->nc', comb, _experts(xf, Wg, Wu, Wd))
            return (shared + routed).reshape(b, t, c)
        x = x + _attention(_rmsnorm(x, w_ln1), Wq, Wkva, Wkvb, Wo)
        residual = x
        xn = _rmsnorm(x, w_ln2)
        x_out = _moe(xn, Wgate, expert_bias, Wg, Wu, Wd, sWg, sWu, sWd)
        return residual + x_out

    def _L3_xattn_ref(Query, Key, Value, Wq, Wk, Wv, Wo):
        import jax, jax.numpy as jnp
        import numpy as np
        B, S, D = (2, 256, 128)
        H = 16
        DK = D // H
        b = Query.shape[0]
        q = (Query @ Wq.T).reshape(b, -1, H, DK).transpose(0, 2, 1, 3)
        k = (Key @ Wk.T).reshape(b, -1, H, DK).transpose(0, 2, 1, 3)
        v = (Value @ Wv.T).reshape(b, -1, H, DK).transpose(0, 2, 1, 3)
        scores = jnp.einsum('bhqd,bhkd->bhqk', q, k) / jnp.sqrt(jnp.float32(DK))
        attn = jax.nn.softmax(scores, axis=1)
        ctx = jnp.einsum('bhqk,bhkd->bhqd', attn, v)
        ctx = ctx.transpose(0, 2, 1, 3).reshape(b, -1, H * DK)
        return ctx @ Wo.T

    def _L3_ffn_ref(lhs, rhs):
        import jax, jax.numpy as jnp
        import numpy as np
        INT8_MAX = 127.0

        def _absmax_scale(x, axes):
            amax = jnp.max(jnp.abs(x), axis=axes, keepdims=True)
            return jnp.maximum(amax, 1e-12) / INT8_MAX
        lhs_scale = _absmax_scale(lhs, (2,))
        rhs_scale = _absmax_scale(rhs, (0,))
        q_lhs = jnp.clip(jnp.round(lhs / lhs_scale), -INT8_MAX, INT8_MAX).astype(jnp.int8)
        q_rhs = jnp.clip(jnp.round(rhs / rhs_scale), -INT8_MAX, INT8_MAX).astype(jnp.int8)
        acc = jax.lax.dot_general(q_lhs, q_rhs, (((2,), (0,)), ((), ())), preferred_element_type=jnp.int32)
        return acc.astype(jnp.float32) * lhs_scale * rhs_scale
    x = x + _L0_xattn_ref(_layernorm(x, axis=-1), ctx_1024, itok_BxS_0_511, L0_xattn_w_kv_comp, L0_xattn_w_q_down, L0_xattn_w_q_up, L0_xattn_w_q_rope, L0_xattn_w_k_up, L0_xattn_w_k_rope, L0_xattn_w_v_up, L0_xattn_w_out)
    x = x + _L0_ffn_ref(_layernorm(x, axis=-1), L0_ffn_ln1_w, L0_ffn_ln1_b, L0_ffn_ln2_w, L0_ffn_ln2_b, L0_ffn_conv_w, L0_ffn_attn_w, L0_ffn_proj_w, L0_ffn_router_w, L0_ffn_expert_wv, L0_ffn_expert_proj)
    x = x + _L1_xattn_ref(_layernorm(x, axis=-1), ctx_1024, ctx_1024, L1_xattn_w_q, L1_xattn_b_q, L1_xattn_w_k, L1_xattn_b_k, L1_xattn_w_v, L1_xattn_b_v, L1_xattn_w_o, L1_xattn_b_o)
    x = x + _L1_ffn_ref(_layernorm(x, axis=-1), L1_ffn_Wq, L1_ffn_routers, L1_ffn_leaf_keys, L1_ffn_leaf_values, L1_ffn_Wout_w, L1_ffn_Wout_b)
    x = x + _L2_xattn_ref(_layernorm(x, axis=-1), ctx_1024, ctx_1024, L2_xattn_Wq, L2_xattn_bq, L2_xattn_Wk, L2_xattn_bk, L2_xattn_Wv, L2_xattn_bv, L2_xattn_Wo, L2_xattn_bo)
    x = x + _L2_ffn_ref(_layernorm(x, axis=-1), L2_ffn_w_ln1, L2_ffn_Wq, L2_ffn_Wkva, L2_ffn_Wkvb, L2_ffn_Wo, L2_ffn_w_ln2, L2_ffn_Wgate, L2_ffn_expert_bias, L2_ffn_Wg, L2_ffn_Wu, L2_ffn_Wd, L2_ffn_sWg, L2_ffn_sWu, L2_ffn_sWd)
    x = x + _L3_xattn_ref(_layernorm(x, axis=-1), ctx_1024, ctx_1024, L3_xattn_Wq, L3_xattn_Wk, L3_xattn_Wv, L3_xattn_Wo)
    x = x + _L3_ffn_ref(_layernorm(x, axis=-1), L3_ffn_rhs)
    return x

_drawn_inputs = setup_inputs


def setup_inputs(seed=0):
    import zlib

    import numpy as np

    out = dict(_drawn_inputs(seed))
    spreads = {'L0_ffn_ln1_w': (1.0, 0.6),
     'L0_ffn_ln1_b': (0.0, 0.8),
     'L0_ffn_ln2_w': (1.0, 0.6),
     'L0_ffn_ln2_b': (0.0, 0.8),
     'L2_xattn_bq': (0.0, 2.0),
     'L2_xattn_bk': (0.0, 2.0),
     'L2_xattn_bv': (0.0, 0.691),
     'L2_xattn_bo': (0.0, 0.667),
     'L2_ffn_w_ln1': (1.0, 0.6),
     'L2_ffn_w_ln2': (1.0, 0.6),
     'L2_ffn_expert_bias': (0.0, 0.8)}
    factors = {'L0_ffn_conv_w': 8.0,
     'L0_ffn_attn_w': 8.0,
     'L0_ffn_proj_w': 8.0,
     'L0_ffn_router_w': 8.0,
     'L0_ffn_expert_wv': 8.0,
     'L0_ffn_expert_proj': 8.0,
     'L1_xattn_b_q': 25.787,
     'L1_xattn_b_k': 64.0,
     'L1_ffn_Wq': 39.034,
     'L1_ffn_routers': 38.632,
     'L1_ffn_leaf_values': 41.145,
     'L1_ffn_Wout_w': 39.847,
     'L1_ffn_Wout_b': 32.859,
     'L2_ffn_Wq': 8.0,
     'L2_ffn_Wkva': 8.0,
     'L2_ffn_Wkvb': 8.0,
     'L2_ffn_Wo': 8.0,
     'L2_ffn_Wgate': 8.0,
     'L2_ffn_Wg': 8.0,
     'L2_ffn_Wu': 8.0,
     'L2_ffn_Wd': 8.0,
     'L2_ffn_sWg': 8.0,
     'L2_ffn_sWu': 8.0,
     'L2_ffn_sWd': 8.0,
     'L1_xattn_w_q': 2.983,
     'L1_xattn_w_k': 2.697,
     'L1_xattn_b_v': 6.71,
     'L1_xattn_b_o': 6.621}
    for name, (base, spread) in spreads.items():
        noise = np.random.default_rng([zlib.crc32(name.encode()), seed]).standard_normal(out[name].shape)
        drawn = base * np.exp(spread * noise) if base else spread * noise
        out[name] = jnp.asarray(drawn.astype(out[name].dtype))
    for name, factor in factors.items():
        out[name] = (out[name] * factor).astype(out[name].dtype)
    return out
```

```python
from contextlib import ExitStack

import concourse.bass as bass
import numpy as np
from concourse import mybir

F32 = mybir.dt.float32
BF16 = mybir.dt.bfloat16
I32 = mybir.dt.int32
ALU = mybir.AluOpType
ACT = mybir.ActivationFunctionType
AX = mybir.AxisListType

NB, T, C = 4, 512, 128
H = 16
LK, KT = 154, 77
QT = T // 128
EPS = 1e-5
BIG = 1e30

PHASES = ["L0x", "L0f", "L1x", "L1f", "L2x", "L2f", "L3x", "L3f"]


class Count:

    def __init__(self, nc, name, per=0, ahead=0):
        self.name, self.per, self.ahead, self.n = name, per, ahead, 0
        self.sem = nc.alloc_semaphore(name)

    def up(self, n=1):
        self.n += n
        return self.sem, n

    def at(self, b, k):
        return self.sem, b * self.per + (k + self.ahead)

    def free(self, b, k):
        return self.sem, b * self.per + k

    def check(self):
        assert self.n == self.per, (self.name, "per trip", self.n, "declared", self.per)


class Phase:

    def __init__(self, nc, name):
        self.nc, self.name, self.ctx, self.counts = nc, name, ExitStack(), []

    def sb(self, name, shape, dt=F32):
        return self.ctx.enter_context(self.nc.sbuf_tensor(f"{self.name}_{name}", shape, dt))

    def count(self, name, per=0, ahead=0):
        c = Count(self.nc, f"{self.name}_{name}", per, ahead)
        self.counts.append(c)
        return c

    def done(self):
        for c in self.counts:
            if c.per:
                c.check()
        self.ctx.close()
        self.nc.clear_and_free_semaphores([c.sem for c in self.counts])
        self.nc.all_engine_barrier()


def link(eng, ins, step, b=0):
    ins.then_inc(*step.up())
    eng.wait_ge(*step.at(b, step.n))


def seq(buf, b):
    return buf[:, bass.ds(b, 1), :].rearrange("p a t -> p (a t)")


def load_all(sp, ld, pairs):
    for dst, src in pairs:
        sp.dma_start(dst, src).then_inc(*ld.up(16))


def phase_input(nc, G, D):
    ph = Phase(nc, "in")
    P = G["P"]
    xt = ph.sb("xt", [128, NB * QT, C])
    ct = ph.sb("ct", [KT, NB * 2, C])
    ld = ph.count("ld")
    x_up = ph.count("x_up")
    c_up = ph.count("c_up")
    x_moved, c_moved = ph.count("x_moved"), ph.count("c_moved")
    loads = [(xt[:], D["x"]), (ct[:], D["ctx"]), (G["ident"][:], D["ident"]), (G["identb"][:], D["identb"]),
             (G["mean"][:], D["mean"]), (G["zero"][:], D["zero"]), (G["eps"][:], D["eps"])]
    with nc.Block() as block:
        @block.sync
        def _(sp):
            load_all(sp, ld, loads)

        @block.tensor
        def _(pe):
            pe.wait_ge(*ld.at(0, 16 * len(loads)))
            for b in range(NB):
                for t in range(QT):
                    m = nc.tensor.transpose(P[:, b, t * 128:(t + 1) * 128], xt[:, b * QT + t, :], G["ident"][:])
                m.then_inc(*x_up.up())
            for i in range(NB * 2):
                m = nc.tensor.transpose(P[:, 4 + i // 6, (i % 6) * KT:(i % 6) * KT + KT], ct[:, i, :],
                                        G["ident"][0:KT, 0:KT])
            m.then_inc(*c_up.up())

        @block.vector
        def _(dve):
            for b in range(NB):
                dve.wait_ge(*x_up.at(0, b + 1))
                nc.vector.tensor_copy(G["X"][:, b, :], P[:, b, :]).then_inc(*x_moved.up())
            dve.wait_ge(*x_moved.at(0, NB))

        @block.scalar
        def _(act):
            act.wait_ge(*c_up.at(0, 1))
            nc.scalar.copy(G["CT"][:, 0:3, :], P[:, 4, 0:3 * LK].rearrange("p (b k) -> p b k", k=LK)).then_inc(*c_moved.up())
            nc.scalar.copy(G["CT"][:, 3, :], P[:, 5, 0:LK]).then_inc(*c_moved.up())
            act.wait_ge(*c_moved.at(0, 2))
    ph.done()


def phase_norm(nc, G, name, src, dst, center=True, gain=None, bias=None):
    ph = Phase(nc, name)
    P = G["P"]
    xc = ph.sb("xc", [128, NB, T]) if center else src
    sq = ph.sb("sq", [128, NB, T])
    rs = ph.sb("rs", [128, NB, T])
    step, ld = ph.count("step"), ph.count("ld")
    given = [v for v in (gain, bias) if v is not None]
    cols = [ph.sb(f"col{n}", [128, 1]) for n in range(len(given))]
    gain, bias = ([c[:, 0:1] for c in cols] + [None, None])[:2]
    mean_up, cent, squared, var_up, ln, rstd, out = (
        ph.count(n) for n in ("mean_up", "cent", "squared", "var_up", "ln", "rstd", "out"))
    with nc.Block() as block:
        @block.sync
        def _(sp):
            load_all(sp, ld, [(c[:], v) for c, v in zip(cols, given)])

        @block.tensor
        def _(pe):
            if center:
                for b in range(NB):
                    nc.tensor.matmul(P[:, b, :], G["mean"][:], src[:, b, :], start=True, stop=True).then_inc(*mean_up.up())
            for b in range(NB):
                pe.wait_ge(*squared.at(0, b + 1))
                nc.tensor.matmul(P[:, 4 + b, :], G["mean"][:], sq[:, b, :], start=True, stop=True).then_inc(*var_up.up())

        @block.vector
        def _(dve):
            if center:
                for b in range(NB):
                    dve.wait_ge(*mean_up.at(0, b + 1))
                    nc.vector.tensor_tensor(xc[:, b, :], src[:, b, :], P[:, b, :], ALU.subtract).then_inc(*cent.up())
            if given:
                dve.wait_ge(*ld.at(0, 16 * len(given)))
            for b in range(NB):
                dve.wait_ge(*rstd.at(0, b + 1))
                if center:
                    dve.wait_ge(*cent.at(0, b + 1))
                if gain is None:
                    nc.vector.tensor_tensor(dst[:, b, :], xc[:, b, :], rs[:, b, :], ALU.mult).then_inc(*out.up())
                elif bias is None:
                    nc.vector.scalar_tensor_tensor(out=dst[:, b, :], in0=xc[:, b, :], scalar=gain, in1=rs[:, b, :],
                                                   op0=ALU.mult, op1=ALU.mult).then_inc(*out.up())
                else:
                    link(dve, nc.vector.scalar_tensor_tensor(out=dst[:, b, :], in0=xc[:, b, :], scalar=gain,
                                                             in1=rs[:, b, :], op0=ALU.mult, op1=ALU.mult), step)
                    nc.vector.tensor_scalar(dst[:, b, :], dst[:, b, :], bias, None, ALU.add).then_inc(*out.up())
            dve.wait_ge(*out.at(0, NB))

        @block.gpsimd
        def _(pool):
            for b in range(0, NB):
                if center:
                    pool.wait_ge(*cent.at(0, b + 1))
                nc.gpsimd.tensor_tensor(sq[:, b, :], xc[:, b, :], xc[:, b, :], ALU.mult).then_inc(*squared.up())

        @block.scalar
        def _(act):
            for b in range(NB):
                act.wait_ge(*var_up.at(0, b + 1))
                nc.scalar.activation(rs[:, b, :], P[:, 4 + b, :], ACT.Ln, bias=G["eps"][:, 0:1]).then_inc(*ln.up())
                act.wait_ge(*ln.at(0, b + 1))
                nc.scalar.activation(rs[:, b, :], rs[:, b, :], ACT.Exp, scale=-0.5).then_inc(*rstd.up())
    ph.done()


def groups_of(causal):
    out = []
    for g in range(4):
        units = []
        for h in range(4 * g, 4 * g + 4):
            if not causal:
                units += [[(h, kt, 0, T, 0)] for kt in range(2)]
                continue
            units.append([(h, 0, 0, 512, 0)])
            units.append([(h, 1, 128, 384, 0), (h, 3, 384, 128, 384)])
            if h % 2:
                units.append([(h - 1, 2, 256, 256, 0), (h, 2, 256, 256, 256)])
        out.append(units)
    return out


class Attention:

    def __init__(self, ph, G, causal, parts, den_pass, mask=False):
        self.ph, self.G, self.nc, self.causal, self.parts, self.den_pass, self.mask = (
            ph, G, ph.nc, causal, parts, den_pass, mask)
        self.nk = 128 if causal else KT
        self.nkt = 4 if causal else 2
        self.keys = T if causal else LK
        self.groups = groups_of(causal)
        self.per_group = len(self.groups[0])
        self.kper = 1 if causal else 3
        self.kbanks = -(-H // self.kper)
        self.nsel = 8 + self.kbanks if parts else 0
        ns = QT * self.kbanks
        c = ph.count
        self.ring_full = c("ring_full", self.nsel + 4 * self.per_group)
        self.ring_done = c("ring_done", self.nsel + 4 * self.per_group, 4)
        self.s_full, self.s_free = c("s_full", ns), c("s_free", ns, 2)
        self.parts_ready = c("parts_ready", 2) if parts else None
        self.nm_ready, self.mt_full, self.nmt_ready = c("nm_ready", 1), c("mt_full", 1), c("nmt_ready", 1)
        self.o_full, self.o_free = c("o_full", 4, 2), c("o_free", 5, 1)
        self.den_full = None if den_pass else c("den_full", 4)
        self.den_read = None if den_pass else c("den_read", 4)
        self.on_ready = None if den_pass else c("on_ready", 4)
        self.out_full = c("out_full", 1)
        sb = ph.sb
        if parts:
            self.qp, self.kp = sb("qp", [128, 3, T], BF16), sb("kp", [128, 3, self.keys], BF16)
            self.qs, self.ks = sb("qs", [128, 8, T], BF16), sb("ks", [128, H, self.keys], BF16)
            self.selq, self.selk = sb("selq", [128, 8, 3, 128], BF16), sb("selk", [128, H, 3, 128], BF16)
        else:
            self.qe = sb("qe", [128, H, T])
        self.selm = sb("selm", [128, H, 128], BF16)
        self.prob = sb("prob", [128, 2 * self.per_group, T])
        self.nm, self.nmr = sb("nm", [128, QT, H]), sb("nmr", [128, QT, H])
        self.nmp = sb("nmp", [128, QT, 128], BF16)
        self.nmt = sb("nmt", [128, T], BF16)
        self.osp = sb("osp", [128, 2, T])
        self.rec = sb("rec", [128, T])
        self.on = sb("on", [128, 4, T])
        self.seld = None if den_pass else sb("seld", [128, 128])
        self.wo = sb("wo", [128, 4, C])
        self.mt = G["P"][:, 7, 0:256].bitcast(BF16)

    def loads(self, D, seld=None):
        out = [(self.selm[:], D["selm"])]
        if self.parts:
            out += [(self.selq[:], D["selq"]), (self.selk[:], D["selk"])]
        if seld:
            out.append((self.seld[:], D[seld]))
        return out

    def prepare(self, dve):
        self.nc.vector.memset(self.nmp[:], 0.0).then_inc(self.s_free.sem, self.s_free.ahead)
        dve.wait_ge(self.s_free.sem, self.s_free.ahead)
        self.nc.vector.memset(self.nmr[:], 0.0).then_inc(self.o_free.sem, self.o_free.ahead)
        dve.wait_ge(self.o_free.sem, self.o_free.ahead)

    def pe_ahead(self, sem, n):
        one = self.G["identb"][0:32, 0:32]
        self.nc.tensor.matmul(self.G["P"][0:32, 7, 0:32], one, one, start=True, stop=True).then_inc(sem, n)

    def act_ahead(self, scratch):
        self.nc.scalar.copy(scratch, self.G["eps"][:, 0:1]).then_inc(self.ring_done.sem, 4)

    def first_scores_q(self, h, qt):
        if self.parts:
            return self.qs[:, h // 2, qt * 128:(qt + 1) * 128]
        return self.qe[:, h, qt * 128:(qt + 1) * 128]

    def kf(self, h, k0, n):
        return self.ks[:, h, k0:k0 + n] if self.parts else self.kfull[:, k0:k0 + n]

    def q(self, h, q0, n):
        return self.qs[:, h // 2, q0:q0 + n] if self.parts else self.qe[:, h, q0:q0 + n]

    def pe(self, pe, b):
        nc, G, P = self.nc, self.G, self.G["P"]
        mm = nc.tensor.matmul
        unit = 0
        if self.parts:
            pe.wait_ge(*self.parts_ready.at(b, 2))
            for i in range(8 + self.kbanks):
                bank = 2 + unit % 4
                pe.wait_ge(*self.ring_done.free(b, unit + 1))
                if i < 8:
                    for part in range(3):
                        m = mm(P[:, bank, :], self.selq[:, i, part, :], self.qp[:, part, :], start=part == 0, stop=part == 2)
                else:
                    for j, h in enumerate(range((i - 8) * self.kper, min(H, (i - 8) * self.kper + self.kper))):
                        for part in range(3):
                            m = mm(P[:, bank, j * self.keys:(j + 1) * self.keys], self.selk[:, h, part, :],
                                   self.kp[:, part, :], start=part == 0, stop=part == 2)
                m.then_inc(*self.ring_full.up())
                unit += 1
            pe.wait_ge(*self.ring_done.at(b, unit))
        sbank = 0
        for qt in range(QT):
            for i in range(self.kbanks):
                bank = sbank % 2
                pe.wait_ge(*self.s_free.free(b, sbank + 1))
                heads = range(i * self.kper, min(H, (i + 1) * self.kper))
                n = (qt + 1) * 128 if self.causal else LK
                if self.mask:
                    mm(P[:, bank, 0:len(heads) * n].rearrange("p (h k) -> p h k", k=n), G["identb"][:],
                       self.mask_q[:, qt:qt + 1, :].to_broadcast([128, len(heads), n]), start=True, stop=False)
                for j, h in enumerate(heads):
                    m = mm(P[:, bank, j * n:(j + 1) * n], self.first_scores_q(h, qt), self.kf(h, 0, n),
                           start=not self.mask, stop=not self.causal and (not self.mask or j == len(heads) - 1))
                if self.causal:
                    m = mm(P[:, bank, n - 128:n], G["identb"][:], self.mask_q[:], start=False, stop=True)
                m.then_inc(*self.s_full.up())
                sbank += 1
        pe.wait_ge(*self.nm_ready.at(b, 1))
        for qt in range(QT):
            m = nc.tensor.transpose(self.mt[:, qt * 128:(qt + 1) * 128], self.nmp[:, qt, :], G["identb"][:])
        m.then_inc(*self.mt_full.up())
        pe.wait_ge(*self.nmt_ready.at(b, 1))

        def scores(g):
            nonlocal unit
            for tiles in self.groups[g]:
                bank = 2 + unit % 4
                pe.wait_ge(*self.ring_done.free(b, unit + 1))
                for h, kt, q0, n, col in tiles:
                    out = P[0:self.nk, bank, col:col + n]
                    mm(out, self.kf(h, kt * self.nk, self.nk), self.q(h, q0, n), start=True, stop=False)
                    if self.causal:
                        mm(out[:, 0:128], G["identb"][:], self.mask_k[:], start=False, stop=False)
                    if self.mask:
                        mm(out, G["identb"][0:KT, 0:KT], self.mask_k[:, kt, :], start=False, stop=False)
                    m = mm(out, self.selm[:, h, 0:self.nk], self.nmt[:, q0:q0 + n], start=False, stop=True)
                m.then_inc(*self.ring_full.up())
                unit += 1

        def values(g):
            if g == 0:
                self.wait_values(pe, b)
            pe.wait_ge(*self.ring_done.at(b, self.nsel + (g + 1) * self.per_group))
            pe.wait_ge(*self.o_free.free(b, g + 1))
            where = {}
            for u, tiles in enumerate(self.groups[g]):
                for h, kt, q0, n, col in tiles:
                    where[h, kt] = ((g % 2) * self.per_group + u, q0, n, col)
            for kt in range(self.nkt):
                for bank in (6, 7)[:2 if self.den_pass else 1]:
                    for j in range(4):
                        slot, q0, n, col = where[4 * g + j, kt]
                        lhs = self.v(kt, 4 * g + j) if bank == 6 else self.ones[0:self.nk, 0:32]
                        m = mm(P[32 * j:32 * j + 32, bank, q0:q0 + n], lhs,
                               self.prob[0:self.nk, slot, col:col + n], start=kt == 0, stop=kt == self.nkt - 1)
            m.then_inc(*self.o_full.up())

        def denominators(g):
            pe.wait_ge(*self.o_free.at(b, g + 1))
            if g:
                pe.wait_ge(*self.den_read.at(b, g))
            mm(P[:, 7, :], self.seld[:], self.osp[:, g % 2, :], start=True, stop=True).then_inc(*self.den_full.up())

        scores(0)
        for g in range(4):
            if g < 3:
                scores(g + 1)
            values(g)
            if g and not self.den_pass:
                denominators(g - 1)
        if not self.den_pass:
            denominators(3)
        pe.wait_ge(*self.o_free.free(b, 5))
        for g in range(4):
            if not self.den_pass:
                pe.wait_ge(*self.on_ready.at(b, g + 1))
            m = mm(P[:, 6, :], self.wo[:, g, :], self.on[:, g, :], start=g == 0, stop=g == 3)
        m.then_inc(*self.out_full.up())

    def act(self, act, b):
        nc, P = self.nc, self.G["P"]
        unit = 0
        for i in range(self.nsel):
            act.wait_ge(*self.ring_full.at(b, unit + 1))
            bank = 2 + unit % 4
            if i < 8:
                m = nc.scalar.copy(self.qs[:, i, :], P[:, bank, :])
            else:
                h0 = (i - 8) * self.kper
                n = min(H, h0 + self.kper) - h0
                m = nc.scalar.copy(self.ks[:, h0:h0 + n, :], P[:, bank, 0:n * self.keys].rearrange("p (h k) -> p h k", k=self.keys))
            m.then_inc(*self.ring_done.up())
            unit += 1
        for g in range(4):
            act.wait_ge(*self.o_full.free(b, g + 1))
            for u in range(self.per_group):
                act.wait_ge(*self.ring_full.at(b, unit + 1))
                nc.scalar.activation(self.prob[0:self.nk, (g % 2) * self.per_group + u, :], P[0:self.nk, 2 + unit % 4, :],
                                     ACT.Exp).then_inc(*self.ring_done.up())
                unit += 1

    def dve(self, dve, b, resid, bias):
        nc, P, G, step = self.nc, self.G["P"], self.G, self.step
        sbank = 0
        for qt in range(QT):
            n = (qt + 1) * 128 if self.causal else LK
            for i in range(self.kbanks):
                h0, h1 = i * self.kper, min(H, (i + 1) * self.kper)
                dve.wait_ge(*self.s_full.at(b, sbank + 1))
                nc.vector.tensor_reduce(self.nm[:, qt, h0:h1], P[:, sbank % 2, 0:(h1 - h0) * n].rearrange("p (h k) -> p h k", k=n),
                                        AX.X, ALU.max, negate=True).then_inc(*self.s_free.up())
                sbank += 1
        dve.wait_ge(*self.s_free.at(b, sbank))
        part = [self.nmp[:, :, p * H:(p + 1) * H] for p in range(3)]
        link(dve, nc.vector.tensor_copy(part[0], self.nm[:]), step, b)
        link(dve, nc.vector.tensor_tensor(self.nmr[:], self.nm[:], part[0], ALU.subtract), step, b)
        link(dve, nc.vector.tensor_copy(part[1], self.nmr[:]), step, b)
        nc.vector.tensor_tensor(part[2], self.nmr[:], part[1], ALU.subtract).then_inc(*self.nm_ready.up())
        dve.wait_ge(*self.mt_full.at(b, 1))
        nc.vector.tensor_copy(self.nmt[:], self.mt).then_inc(*self.nmt_ready.up())

        def take(g):
            dve.wait_ge(*self.o_full.at(b, g + 1))
            if self.den_pass:
                link(dve, nc.vector.reciprocal(self.rec[:], P[:, 7, :]), step, b)
                nc.vector.tensor_tensor(self.on[:, g, :], P[:, 6, :], self.rec[:], ALU.mult).then_inc(*self.o_free.up())
            else:
                if g >= 2:
                    dve.wait_ge(*self.on_ready.at(b, g - 1))
                nc.vector.tensor_copy(self.osp[:, g % 2, :], P[:, 6, :]).then_inc(*self.o_free.up())

        def divide(g):
            dve.wait_ge(*self.den_full.at(b, g + 1))
            if g:
                dve.wait_ge(*self.on_ready.at(b, g))
            nc.vector.reciprocal(self.rec[:], P[:, 7, :]).then_inc(*self.den_read.up())
            dve.wait_ge(*self.den_read.at(b, g + 1))
            dve.wait_ge(*self.o_free.at(b, g + 1))
            nc.vector.tensor_tensor(self.on[:, g, :], self.osp[:, g % 2, :], self.rec[:], ALU.mult).then_inc(*self.on_ready.up())

        for g in range(4):
            take(g)
            if g and not self.den_pass:
                divide(g - 1)
        if not self.den_pass:
            divide(3)
        dve.wait_ge(*self.out_full.at(b, 1))
        at = seq(resid, b)
        nc.vector.scalar_tensor_tensor(out=at, in0=P[:, 6, :], scalar=bias, in1=at,
                                       op0=ALU.add, op1=ALU.add).then_inc(*self.o_free.up())


def cut(nc, dve, b, step, ps, bias, scale, full, rest, parts, ready):
    if ps is not None:
        link(dve, nc.vector.tensor_scalar(full, ps, bias, scale, ALU.add, ALU.mult), step, b)
    link(dve, nc.vector.tensor_copy(parts[:, 0, :], full), step, b)
    link(dve, nc.vector.tensor_tensor(rest, full, parts[:, 0, :], ALU.subtract), step, b)
    link(dve, nc.vector.tensor_copy(parts[:, 1, :], rest), step, b)
    nc.vector.tensor_tensor(parts[:, 2, :], rest, parts[:, 1, :], ALU.subtract).then_inc(*ready.up())


def phase_cross(nc, G, D, name):
    ph = Phase(nc, name)
    P, sb = G["P"], ph.sb
    A = Attention(ph, G, causal=False, parts=True, den_pass=False)
    A.step = step = ph.count("step", 13 - 2)
    ld = ph.count("ld")
    wq, wk, wv = sb("wq", [128, C]), sb("wk", [128, C]), sb("wv", [128, 512])
    bqt, bkt, bot, bvt = sb("bq", [128, 1]), sb("bk", [128, 1]), sb("bo", [128, 1]), sb("bv", [KT, 512])
    ctb = sb("ctb", [128, LK])
    qf, qr, kf, kr = sb("qf", [128, T]), sb("qr", [128, T]), sb("kf", [128, LK]), sb("kr", [128, LK])
    va = sb("va", [KT, 2, 512])
    A.v = lambda kt, h: va[:, kt, 32 * h:32 * h + 32]
    ctb_ready = ph.count("ctb_ready", 1)
    q_full, k_full, v_full, v_ready = (ph.count(n, k) for n, k in (("q_full", 1), ("k_full", 1), ("v_full", 2), ("v_ready", 2)))
    loads = [(wq[:], D[name + "_wq"]), (wk[:], D[name + "_wk"]), (wv[:], D[name + "_wv"]), (A.wo[:], D[name + "_wo"]),
             (bqt[:], D[name + "_bq"]), (bkt[:], D[name + "_bk"]), (bot[:], D[name + "_bo"]), (bvt[:], D[name + "_bv"]),
             ] + A.loads(D, "seld8")
    with nc.Block() as block:
        @block.sync
        def _(sp):
            load_all(sp, ld, loads)

        def pe_values(pe, b):
            for kt in range(2):
                if kt == 0:
                    pe.wait_ge(*A.o_free.free(b, 1))
                nc.tensor.matmul(P[0:KT, 6 + kt, :], ctb[:, kt * KT:(kt + 1) * KT], wv[:], start=True, stop=True)\
                    .then_inc(*v_full.up())

        A.wait_values = lambda pe, b: pe.wait_ge(*v_ready.at(b, 2))

        @block.gpsimd
        def _(pool):
            with nc.gpsimd.Fori(0, NB) as b:
                pool.wait_ge(v_full.sem, b * 2 + 1)
                nc.gpsimd.tensor_copy(ctb[:], seq(G["CT"], b)).then_inc(*ctb_ready.up())

        @block.tensor
        def _(pe):
            pe.wait_ge(*ld.at(0, 16 * len(loads)))
            A.pe_ahead(A.o_full.sem, 2)
            A.pe_ahead(v_full.sem, 1)
            with nc.tensor.Fori(0, NB) as b:
                nc.tensor.matmul(P[:, 0, :], wq[:], seq(G["Y"], b), start=True, stop=True).then_inc(*q_full.up())
                pe.wait_ge(*ctb_ready.at(b, 1))
                nc.tensor.matmul(P[:, 1, 0:LK], wk[:], ctb[:], start=True, stop=True).then_inc(*k_full.up())
                pe_values(pe, b)
                A.pe(pe, b)

        @block.scalar
        def _(act):
            A.act_ahead(G["scr"][:, 0:1])
            with nc.scalar.Fori(0, NB) as b:
                A.act(act, b)

        @block.vector
        def _(dve):
            dve.wait_ge(*ld.at(0, 16 * len(loads)))
            A.prepare(dve)
            with nc.vector.Fori(0, NB) as b:
                dve.wait_ge(*q_full.at(b, 1))
                cut(nc, dve, b, step, P[:, 0, :], bqt[:, 0:1], 8.0 ** -0.5, qf[:], qr[:], A.qp, A.parts_ready)
                dve.wait_ge(*k_full.at(b, 1))
                cut(nc, dve, b, step, P[:, 1, 0:LK], bkt[:, 0:1], 1.0, kf[:], kr[:], A.kp, A.parts_ready)
                for kt in range(2):
                    dve.wait_ge(v_full.sem, b * 2 + kt + 2)
                    nc.vector.tensor_tensor(va[:, kt, :], P[0:KT, 6 + kt, :], bvt[:], ALU.add).then_inc(*v_ready.up())
                A.dve(dve, b, G["X"], bot[:, 0:1])
    ph.done()


def phase_conv_attention(nc, G, D):
    name = "L0f"
    ph = Phase(nc, name)
    P, sb = G["P"], ph.sb
    A = Attention(ph, G, causal=True, parts=True, den_pass=False)
    A.step = step = ph.count("step", 15)
    ld = ph.count("ld")
    conv = sb("conv", [128, 3])
    wq, wqr, wk, wkr, wv = (sb(n, [128, w]) for n, w in (("wq", C), ("wqr", C), ("wk", C), ("wkr", C), ("wv", 512)))
    bvt = sb("bv", [128, 512])
    cq, sq, ck, sk = (sb(n, [128, T]) for n in ("cq", "sq", "ck", "sk"))
    A.mask_q, A.mask_k = sb("mask_q", [128, 128], BF16), sb("mask_k", [128, 128], BF16)
    hb, full, rest = sb("hb", [128, T]), sb("full", [128, T]), sb("rest", [128, T])
    va = sb("va", [128, 4, 512])
    A.v = lambda kt, h: va[:, kt, 32 * h:32 * h + 32]
    h_ready, q_full, k_full = ph.count("h_ready", 1), ph.count("q_full", 1), ph.count("k_full", 1)
    v_full, v_ready = ph.count("v_full", 4), ph.count("v_ready", 4)
    loads = [(conv[:], D["L0f_conv"]), (wq[:], D["L0f_wq"]), (wqr[:], D["L0f_wqr"]), (wk[:], D["L0f_wk"]),
             (wkr[:], D["L0f_wkr"]), (wv[:], D["L0f_wv"]), (bvt[:], D["L0f_bv"]), (A.wo[:], D["L0f_wo"]),
             (cq[:], D["L0f_cq"]), (sq[:], D["L0f_sq"]), (ck[:], D["L0f_ck"]), (sk[:], D["L0f_sk"]),
             (A.mask_q[:], D["mask_q"]), (A.mask_k[:], D["mask_k"])] + A.loads(D, "seld8")
    A.wait_values = lambda pe, b: pe.wait_ge(*v_ready.at(b, 4))
    with nc.Block() as block:
        @block.sync
        def _(sp):
            load_all(sp, ld, loads)

        @block.tensor
        def _(pe):
            mm = nc.tensor.matmul
            pe.wait_ge(*ld.at(0, 16 * len(loads)))
            A.pe_ahead(A.o_full.sem, 2)
            with nc.tensor.Fori(0, NB) as b:
                pe.wait_ge(*h_ready.at(b, 1))
                mm(P[:, 0, :], wq[:], hb[:], start=True, stop=True)
                mm(P[:, 1, :], wqr[:], hb[:], start=True, stop=True).then_inc(*q_full.up())
                pe.wait_ge(*A.o_free.free(b, 1))
                mm(P[:, 6, :], wk[:], hb[:], start=True, stop=True)
                mm(P[:, 7, :], wkr[:], hb[:], start=True, stop=True).then_inc(*k_full.up())
                for kt in range(4):
                    if kt == 0:
                        pe.wait_ge(*A.parts_ready.at(b, 1))
                    if kt >= 2:
                        pe.wait_ge(*v_ready.at(b, kt - 1))
                    mm(P[:, kt % 2, :], hb[:, kt * 128:(kt + 1) * 128], wv[:], start=True, stop=True).then_inc(*v_full.up())
                pe.wait_ge(*v_ready.at(b, 4))
                A.pe(pe, b)

        @block.scalar
        def _(act):
            A.act_ahead(G["scr"][:, 0:1])
            with nc.scalar.Fori(0, NB) as b:
                A.act(act, b)

        @block.vector
        def _(dve):
            dve.wait_ge(*ld.at(0, 16 * len(loads)))
            A.prepare(dve)
            with nc.vector.Fori(0, NB) as b:
                z = seq(G["Z"], b)
                link(dve, nc.vector.tensor_scalar(hb[:], z, conv[:, 2:3], None, ALU.mult), step, b)
                link(dve, nc.vector.scalar_tensor_tensor(out=hb[:, 1:T], in0=z[:, 0:T - 1], scalar=conv[:, 1:2],
                                                         in1=hb[:, 1:T], op0=ALU.mult, op1=ALU.add), step, b)
                nc.vector.scalar_tensor_tensor(out=hb[:, 2:T], in0=z[:, 0:T - 2], scalar=conv[:, 0:1],
                                               in1=hb[:, 2:T], op0=ALU.mult, op1=ALU.add).then_inc(*h_ready.up())
                for ready, bank, cos, sin, parts in ((q_full, 0, cq, sq, A.qp), (k_full, 6, ck, sk, A.kp)):
                    dve.wait_ge(*ready.at(b, 1))
                    if bank == 6:
                        dve.wait_ge(*A.parts_ready.at(b, 1))
                    nc.vector.tensor_tensor(full[:], P[:, bank, :], cos[:], ALU.mult)
                    link(dve, nc.vector.tensor_tensor(rest[:], P[:, bank + 1, :], sin[:], ALU.mult), step, b)
                    link(dve, nc.vector.tensor_tensor(full[:], full[:], rest[:], ALU.add), step, b)
                    cut(nc, dve, b, step, None, None, None, full[:], rest[:], parts, A.parts_ready)
                for kt in range(4):
                    dve.wait_ge(*v_full.at(b, kt + 1))
                    nc.vector.tensor_tensor(va[:, kt, :], P[:, kt % 2, :], bvt[:], ALU.add).then_inc(*v_ready.up())
                A.dve(dve, b, G["Y"], G["zero"][:, 0:1])
    ph.done()


def phase_latent(nc, G, D, name):
    window = name == "L0x"
    ph = Phase(nc, name)
    P, sb = G["P"], ph.sb
    rot, lat, up_dim = (64, 32, 64) if window else (32, 16, 32)
    per_b = 128 // rot
    A = Attention(ph, G, causal=not window, parts=False, den_pass=window, mask=window)
    A.step = step = ph.count("step", 12 if window else 4)
    ld, pre_full, pre_done = ph.count("ld"), ph.count("pre_full"), ph.count("pre_done")
    keys = A.keys
    wa, wb = sb("wa", [128, H, 128]), sb("wb", [128, H // per_b, 128])
    wqT = sb("wqT", [up_dim, H, 48 if window else 128])
    wkT = sb("wkT", [up_dim, H, lat])
    wvT = sb("wvT", [up_dim, H, 32])
    woh = sb("woh", [up_dim, H, C])
    wka, wkb, wlat = sb("wka", [128, 128]), sb("wkb", [128, 128]), sb("wlat", [128, 128 if window else lat])
    cq, sq, ck, sk = sb("cq", [128, T]), sb("sq", [128, T]), sb("ck", [128, keys]), sb("sk", [128, keys])
    src = sb("src", [128, keys])
    kf, kt_, tmp = sb("kf", [128, keys]), sb("kt", [128, keys]), sb("tmp", [rot, 2, T])
    va = sb("va", [A.nk, A.nkt, 32])
    A.kfull = kf
    A.v = lambda kt, h: va[:, kt, :]
    loads = [(t[:], D[f"{name}_{n}"]) for t, n in ((wa, "wa"), (wb, "wb"), (wqT, "wqT"), (wkT, "wkT"), (wvT, "wvT"),
             (woh, "woh"), (wka, "wka"), (wkb, "wkb"), (wlat, "wlat"), (cq, "cq"), (sq, "sq"), (ck, "ck"), (sk, "sk"))]
    loads += A.loads(D, None if window else "seld16")
    if window:
        wqd, qc, kvc = sb("wqd", [128, 128]), sb("qc", [128, T]), sb("kvc", [128, LK])
        segc_i, segr_i = sb("segc_i", [128, NB * QT], I32), sb("segr_i", [KT, NB, T], I32)
        segc, segr = sb("segc", [128, NB, QT]), sb("segr", [KT, NB, T])
        keyrow, keycol = sb("keyrow", [128, LK]), sb("keycol", [KT, 2])
        A.mask_q, A.mask_k = sb("mask_q", [128, QT, LK], BF16), sb("mask_k", [KT, 2, T], BF16)
        dq, dk = sb("dq", [128, QT, LK]), sb("dk", [KT, 2, T])
        A.ones = sb("ones", [128, 32])
        qc_full, kvc_full, qc_ready, kvc_ready = (ph.count(n, 1) for n in ("qc_full", "kvc_full", "qc_ready", "kvc_ready"))
        masks_ready = ph.count("masks_ready", 2)
        loads += [(wqd[:], D["L0x_wqd"]), (segc_i[:], D["segc"]), (segr_i[:], D["segr"]),
                  (keyrow[:], D["keyrow"]), (keycol[:], D["keycol"])]
        q_in = lambda b: qc[:]
    else:
        A.mask_q, A.mask_k = sb("mask_q", [128, 128], BF16), sb("mask_k", [128, 128], BF16)
        loads += [(A.mask_q[:], D["mask_q"]), (A.mask_k[:], D["mask_k"])]
        q_in = lambda b: src[:]
    ahead_step, ahead_done = ph.count("ahead_step"), ph.count("ahead_done")
    src_ready = ph.count("src_ready", 1)
    k_full, k_ready, v_ready = (ph.count(n, 1) for n in ("k_full", "k_ready", "v_ready"))
    v_full = ph.count("v_full", 1, 1)
    a_full, a_free = ph.count("a_full", H, 1), ph.count("a_free", H, 2)
    b_full = ph.count("b_full", H // per_b)
    src_read = v_full if window else a_full
    t_ready, qe_ready = ph.count("t_ready", H), ph.count("qe_ready", H, 2)
    A.wait_values = lambda pe, b: pe.wait_ge(*v_ready.at(b, 1))
    with nc.Block() as block:
        @block.sync
        def _(sp):
            load_all(sp, ld, loads)

        @block.gpsimd
        def _(pool):
            nc.gpsimd.memset(tmp[:], 0.0).then_inc(qe_ready.sem, 2)
            with nc.gpsimd.Fori(0, NB) as b:
                pool.wait_ge(*src_read.free(b, 1))
                nc.gpsimd.tensor_copy(src[:], seq(G["CT"] if window else G["Z"], b)).then_inc(*src_ready.up())
                for h in range(H):
                    pool.wait_ge(*t_ready.at(b, h + 1))
                    nc.gpsimd.tensor_tensor(A.qe[0:rot, h, :], A.qe[0:rot, h, :], tmp[:, h % 2, :], ALU.add)\
                        .then_inc(*qe_ready.up())

        @block.tensor
        def _(pe):
            mm = nc.tensor.matmul
            pe.wait_ge(*ld.at(0, 16 * len(loads)))
            for h in range(H):
                mm(P[0:wqT.shape[2], 0, h * lat:(h + 1) * lat], wqT[:, h, :], wkT[:, h, :], start=True, stop=True)
            for h in range(H):
                m = mm(P[32 * (h % 4):32 * (h % 4) + 32, 1, (h // 4) * C:(h // 4 + 1) * C], wvT[:, h, :], woh[:, h, :],
                       start=True, stop=True)
            m.then_inc(*pre_full.up())
            A.pe_ahead(A.o_full.sem, 2)
            A.pe_ahead(v_full.sem, 1)
            A.pe_ahead(a_full.sem, 1)
            pe.wait_ge(*pre_done.at(0, 2))
            pe.wait_ge(*ahead_done.at(0, 1))
            with nc.tensor.Fori(0, NB) as b:
                pe.wait_ge(*a_free.free(b, 2))
                if window:
                    mm(P[:, 0, :], wqd[:], seq(G["Y"], b), start=True, stop=True).then_inc(*qc_full.up())
                pe.wait_ge(*A.o_free.free(b, 1))
                pe.wait_ge(*src_ready.at(b, 1))
                if window:
                    mm(P[:, 1, 0:LK], wlat[:], src[:], start=True, stop=True).then_inc(*kvc_full.up())
                for kt in range(A.nkt):
                    m = mm(P[0:A.nk, 6, 32 * kt:32 * kt + lat], src[:, kt * A.nk:(kt + 1) * A.nk], wlat[:, 0:lat],
                           start=True, stop=True)
                m.then_inc(*v_full.up())
                if window:
                    pe.wait_ge(*kvc_ready.at(b, 1))
                ksrc = kvc if window else src
                mm(P[:, 7, 0:keys], wka[:], ksrc[:], start=True, stop=True)
                m = mm(P[:, 1, 0:keys], wkb[:], ksrc[:], start=True, stop=True)
                m.then_inc(*k_full.up())
                pe.wait_ge(*k_ready.at(b, 1))
                pe.wait_ge(*v_ready.at(b, 1))
                if window:
                    pe.wait_ge(*qc_ready.at(b, 1))
                for h in range(H):
                    if h % per_b == 0:
                        i = h // per_b
                        if i >= 2:
                            pe.wait_ge(*t_ready.at(b, per_b * (i - 1)))
                        mm(P[:, 6 + i % 2, :], wb[:, i, :], q_in(b), start=True, stop=True).then_inc(*b_full.up())
                    pe.wait_ge(*a_free.free(b, h + 1))
                    m = mm(P[:, h % 2, :], wa[:, h, :], q_in(b), start=True, stop=True)
                    m.then_inc(*a_full.up())
                pe.wait_ge(*qe_ready.at(b, H))
                if window:
                    pe.wait_ge(*masks_ready.at(b, 2))
                A.pe(pe, b)

        @block.scalar
        def _(act):
            A.act_ahead(G["scr"][:, 0:1])
            act.wait_ge(*pre_full.at(0, 1))
            nc.scalar.copy(wa[0:wqT.shape[2], :, rot:rot + lat], P[0:wqT.shape[2], 0, 0:H * lat].rearrange("p (h r) -> p h r", r=lat))\
                .then_inc(*pre_done.up())
            nc.scalar.copy(A.wo[:], P[:, 1, :].rearrange("p (g c) -> p g c", c=C)).then_inc(*pre_done.up())
            with nc.scalar.Fori(0, NB) as b:
                if window:
                    act.wait_ge(*qc_full.at(b, 1))
                    nc.scalar.copy(qc[:], P[:, 0, :]).then_inc(*qc_ready.up())
                    act.wait_ge(*kvc_full.at(b, 1))
                    nc.scalar.copy(kvc[:], P[:, 1, 0:LK]).then_inc(*kvc_ready.up())
                act.wait_ge(*v_full.at(b, 1))
                nc.scalar.copy(va[:, :, 0:lat], P[0:A.nk, 6, 0:32 * A.nkt].rearrange("p (k r) -> p k r", r=32)[:, :, 0:lat])\
                    .then_inc(*v_ready.up())
                A.act(act, b)

        @block.vector
        def _(dve):
            dve.wait_ge(*ld.at(0, 16 * len(loads)))
            A.prepare(dve)
            nc.vector.memset(kt_[:, 0:1], 0.0).then_inc(a_free.sem, 2)
            dve.wait_ge(a_free.sem, 2)
            if window:
                link(dve, nc.vector.tensor_copy(segc[:].rearrange("p b t -> p (b t)"), segc_i[:]), ahead_step)
                link(dve, nc.vector.tensor_copy(segr[:], segr_i[:]), ahead_step)
                nc.vector.memset(A.ones[:], 1.0).then_inc(*ahead_done.up())
            else:
                link(dve, nc.vector.memset(va[:, :, lat:32], 0.0), ahead_step)
                nc.vector.memset(va[:, :, lat:lat + 1], 1.0).then_inc(*ahead_done.up())
            dve.wait_ge(*ahead_done.at(0, 1))
            with nc.vector.Fori(0, NB) as b:
                if window:
                    sg = segc[:, bass.ds(b, 1), :].rearrange("p a t -> p (a t)")
                    for qt in range(QT):
                        m = nc.vector.tensor_scalar(dq[:, qt, :], keyrow[:], sg[:, qt:qt + 1], None, ALU.subtract)
                    link(dve, m, step, b)
                    link(dve, nc.vector.tensor_tensor(dq[:], dq[:], dq[:], ALU.mult), step, b)
                    nc.vector.tensor_scalar(A.mask_q[:], dq[:], 1.5, -BIG, ALU.is_gt, ALU.mult).then_inc(*masks_ready.up())
                    for kt in range(2):
                        m = nc.vector.tensor_scalar(dk[:, kt, :], seq(segr, b), keycol[:, kt:kt + 1], None, ALU.subtract)
                    link(dve, m, step, b)
                    link(dve, nc.vector.tensor_tensor(dk[:], dk[:], dk[:], ALU.mult), step, b)
                    nc.vector.tensor_scalar(A.mask_k[:], dk[:], 1.5, -BIG, ALU.is_gt, ALU.mult).then_inc(*masks_ready.up())
                dve.wait_ge(*k_full.at(b, 1))
                nc.vector.tensor_tensor(kf[:], P[:, 7, 0:keys], ck[:], ALU.mult)
                link(dve, nc.vector.tensor_tensor(kt_[:], P[:, 1, 0:keys], sk[:], ALU.mult), step, b)
                nc.vector.tensor_tensor(kf[:], kf[:], kt_[:], ALU.add).then_inc(*k_ready.up())
                for h in range(H):
                    if h % per_b == 0:
                        dve.wait_ge(*b_full.at(b, h // per_b + 1))
                    dve.wait_ge(*a_full.at(b, h + 1))
                    nc.vector.tensor_tensor(A.qe[:, h, :], P[:, h % 2, :], cq[:], ALU.mult).then_inc(*a_free.up())
                    dve.wait_ge(*qe_ready.free(b, h + 1))
                    j = h % per_b
                    m = nc.vector.tensor_tensor(tmp[:, h % 2, :], P[rot * j:rot * j + rot, 6 + (h // per_b) % 2, :],
                                                sq[rot * j:rot * j + rot, :], ALU.mult)
                    m.then_inc(*t_ready.up())
                A.dve(dve, b, G["X"] if window else G["Y"], G["zero"][:, 0:1])
    ph.done()


def one_hot_of_max(nc, dve, b, step, logits, mx, eq, prio, top, hot, E):
    wide = [128, QT, E]
    link(dve, nc.vector.tensor_reduce(mx, logits, AX.X, ALU.max), step, b)
    link(dve, nc.vector.tensor_tensor(eq, logits, mx.unsqueeze(2).to_broadcast(wide), ALU.is_ge), step, b)
    link(dve, nc.vector.tensor_tensor(eq, eq, prio, ALU.mult), step, b)
    link(dve, nc.vector.tensor_reduce(top, eq, AX.X, ALU.max), step, b)
    return nc.vector.tensor_tensor(hot, eq, top.unsqueeze(2).to_broadcast(wide), ALU.is_equal)


def phase_experts(nc, G, D, name):
    one = name == "L0m"
    ph = Phase(nc, name)
    P, sb = G["P"], ph.sb
    E = 4 if one else 8
    NM = 4
    NC = 4 if one else 5
    step = ph.count("step", 17 if one else 26)
    ld = ph.count("ld")
    router, prio, sel = sb("router", [128, E]), sb("prio", [128, QT, E]), sb("sel", [E, NM, 128])
    if one:
        w1, w2 = sb("w1", [128, E, 1024]), sb("w2", [128, E, 4, C])
        hm = sb("hm", [128, E, T])
    else:
        w1, w2 = sb("w1", [128, NC, 2, 128]), sb("w2", [128, NC, C])
        ebias = sb("ebias", [128, QT, E])
    loads = [(router[:], D[name + "_router"]), (prio[:], D[name + "_prio"]), (sel[:], D[name + "_sel"]),
             (w1[:], D[name + "_w1"]), (w2[:], D[name + "_w2"])] + ([] if one else [(ebias[:], D["L2m_ebias"])])
    zb = sb("zb", [128, T])
    lg, eq, hot = (sb(n, [128, QT, E]) for n in ("lg", "eq", "hot"))
    lg2, hot2, e2, r2 = sb("lg2", [128, QT, E]), sb("hot2", [128, QT, E]), sb("e2", [128, QT]), sb("r2", [128, QT])
    mx, top, mx2 = sb("mx", [128, QT]), sb("top", [128, QT]), sb("mx2", [128, QT])
    hott = sb("hott", [E, T])
    me = sb("me", [128, NM, T])
    ex, rc, act_ = sb("ex", [128, 2, T]), sb("rc", [128, T]), sb("act", [128, NC, T])
    acc, prod = sb("acc", [128, T]), sb("prod", [128, T])
    n_out = E if one else 1
    zb_ready, lg_full, hot_ready, ht_full, hott_ready = (
        ph.count(n, 1, a) for n, a in (("zb_ready", 0), ("lg_full", 0), ("hot_ready", 0), ("ht_full", 0), ("hott_ready", 0)))
    gap, gap_done = ph.count("gap", 0 if one else 1), ph.count("gap_done", 0 if one else 1)
    masks_full, me_ready, hm_ready = ph.count("masks_full", NM), ph.count("me_ready", NM), ph.count("hm_ready", NM if one else 0)
    gv_full, gv_free = ph.count("gv_full", NC), ph.count("gv_free", NC, 2)
    exp_ready, act_ready = ph.count("exp_ready", NC), gv_free
    out_full, x_done = ph.count("out_full", n_out, 1), ph.count("x_done", 1, 1)
    with nc.Block() as block:
        @block.sync
        def _(sp):
            load_all(sp, ld, loads)

        @block.gpsimd
        def _(pool):
            with nc.gpsimd.Fori(0, NB) as b:
                pool.wait_ge(*out_full.free(b, 1))
                nc.gpsimd.tensor_copy(zb[:], seq(G["Z"], b)).then_inc(*zb_ready.up())
                if one:
                    pool.wait_ge(*zb_ready.at(b, 1))
                    for e in range(E):
                        pool.wait_ge(*me_ready.at(b, e + 1))
                        nc.gpsimd.tensor_tensor(hm[:, e, :], zb[:], me[:, e, :], ALU.mult).then_inc(*hm_ready.up())

        @block.tensor
        def _(pe):
            mm = nc.tensor.matmul
            pe.wait_ge(*ld.at(0, 16 * len(loads)))
            one_ = G["identb"][0:32, 0:32]
            mm(P[0:32, 7, 0:32], one_, one_, start=True, stop=True).then_inc(out_full.sem, 1)
            with nc.tensor.Fori(0, NB) as b:
                pe.wait_ge(*gv_free.free(b, 2))
                pe.wait_ge(*zb_ready.at(b, 1))
                for t in range(QT):
                    m = mm(P[:, 0, t * E:(t + 1) * E], zb[:, t * 128:(t + 1) * 128], router[:], start=True, stop=True)
                m.then_inc(*lg_full.up())
                pe.wait_ge(*hot_ready.at(b, 1))
                for t in range(QT):
                    m = nc.tensor.transpose(P[0:E, 1, t * 128:(t + 1) * 128], hot[:, t, :], G["ident"][:])
                m.then_inc(*ht_full.up())
                pe.wait_ge(*hott_ready.at(b, 1))
                pe.wait_ge(*x_done.free(b, 1))
                for n in range(NM):
                    mm(P[:, 2 + n, :], sel[:, n, :], hott[:], start=True, stop=True).then_inc(*masks_full.up())
                if not one:
                    pe.wait_ge(*me_ready.at(b, NM))
                for c in range(NC):
                    pe.wait_ge(*gv_free.free(b, c + 1))
                    for half in range(2):
                        bank = 2 * (c % 2) + half
                        if one:
                            for e in range(E):
                                if c == half == 0:
                                    pe.wait_ge(*hm_ready.at(b, e + 1))
                                lhs = w1[:, e, half * 512 + c * 128:half * 512 + c * 128 + 128]
                                m = mm(P[:, bank, :], lhs, hm[:, e, :], start=e == 0, stop=e == E - 1)
                        else:
                            m = mm(P[:, bank, :], w1[:, c, half, :], zb[:], start=True, stop=True)
                    m.then_inc(*gv_full.up())
                pe.wait_ge(*gv_free.at(b, NC))
                for e in range(n_out):
                    for c in range(NC):
                        m = mm(P[:, 4 + e, :], w2[:, e, c, :] if one else w2[:, c, :], act_[:, c, :],
                               start=c == 0, stop=c == NC - 1)
                    m.then_inc(*out_full.up())

        @block.scalar
        def _(act):
            with nc.scalar.Fori(0, NB) as b:
                if not one:
                    act.wait_ge(*gap.at(b, 1))
                    nc.scalar.activation(e2[:], mx2[:], ACT.Exp).then_inc(*gap_done.up())
                for n in range(NM):
                    act.wait_ge(*masks_full.at(b, n + 1))
                    nc.scalar.copy(me[:, n, :], P[:, 2 + n, :]).then_inc(*me_ready.up())
                for c in range(NC):
                    act.wait_ge(*gv_full.at(b, c + 1))
                    act.wait_ge(*gv_free.free(b, c + 1))
                    nc.scalar.activation(ex[:, c % 2, :], P[:, 2 * (c % 2), :], ACT.Tanh, scale=0.5).then_inc(*exp_ready.up())

        @block.vector
        def _(dve):
            dve.wait_ge(*ld.at(0, 16 * len(loads)))
            nc.vector.memset(acc[:, 0:1], 0.0).then_inc(gv_free.sem, 2)
            dve.wait_ge(gv_free.sem, 2)
            nc.vector.memset(acc[:, 0:1], 0.0).then_inc(x_done.sem, 1)
            dve.wait_ge(x_done.sem, 1)
            with nc.vector.Fori(0, NB) as b:
                dve.wait_ge(*lg_full.at(b, 1))
                ps = P[:, 0, 0:QT * E].rearrange("p (t e) -> p t e", e=E)
                if one:
                    link(dve, nc.vector.tensor_copy(lg[:], ps), step, b)
                    one_hot_of_max(nc, dve, b, step, lg[:], mx[:], eq[:], prio[:], top[:], hot[:], E)\
                        .then_inc(*hot_ready.up())
                else:
                    link(dve, nc.vector.tensor_tensor(lg[:], ps, ebias[:], ALU.add), step, b)
                    link(dve, one_hot_of_max(nc, dve, b, step, lg[:], mx[:], eq[:], prio[:], top[:], hot[:], E), step, b)
                    link(dve, nc.vector.scalar_tensor_tensor(out=lg2[:], in0=hot[:], scalar=-BIG, in1=lg[:],
                                                             op0=ALU.mult, op1=ALU.add), step, b)
                    link(dve, one_hot_of_max(nc, dve, b, step, lg2[:], mx2[:], eq[:], prio[:], top[:], hot2[:], E), step, b)
                    nc.vector.tensor_tensor(mx2[:], mx2[:], mx[:], ALU.subtract).then_inc(*gap.up())
                    dve.wait_ge(*gap_done.at(b, 1))
                    link(dve, nc.vector.tensor_scalar(r2[:], e2[:], 1.0, None, ALU.add), step, b)
                    link(dve, nc.vector.reciprocal(r2[:], r2[:]), step, b)
                    wide = [128, QT, E]
                    link(dve, nc.vector.tensor_tensor(hot2[:], hot2[:], e2[:].unsqueeze(2).to_broadcast(wide), ALU.mult), step, b)
                    link(dve, nc.vector.tensor_tensor(hot2[:], hot2[:], hot[:], ALU.add), step, b)
                    nc.vector.tensor_tensor(hot[:], hot2[:], r2[:].unsqueeze(2).to_broadcast(wide), ALU.mult).then_inc(*hot_ready.up())
                dve.wait_ge(*ht_full.at(b, 1))
                nc.vector.tensor_copy(hott[:], P[0:E, 1, :]).then_inc(*hott_ready.up())
                for c in range(NC):
                    dve.wait_ge(*exp_ready.at(b, c + 1))
                    g, v, e = P[:, 2 * (c % 2), :], P[:, 2 * (c % 2) + 1, :], ex[:, c % 2, :]
                    dve.wait_ge(*gv_free.free(b, c + 2))
                    link(dve, nc.vector.scalar_tensor_tensor(out=rc[:], in0=e, scalar=1.0, in1=g, op0=ALU.add, op1=ALU.mult), step, b)
                    if not one and c < NM:
                        link(dve, nc.vector.tensor_tensor(rc[:], rc[:], me[:, c, :], ALU.mult), step, b)
                    nc.vector.scalar_tensor_tensor(out=act_[:, c, :], in0=v, scalar=0.5, in1=rc[:], op0=ALU.mult, op1=ALU.mult)\
                        .then_inc(*gv_free.up())
                x = seq(G["X"], b)
                link(dve, nc.vector.tensor_tensor(x, x, seq(G["Y"], b), ALU.add), step, b)
                if one:
                    for e in range(E):
                        dve.wait_ge(*out_full.at(b, e + 1))
                        link(dve, nc.vector.tensor_tensor(prod[:], P[:, 4 + e, :], me[:, e, :], ALU.mult), step, b)
                        ins = nc.vector.tensor_tensor(x, x, prod[:], ALU.add)
                        if e < E - 1:
                            link(dve, ins, step, b)
                        else:
                            ins.then_inc(*x_done.up())
                else:
                    dve.wait_ge(*out_full.at(b, 1))
                    nc.vector.tensor_tensor(x, x, P[:, 4, :], ALU.add).then_inc(*x_done.up())
    ph.done()


def phase_tree(nc, G, D):
    ph = Phase(nc, "L1f")
    P, sb = G["P"], ph.sb
    N = 255
    step = ph.count("step", 10)
    ld, pre_full, pre_done = ph.count("ld"), ph.count("pre_full"), ph.count("pre_done")
    wq, rt, lvT, woT, bias = sb("wq", [128, C]), sb("rt", [128, N]), sb("lvT", [128, 256]), sb("woT", [128, C]), sb("bias", [128, 1])
    gw, lw = sb("gw", [128, N]), sb("lw", [128, 2, C])
    yb, ex, g, og = sb("yb", [128, T]), sb("ex", [128, QT, 256]), sb("g", [128, QT, 256]), sb("og", [128, QT, 256])
    lp = [sb("lp0", [128, QT, 256]), sb("lp1", [128, QT, 256])]
    lt = sb("lt", [128, 2, T])
    loads = [(wq[:], D["L1f_wq"]), (rt[:], D["L1f_rt"]), (lvT[:], D["L1f_lvT"]), (woT[:], D["L1f_woT"]), (bias[:], D["L1f_bias"])]
    yb_ready, z_full, e_ready, lp_ready, lt_full, lt_ready = (
        ph.count(n, k, a) for n, k, a in (("yb_ready", 1, 0), ("z_full", 1, 1), ("e_ready", 1, 0), ("lp_ready", 1, 0),
                                          ("lt_full", 1, 0), ("lt_ready", 1, 0)))
    y_full = ph.count("y_full", 1)
    z = P[:, 0:2, :].rearrange("p b (t n) -> p (b t) n", n=256)
    with nc.Block() as block:
        @block.sync
        def _(sp):
            load_all(sp, ld, loads)

        @block.gpsimd
        def _(pool):
            with nc.gpsimd.Fori(0, NB) as b:
                pool.wait_ge(*z_full.free(b, 1))
                nc.gpsimd.tensor_copy(yb[:], seq(G["Y"], b)).then_inc(*yb_ready.up())

        @block.tensor
        def _(pe):
            mm = nc.tensor.matmul
            pe.wait_ge(*ld.at(0, 16 * len(loads)))
            mm(P[:, 0, 0:N], wq[:], rt[:], start=True, stop=True)
            for c in range(2):
                m = mm(P[:, 1, c * C:(c + 1) * C], lvT[:, c * 128:(c + 1) * 128], woT[:], start=True, stop=True)
            m.then_inc(*pre_full.up())
            mm(P[0:32, 7, 0:32], G["identb"][0:32, 0:32], G["identb"][0:32, 0:32], start=True, stop=True).then_inc(z_full.sem, 1)
            pe.wait_ge(*pre_done.at(0, 2))
            with nc.tensor.Fori(0, NB) as b:
                pe.wait_ge(*yb_ready.at(b, 1))
                for t in range(QT):
                    m = mm(z[:, t, 0:N], yb[:, t * 128:(t + 1) * 128], gw[:], start=True, stop=True)
                m.then_inc(*z_full.up())
                pe.wait_ge(*lp_ready.at(b, 1))
                for t in range(QT):
                    for c in range(2):
                        m = nc.tensor.transpose(P[:, 2 + c, t * 128:(t + 1) * 128], lp[1][:, t, c * 128:(c + 1) * 128], G["ident"][:])
                m.then_inc(*lt_full.up())
                pe.wait_ge(*lt_ready.at(b, 1))
                for c in range(2):
                    m = mm(P[:, 4, :], lw[:, c, :], lt[:, c, :], start=c == 0, stop=c == 1)
                m.then_inc(*y_full.up())

        @block.scalar
        def _(act):
            act.wait_ge(*pre_full.at(0, 1))
            nc.scalar.copy(gw[:], P[:, 0, 0:N]).then_inc(*pre_done.up())
            nc.scalar.copy(lw[:], P[:, 1, 0:2 * C].rearrange("p (c n) -> p c n", c=2)).then_inc(*pre_done.up())
            with nc.scalar.Fori(0, NB) as b:
                act.wait_ge(*z_full.at(b, 1))
                nc.scalar.activation(ex[:, :, 0:N], z[:, :, 0:N], ACT.Tanh, scale=0.5).then_inc(*e_ready.up())
                act.wait_ge(*lt_full.at(b, 1))
                nc.scalar.copy(lt[:], P[:, 2:4, :]).then_inc(*lt_ready.up())

        @block.vector
        def _(dve):
            dve.wait_ge(*ld.at(0, 16 * len(loads)))
            with nc.vector.Fori(0, NB) as b:
                dve.wait_ge(*e_ready.at(b, 1))
                link(dve, nc.vector.tensor_scalar(g[:, :, 0:N], ex[:, :, 0:N], 0.5, 0.5, ALU.mult, ALU.add), step, b)
                link(dve, nc.vector.tensor_scalar(og[:, :, 0:N], g[:, :, 0:N], -1.0, 1.0, ALU.mult, ALU.add), step, b)
                nc.vector.tensor_copy(lp[0][:, :, 0:1], og[:, :, 0:1])
                link(dve, nc.vector.tensor_copy(lp[0][:, :, 1:2], g[:, :, 0:1]), step, b)
                for level in range(1, 8):
                    n = 2 ** level
                    old, new = lp[(level - 1) % 2][:, :, 0:n], lp[level % 2][:, :, 0:2 * n].rearrange("p t (n s) -> p t n s", s=2)
                    nc.vector.tensor_tensor(new[:, :, :, 0], old, og[:, :, n - 1:2 * n - 1], ALU.mult)
                    ins = nc.vector.tensor_tensor(new[:, :, :, 1], old, g[:, :, n - 1:2 * n - 1], ALU.mult)
                    if level < 7:
                        link(dve, ins, step, b)
                    else:
                        ins.then_inc(*lp_ready.up())
                dve.wait_ge(*y_full.at(b, 1))
                x = seq(G["X"], b)
                link(dve, nc.vector.scalar_tensor_tensor(out=x, in0=P[:, 4, :], scalar=bias[:, 0:1], in1=x,
                                                         op0=ALU.add, op1=ALU.add), step, b)
    ph.done()


def phase_over_heads(nc, G, D):
    ph = Phase(nc, "L3x")
    P, sb = G["P"], ph.sb
    NSEL, KPER = 14, 3
    step = ph.count("step", 2 * 4 + 8 * 2)
    ld = ph.count("ld")
    wq, wk, wv, wo = sb("wq", [128, C]), sb("wk", [128, C]), sb("wv", [128, 512]), sb("wo", [128, 4, C])
    selq, selk = sb("selq", [128, 8, 3, 128], BF16), sb("selk", [128, H, 3, 128], BF16)
    loads = [(wq[:], D["L3x_wq"]), (wk[:], D["L3x_wk"]), (wv[:], D["L3x_wv"]), (wo[:], D["L3x_wo"]),
             (selq[:], D["selq"]), (selk[:], D["selk"])]
    ctb = sb("ctb", [128, LK])
    qf, qr, kf, kr = sb("qf", [128, T]), sb("qr", [128, T]), sb("kf", [128, LK]), sb("kr", [128, LK])
    qp, kp = sb("qp", [128, 3, T], BF16), sb("kp", [128, 3, LK], BF16)
    qs, ks = sb("qs", [128, 8, T], BF16), sb("ks", [128, H, LK], BF16)
    va = sb("va", [KT, 2, 512])
    mx, sm = sb("mx", [KT, 128]), sb("sm", [KT, 2, 128])
    ex = sb("ex", [KT, 2, H, 128])
    pall = sb("pall", [KT, 2, H, T])
    on = sb("on", [128, 4, T])
    ctb_ready, q_full, k_full = (ph.count(n, 1) for n in ("ctb_ready", "q_full", "k_full"))
    v_full, v_ready, parts_ready = ph.count("v_full", 2, 1), ph.count("v_ready", 2), ph.count("parts_ready", 2)
    ring_full, ring_done = ph.count("ring_full", NSEL), ph.count("ring_done", NSEL, 4)
    st_full, sub_done, exp_done, sum_ready = (ph.count(n, 8) for n in ("st_full", "sub_done", "exp_done", "sum_ready"))
    p_ready = ph.count("p_ready", 8, 2)
    o_full, on_ready, out_full, x_done = ph.count("o_full", 4), ph.count("on_ready", 4), ph.count("out_full", 1), ph.count("x_done", 1, 1)
    with nc.Block() as block:
        @block.sync
        def _(sp):
            load_all(sp, ld, loads)

        @block.gpsimd
        def _(pool):
            nc.gpsimd.memset(ctb[:, 0:1], 0.0).then_inc(p_ready.sem, 2)
            pool.wait_ge(p_ready.sem, 2)
            with nc.gpsimd.Fori(0, NB) as b:
                pool.wait_ge(*v_full.free(b, 1))
                nc.gpsimd.tensor_copy(ctb[:], seq(G["CT"], b)).then_inc(*ctb_ready.up())
                for u in range(8):
                    kt, qt = divmod(u, QT)
                    pool.wait_ge(*sum_ready.at(b, u + 1))
                    nc.gpsimd.tensor_tensor(pall[:, kt, :, qt * 128:(qt + 1) * 128], ex[:, u % 2, :, :],
                                            sm[:, u % 2, :].unsqueeze(1).to_broadcast([KT, H, 128]), ALU.mult)\
                        .then_inc(*p_ready.up())

        @block.tensor
        def _(pe):
            mm = nc.tensor.matmul
            pe.wait_ge(*ld.at(0, 16 * len(loads)))
            mm(P[0:32, 7, 0:32], G["identb"][0:32, 0:32], G["identb"][0:32, 0:32], start=True, stop=True).then_inc(v_full.sem, 1)
            with nc.tensor.Fori(0, NB) as b:
                pe.wait_ge(*x_done.free(b, 1))
                mm(P[:, 0, :], wq[:], seq(G["Y"], b), start=True, stop=True).then_inc(*q_full.up())
                pe.wait_ge(*ctb_ready.at(b, 1))
                mm(P[:, 1, 0:LK], wk[:], ctb[:], start=True, stop=True).then_inc(*k_full.up())
                for kt in range(2):
                    mm(P[0:KT, 2 + kt, :], ctb[:, kt * KT:(kt + 1) * KT], wv[:], start=True, stop=True).then_inc(*v_full.up())
                pe.wait_ge(*parts_ready.at(b, 2))
                for i in range(NSEL):
                    bank = 4 + i % 4
                    pe.wait_ge(*ring_done.free(b, i + 1))
                    if i < 8:
                        for part in range(3):
                            m = mm(P[:, bank, :], selq[:, i, part, :], qp[:, part, :], start=part == 0, stop=part == 2)
                    else:
                        for j, h in enumerate(range((i - 8) * KPER, min(H, (i - 7) * KPER))):
                            for part in range(3):
                                m = mm(P[:, bank, j * LK:(j + 1) * LK], selk[:, h, part, :], kp[:, part, :],
                                       start=part == 0, stop=part == 2)
                    m.then_inc(*ring_full.up())
                pe.wait_ge(*ring_done.at(b, NSEL))
                pe.wait_ge(*v_ready.at(b, 2))
                for u in range(8):
                    kt, qt = divmod(u, QT)
                    if u:
                        pe.wait_ge(*sub_done.at(b, u))
                    for h in range(H):
                        m = mm(P[0:KT, h // 4, (h % 4) * 128:(h % 4) * 128 + 128], ks[:, h, kt * KT:(kt + 1) * KT],
                               qs[:, h // 2, qt * 128:(qt + 1) * 128], start=True, stop=True)
                    m.then_inc(*st_full.up())
                pe.wait_ge(*p_ready.at(b, 8))
                for g in range(4):
                    for kt in range(2):
                        for j in range(4):
                            h = 4 * g + j
                            m = mm(P[32 * j:32 * j + 32, 4 + g, :], va[:, kt, 32 * h:32 * h + 32], pall[:, kt, h, :],
                                   start=kt == 0, stop=kt == 1)
                    m.then_inc(*o_full.up())
                pe.wait_ge(*sub_done.at(b, 8))
                for g in range(4):
                    pe.wait_ge(*on_ready.at(b, g + 1))
                    m = mm(P[:, 0, :], wo[:, g, :], on[:, g, :], start=g == 0, stop=g == 3)
                m.then_inc(*out_full.up())

        @block.scalar
        def _(act):
            nc.scalar.copy(G["scr"][:, 0:1], G["eps"][:, 0:1]).then_inc(ring_done.sem, 4)
            with nc.scalar.Fori(0, NB) as b:
                for i in range(NSEL):
                    act.wait_ge(*ring_full.at(b, i + 1))
                    if i < 8:
                        m = nc.scalar.copy(qs[:, i, :], P[:, 4 + i % 4, :])
                    else:
                        h0, n = (i - 8) * KPER, min(H, (i - 7) * KPER) - (i - 8) * KPER
                        m = nc.scalar.copy(ks[:, h0:h0 + n, :], P[:, 4 + i % 4, 0:n * LK].rearrange("p (h k) -> p h k", k=LK))
                    m.then_inc(*ring_done.up())
                for u in range(8):
                    act.wait_ge(*sub_done.at(b, u + 1))
                    nc.scalar.activation(ex[:, u % 2, :, :], ex[:, u % 2, :, :], ACT.Exp).then_inc(*exp_done.up())
                for g in range(4):
                    act.wait_ge(*o_full.at(b, g + 1))
                    nc.scalar.copy(on[:, g, :], P[:, 4 + g, :]).then_inc(*on_ready.up())

        @block.vector
        def _(dve):
            dve.wait_ge(*ld.at(0, 16 * len(loads)))
            nc.vector.memset(mx[:, 0:1], 0.0).then_inc(x_done.sem, 1)
            dve.wait_ge(x_done.sem, 1)
            scores = P[0:KT, 0:4, :].rearrange("p b (j q) -> p (b j) q", q=128)

            def total(b, u):
                dve.wait_ge(*exp_done.at(b, u + 1))
                dve.wait_ge(*p_ready.free(b, u + 1))
                link(dve, nc.vector.tensor_reduce(sm[:, u % 2, :], ex[:, u % 2, :, :].rearrange("p h q -> p q h"), AX.X, ALU.add), step, b)
                nc.vector.reciprocal(sm[:, u % 2, :], sm[:, u % 2, :]).then_inc(*sum_ready.up())

            with nc.vector.Fori(0, NB) as b:
                dve.wait_ge(*q_full.at(b, 1))
                cut(nc, dve, b, step, P[:, 0, :], G["zero"][:, 0:1], 8.0 ** -0.5, qf[:], qr[:], qp, parts_ready)
                dve.wait_ge(*k_full.at(b, 1))
                cut(nc, dve, b, step, P[:, 1, 0:LK], G["zero"][:, 0:1], 1.0, kf[:], kr[:], kp, parts_ready)
                for kt in range(2):
                    dve.wait_ge(*v_full.at(b, kt + 1))
                    nc.vector.tensor_copy(va[:, kt, :], P[0:KT, 2 + kt, :]).then_inc(*v_ready.up())
                for u in range(8):
                    dve.wait_ge(*st_full.at(b, u + 1))
                    link(dve, nc.vector.tensor_reduce(mx[:], scores.rearrange("p h q -> p q h"), AX.X, ALU.max), step, b)
                    dve.wait_ge(*p_ready.free(b, u + 1))
                    nc.vector.tensor_tensor(ex[:, u % 2, :, :], scores, mx[:].unsqueeze(1).to_broadcast([KT, H, 128]),
                                            ALU.subtract).then_inc(*sub_done.up())
                    if u:
                        total(b, u - 1)
                    dve.wait_ge(*sub_done.at(b, u + 1))
                total(b, 7)
                dve.wait_ge(*out_full.at(b, 1))
                x = seq(G["X"], b)
                nc.vector.tensor_tensor(x, x, P[:, 0, :], ALU.add).then_inc(*x_done.up())
    ph.done()


def phase_output(nc, G, D):
    ph = Phase(nc, "out")
    P, sb = G["P"], ph.sb
    ROUND = 1.5 * 2.0 ** 23
    ld = ph.count("ld")
    rhs, rt, rs, ri, rqT, rq = (sb("rhs", [128, C]), sb("rt", [128, C]), sb("rs", [128, 1]), sb("ri", [128, 1]),
                                sb("rqT", [128, C], BF16), sb("rq", [128, C], BF16))
    diag, rsb = sb("diag", [128, 128]), sb("rsb", [128, 128])
    zb, xb = sb("zb", [128, T]), sb("xb", [128, T])
    amax, sc, inv = sb("amax", [128, QT]), sb("sc", [128, QT]), sb("inv", [128, QT])
    qz, qb, qt_ = sb("qz", [128, QT, 128]), sb("qb", [128, QT, 128], BF16), sb("qt", [128, T], BF16)
    o = sb("o", [128, NB * QT, C])
    pre, pre_pe, pstep = ph.count("pre"), ph.count("pre_pe"), ph.count("pstep")
    step = ph.count("step", 7)
    b_ready, z_full, q_ready, qt_full, qt_done = (ph.count(n, k, a) for n, k, a in (
        ("b_ready", 2, 0), ("z_full", 1, 0), ("q_ready", 1, 0), ("qt_full", 1, 0), ("qt_done", 1, 0)))
    y_full, o_ready, stored = ph.count("y_full", 1, 1), ph.count("o_ready", 1), ph.count("stored", 16)
    loads = [(rhs[:], D["L3f_rhs"])]
    qview = P[:, 1, 0:256].bitcast(BF16)
    wide = [128, QT, 128]
    with nc.Block() as block:
        @block.sync
        def _(sp):
            load_all(sp, ld, loads)
            with nc.sync.Fori(0, NB) as b:
                sp.wait_ge(*o_ready.at(b, 1))
                sp.dma_start(D["out"][:, bass.ds(b * QT, QT), :], o[:, bass.ds(b * QT, QT), :]).then_inc(*stored.up(16))
            sp.wait_ge(stored.sem, 16 * NB)

        @block.gpsimd
        def _(pool):
            with nc.gpsimd.Fori(0, NB) as b:
                pool.wait_ge(*y_full.free(b, 1))
                nc.gpsimd.tensor_copy(zb[:], seq(G["Z"], b)).then_inc(*b_ready.up())
                nc.gpsimd.tensor_copy(xb[:], seq(G["X"], b)).then_inc(*b_ready.up())

        @block.tensor
        def _(pe):
            mm = nc.tensor.matmul
            pe.wait_ge(*ld.at(0, 16 * len(loads)))
            nc.tensor.transpose(P[:, 0, 0:128], rhs[:], G["ident"][:]).then_inc(*pre_pe.up())
            pe.wait_ge(*pre.at(0, 1))
            nc.tensor.transpose(qview[:, 0:128], rqT[:], G["identb"][:])
            mm(P[:, 2, 0:128], G["mean"][:], diag[:], start=True, stop=True).then_inc(*pre_pe.up())
            mm(P[0:32, 7, 0:32], G["identb"][0:32, 0:32], G["identb"][0:32, 0:32], start=True, stop=True).then_inc(y_full.sem, 1)
            pe.wait_ge(*pre.at(0, 2))
            with nc.tensor.Fori(0, NB) as b:
                pe.wait_ge(*b_ready.at(b, 1))
                for t in range(QT):
                    m = nc.tensor.transpose(P[:, 0, t * 128:(t + 1) * 128], zb[:, t * 128:(t + 1) * 128], G["ident"][:])
                m.then_inc(*z_full.up())
                pe.wait_ge(*q_ready.at(b, 1))
                for t in range(QT):
                    m = nc.tensor.transpose(qview[:, t * 128:(t + 1) * 128], qb[:, t, :], G["identb"][:])
                m.then_inc(*qt_full.up())
                pe.wait_ge(*qt_done.at(b, 1))
                pe.wait_ge(*b_ready.at(b, 2))
                for t in range(QT):
                    mm(P[:, 2, t * 128:(t + 1) * 128], qt_[:, t * 128:(t + 1) * 128], rq[:], start=True, stop=True)
                for t in range(QT):
                    m = nc.tensor.transpose(P[:, 3, t * 128:(t + 1) * 128], xb[:, t * 128:(t + 1) * 128], G["ident"][:])
                m.then_inc(*y_full.up())

        @block.scalar
        def _(act):
            with nc.scalar.Fori(0, NB) as b:
                act.wait_ge(*qt_full.at(b, 1))
                nc.scalar.copy(qt_[:], qview).then_inc(*qt_done.up())

        @block.vector
        def _(dve):
            def plink(ins):
                link(dve, ins, pstep)
            dve.wait_ge(*pre_pe.at(0, 1))
            plink(nc.vector.tensor_reduce(rs[:], P[:, 0, 0:128], AX.X, ALU.max, apply_absolute_value=True))
            plink(nc.vector.tensor_scalar(rs[:], rs[:], 1e-12, 1.0 / 127.0, ALU.max, ALU.mult))
            plink(nc.vector.reciprocal(ri[:], rs[:]))
            plink(nc.vector.tensor_scalar(rt[:], P[:, 0, 0:128], ri[:, 0:1], None, ALU.mult))
            plink(nc.vector.tensor_scalar(rt[:], rt[:], ROUND, ROUND, ALU.add, ALU.subtract))
            plink(nc.vector.tensor_scalar(diag[:], G["ident"][:], rs[:, 0:1], 128.0, ALU.mult, ALU.mult))
            nc.vector.tensor_scalar(rqT[:], rt[:], 127.0, -127.0, ALU.min, ALU.max).then_inc(*pre.up())
            dve.wait_ge(*pre_pe.at(0, 2))
            plink(nc.vector.tensor_copy(rq[:], qview[:, 0:128]))
            nc.vector.tensor_copy(rsb[:], P[:, 2, 0:128]).then_inc(*pre.up())
            dve.wait_ge(*pre.at(0, 2))
            with nc.vector.Fori(0, NB) as b:
                dve.wait_ge(*z_full.at(b, 1))
                zt = P[:, 0, :].rearrange("p (t c) -> p t c", c=128)
                link(dve, nc.vector.tensor_reduce(amax[:], zt, AX.X, ALU.max, apply_absolute_value=True), step, b)
                link(dve, nc.vector.tensor_scalar(sc[:], amax[:], 1e-12, 1.0 / 127.0, ALU.max, ALU.mult), step, b)
                link(dve, nc.vector.reciprocal(inv[:], sc[:]), step, b)
                link(dve, nc.vector.tensor_tensor(qz[:], zt, inv[:].unsqueeze(2).to_broadcast(wide), ALU.mult), step, b)
                link(dve, nc.vector.tensor_scalar(qz[:], qz[:], ROUND, ROUND, ALU.add, ALU.subtract), step, b)
                nc.vector.tensor_scalar(qb[:], qz[:], 127.0, -127.0, ALU.min, ALU.max).then_inc(*q_ready.up())
                dve.wait_ge(*y_full.at(b, 1))
                y = P[:, 2, :].rearrange("p (t c) -> p t c", c=128)
                link(dve, nc.vector.tensor_tensor(qz[:], y, sc[:].unsqueeze(2).to_broadcast(wide), ALU.mult), step, b)
                link(dve, nc.vector.tensor_tensor(qz[:], qz[:], rsb[:].unsqueeze(1).to_broadcast(wide), ALU.mult), step, b)
                nc.vector.tensor_tensor(o[:, bass.ds(b * QT, QT), :], qz[:], P[:, 3, :].rearrange("p (t c) -> p t c", c=128),
                                        ALU.add).then_inc(*o_ready.up())
    ph.done()


def phase_output_plain(nc, G, D):
    ph = Phase(nc, "out")
    P = G["P"]
    xt = ph.sb("xt", [128, NB * QT, C])
    up, moved, st = ph.count("up"), ph.count("moved"), ph.count("st")
    with nc.Block() as block:
        @block.tensor
        def _(pe):
            for b in range(NB):
                for t in range(QT):
                    m = nc.tensor.transpose(P[:, b, t * 128:(t + 1) * 128], G["X"][:, b, t * 128:(t + 1) * 128], G["ident"][:])
                m.then_inc(*up.up())

        @block.vector
        def _(dve):
            for b in range(NB):
                dve.wait_ge(*up.at(0, b + 1))
                nc.vector.tensor_copy(xt[:, b * QT:(b + 1) * QT, :], P[:, b, :].rearrange("p (t c) -> p t c", c=C)).then_inc(*moved.up())

        @block.sync
        def _(sp):
            for b in range(NB):
                sp.wait_ge(*moved.at(0, b + 1))
                sp.dma_start(D["out"][:, b * QT:(b + 1) * QT, :], xt[:, b * QT:(b + 1) * QT, :]).then_inc(*st.up(16))
            sp.wait_ge(*st.at(0, 16 * NB))
    ph.done()


def build(nc, D):
    ctx = ExitStack()
    with ctx:
        def sb(name, shape, dt=F32):
            return ctx.enter_context(nc.sbuf_tensor(name, shape, dt))
        G = {"X": sb("X", [128, NB, T]), "Y": sb("Y", [128, NB, T]), "Z": sb("Z", [128, NB, T]),
             "CT": sb("CT", [128, NB, LK]), "ident": sb("ident", [128, 128]), "identb": sb("identb", [128, 128], BF16),
             "mean": sb("mean", [128, 128]), "eps": sb("eps", [128, 2]), "zero": sb("zero", [128, 1]), "scr": sb("scr", [128, 2]),
             "P": ctx.enter_context(nc.psum_tensor("P", [128, 8, 512], F32))}
        phase_input(nc, G, D)
        X, Y, Z = G["X"], G["Y"], G["Z"]
        if "L0x" in PHASES:
            phase_norm(nc, G, "n0x", X, Y)
            phase_latent(nc, G, D, "L0x")
        if "L0f" in PHASES:
            phase_norm(nc, G, "n0f", X, Y)
            phase_norm(nc, G, "n0a", Y, Z, gain=D["L0_ln1_w"], bias=D["L0_ln1_b"])
            phase_conv_attention(nc, G, D)
            phase_norm(nc, G, "n0m", Y, Z, gain=D["L0_ln2_w"], bias=D["L0_ln2_b"])
            phase_experts(nc, G, D, "L0m")
        if "L1x" in PHASES:
            phase_norm(nc, G, "n1x", X, Y)
            phase_cross(nc, G, D, "L1x")
        if "L1f" in PHASES:
            phase_norm(nc, G, "n1f", X, Y)
            phase_tree(nc, G, D)
        if "L2x" in PHASES:
            phase_norm(nc, G, "n2x", X, Y)
            phase_cross(nc, G, D, "L2x")
        if "L2f" in PHASES:
            phase_norm(nc, G, "n2f", X, Y)
            phase_norm(nc, G, "n2a", Y, Z, center=False, gain=D["L2_w_ln1"])
            phase_latent(nc, G, D, "L2f")
            phase_norm(nc, G, "n2m", Y, Z, center=False, gain=D["L2_w_ln2"])
            phase_experts(nc, G, D, "L2m")
        if "L3x" in PHASES:
            phase_norm(nc, G, "n3x", X, Y)
            phase_over_heads(nc, G, D)
        if "L3f" in PHASES:
            phase_norm(nc, G, "n3f", X, Z)
            phase_output(nc, G, D)
        else:
            phase_output_plain(nc, G, D)


def lay_out(i):
    f32, bf = np.float32, mybir.dt.np(BF16)
    d = {}
    tok = lambda a: np.ascontiguousarray(a.reshape(-1, 128, a.shape[-1]).transpose(1, 0, 2))
    col = lambda a: np.ascontiguousarray(a.reshape(-1, 1))
    d["x"] = tok(i["x"])
    d["ctx"] = np.ascontiguousarray(i["ctx_1024"].reshape(NB * 2, KT, C).transpose(1, 0, 2))
    d["ident"] = np.eye(128, dtype=f32)
    d["identb"] = np.eye(128).astype(bf)
    d["mean"] = np.full((128, 128), 1 / 128, f32)
    d["eps"] = np.full((128, 2), EPS, f32)

    qpart, kpart = (0, 0, 1, 0, 2, 1), (0, 1, 0, 2, 0, 1)
    selq, selk = np.zeros((128, 8, 3, 128), f32), np.zeros((128, H, 3, 128), f32)
    selm = np.zeros((128, H, 128), f32)
    seld8, seld16 = np.zeros((128, 128), f32), np.zeros((128, 128), f32)
    for h in range(H):
        for c in range(6):
            for e in range(8):
                row = 64 * (h % 2) + 8 * c + e
                selq[8 * h + e, h // 2, qpart[c], row] = 1
                selk[8 * h + e, h, kpart[c], row] = 1
        for p in range(3):
            selm[16 * p + h, h, :] = 1
    for j in range(4):
        seld8[32 * j + 8, 32 * j:32 * j + 32] = 1
        seld16[32 * j + 16, 32 * j:32 * j + 32] = 1
    d["selq"], d["selk"], d["selm"] = selq.astype(bf), selk.astype(bf), selm.astype(bf)
    d["seld8"], d["seld16"] = seld8, seld16

    def spread_cols(w):
        n, e = w.shape[0], w.shape[1] // H
        out = np.zeros((n, H, 32), w.dtype)
        out[:, :, :e] = w.reshape(n, H, e)
        return out.reshape(n, H * 32)

    def spread_rows(w):
        return np.ascontiguousarray(spread_cols(w.T).T.reshape(4, 128, C).transpose(1, 0, 2))

    def values_bias(b):
        out = spread_cols(b.reshape(1, -1)).reshape(H, 32)
        out[:, 8] = 1
        return np.ascontiguousarray(np.broadcast_to(out.reshape(1, -1), (KT, 512)))

    def block_diagonal(w):
        out = np.zeros((H, 8, H, 8), w.dtype)
        for h in range(H):
            out[h, :, h, :] = w[h]
        return out.reshape(C, C)

    p = "L1_xattn_"
    d["L1x_wq"], d["L1x_wk"] = (np.ascontiguousarray(i[p + w].T) for w in ("w_q", "w_k"))
    d["L1x_wv"], d["L1x_wo"] = spread_cols(i[p + "w_v"].T), spread_rows(np.ascontiguousarray(i[p + "w_o"].T))
    d["L1x_bq"], d["L1x_bk"], d["L1x_bo"] = (col(i[p + b]) for b in ("b_q", "b_k", "b_o"))
    d["L1x_bv"] = values_bias(i[p + "b_v"])

    d["zero"] = np.zeros((128, 1), f32)
    k, q = np.arange(128)[:, None], np.arange(128)[None, :]
    d["mask_k"] = np.where(k > q, -BIG, 0).astype(f32).astype(bf)
    d["mask_q"] = np.ascontiguousarray(d["mask_k"].T)

    def rope(n, half, base, pos_exp):
        inv = (1.0 / np.float32(base) ** pos_exp.astype(f32)).astype(f32)
        ang = (np.arange(n, dtype=f32)[None, :] * inv[:, None]).astype(f32)
        return np.cos(ang).astype(f32), np.sin(ang).astype(f32)

    cos, sin = rope(T, 4, 10000.0, np.arange(0, 8, 2) / 8)
    cos8, sin8 = np.tile(cos, (32, 1)), np.tile(np.concatenate([-sin, sin]), (16, 1))
    s8 = f32(8.0) ** f32(-0.5)
    d["L0f_cq"], d["L0f_sq"], d["L0f_ck"], d["L0f_sk"] = cos8 * s8, sin8 * s8, cos8, sin8
    p = "L0_ffn_"
    d["L0f_conv"] = np.ascontiguousarray(i[p + "conv_w"][:, 0, :])
    wq, wk, wv = np.split(i[p + "attn_w"], 3, axis=1)
    swap = np.arange(C).reshape(16, 2, 4)[:, ::-1].reshape(-1)
    d["L0f_wq"], d["L0f_wqr"], d["L0f_wk"], d["L0f_wkr"] = wq, wq[:, swap], wk, wk[:, swap]
    d["L0f_wv"], d["L0f_wo"] = spread_cols(wv), spread_rows(i[p + "proj_w"])
    d["L0f_bv"] = np.ascontiguousarray(np.broadcast_to(values_bias(np.zeros(C, f32))[0:1], (128, 512)))
    for n in ("ln1_w", "ln1_b", "ln2_w", "ln2_b"):
        d["L0_" + n] = col(i[p + n])

    def padded(a, shape, at=(0, 0)):
        out = np.zeros(shape, a.dtype)
        out[tuple(slice(o, o + n) for o, n in zip(at, a.shape))] = a
        return out

    p = "L0_xattn_"
    wa, wb = np.zeros((128, H, 128), f32), np.zeros((128, 8, 128), f32)
    qr = i[p + "w_q_rope"].reshape(48, H, 64)
    wa[:48, :, :64] = qr
    wb[:48] = qr.reshape(48, H, 2, 32)[:, :, ::-1].reshape(48, 8, 128)
    d["L0x_wa"], d["L0x_wb"] = wa, wb
    d["L0x_wqd"] = padded(i[p + "w_q_down"], (128, 128))
    d["L0x_wqT"] = i[p + "w_q_up"].reshape(48, H, 64).transpose(2, 1, 0)
    d["L0x_wkT"] = i[p + "w_k_up"].reshape(32, H, 64).transpose(2, 1, 0)
    d["L0x_wvT"] = i[p + "w_v_up"].reshape(32, H, 64).transpose(2, 1, 0)
    d["L0x_woh"] = i[p + "w_out"].reshape(H, 64, C).transpose(1, 0, 2)
    wka = padded(i[p + "w_k_rope"], (128, 128))
    wka[:32, 64:96] = np.eye(32)
    d["L0x_wka"] = wka
    d["L0x_wkb"] = padded(i[p + "w_k_rope"].reshape(32, 2, 32)[:, ::-1].reshape(32, 64), (128, 128))
    d["L0x_wlat"] = padded(i[p + "w_kv_comp"], (128, 128))
    cos, sin = rope(T, 32, 10000.0, np.arange(32) / 32)
    s128 = f32(1.0) / np.sqrt(128).astype(f32)
    rc, rs = np.tile(cos, (2, 1)), np.concatenate([-sin, sin])
    one = np.ones((32, T), f32)
    d["L0x_cq"] = padded(np.concatenate([rc, one]) * s128, (128, T))
    d["L0x_sq"] = np.tile(rs, (2, 1)) * s128
    d["L0x_ck"] = padded(np.concatenate([rc, one])[:, :LK], (128, LK))
    d["L0x_sk"] = padded(rs[:, :LK], (128, LK))
    seg = i["itok_BxS_0_511"]
    d["segc"] = np.ascontiguousarray(seg.reshape(NB * QT, 128).T)
    d["segr"] = np.ascontiguousarray(np.broadcast_to(seg[None], (KT, NB, T)))
    d["keyrow"] = np.ascontiguousarray(np.broadcast_to(np.arange(1, LK + 1, dtype=f32), (128, LK)))
    d["keycol"] = np.ascontiguousarray(np.arange(1, LK + 1, dtype=f32).reshape(2, KT).T)

    p = "L2_ffn_"
    wq = i[p + "Wq"].reshape(C, H, 64)
    flip = np.arange(32).reshape(16, 2)[:, ::-1].reshape(-1)
    wa = np.zeros((128, H, 128), f32)
    wa[:, :, :32] = wq[:, :, 32:]
    d["L2f_wa"], d["L2f_wb"] = wa, wq[:, :, 32:][:, :, flip].reshape(C, 4, 128)
    d["L2f_wqT"] = wq[:, :, :32].transpose(2, 1, 0)
    kvb = i[p + "Wkvb"].reshape(16, H, 32).transpose(2, 1, 0)
    d["L2f_wkT"] = kvb
    d["L2f_wvT"] = padded(kvb, (32, H, 32), (0, 0, 0))
    d["L2f_woh"] = i[p + "Wo"].reshape(H, 64, C)[:, :32].transpose(1, 0, 2)
    kva = i[p + "Wkva"]
    d["L2f_wka"] = padded(np.concatenate([kva[:, 16:], kva[:, :16]], 1), (128, 128))
    d["L2f_wkb"] = padded(kva[:, 16:][:, flip], (128, 128))
    d["L2f_wlat"] = kva[:, :16]
    cos, sin = rope(T, 16, 100000.0, np.arange(0, 32, 2) / 32)
    rc = np.repeat(cos, 2, axis=0)
    rs = np.stack([-sin, sin], 1).reshape(32, T)
    one = np.ones((16, T), f32)
    d["L2f_cq"] = padded(np.concatenate([rc, one]) * f32(0.125), (128, T))
    d["L2f_sq"] = np.tile(rs, (4, 1)) * f32(0.125)
    d["L2f_ck"] = padded(np.concatenate([rc, one]), (128, T))
    d["L2f_sk"] = padded(rs, (128, T))
    d["L2_w_ln1"], d["L2_w_ln2"] = col(i[p + "w_ln1"]), col(i[p + "w_ln2"])

    p = "L2_xattn_"
    d["L2x_wq"], d["L2x_wk"] = (block_diagonal(i[p + w]) for w in ("Wq", "Wk"))
    d["L2x_wv"], d["L2x_wo"] = spread_cols(block_diagonal(i[p + "Wv"])), spread_rows(i[p + "Wo"])
    d["L2x_bq"], d["L2x_bk"], d["L2x_bo"] = (col(i[p + b]) for b in ("bq", "bk", "bo"))
    d["L2x_bv"] = values_bias(i[p + "bv"].reshape(-1))

    p = "L0_ffn_"
    d["L0m_router"] = i[p + "router_w"]
    d["L0m_w1"] = i[p + "expert_wv"].transpose(1, 0, 2)
    d["L0m_w2"] = i[p + "expert_proj"].reshape(4, 4, 128, C).transpose(2, 0, 1, 3)
    p = "L2_ffn_"
    d["L2m_router"] = i[p + "Wgate"]
    w1, w2 = np.zeros((128, 5, 2, 2, 64), f32), np.zeros((2, 64, 5, C), f32)
    for e in range(8):
        w1[:, e // 2, 0, e % 2], w1[:, e // 2, 1, e % 2] = i[p + "Wg"][e], i[p + "Wu"][e]
        w2[e % 2, :, e // 2] = i[p + "Wd"][e]
    w1[:, 4, 0, 0], w1[:, 4, 1, 0], w2[0, :, 4] = i[p + "sWg"][0], i[p + "sWu"][0], i[p + "sWd"][0]
    d["L2m_w1"], d["L2m_w2"] = w1.reshape(128, 5, 2, 128), w2.reshape(128, 5, C)
    d["L2m_ebias"] = np.broadcast_to(i[p + "expert_bias"], (128, QT, 8))
    for n, e in (("L0m", 4), ("L2m", 8)):
        d[n + "_prio"] = np.broadcast_to(np.arange(e, 0, -1, dtype=f32), (128, QT, e))
        d[n + "_sel"] = np.repeat(np.eye(e, dtype=f32), 128 if e == 4 else 64, axis=1).reshape(e, 4, 128)

    p = "L1_ffn_"
    d["L1f_wq"], d["L1f_rt"], d["L1f_lvT"], d["L1f_woT"] = (
        i[p + "Wq"], i[p + "routers"].T, i[p + "leaf_values"].T, i[p + "Wout_w"].T)
    d["L1f_bias"] = col(i[p + "Wout_b"])
    p = "L3_xattn_"
    d["L3x_wq"], d["L3x_wk"] = i[p + "Wq"].T, i[p + "Wk"].T
    d["L3x_wv"], d["L3x_wo"] = spread_cols(i[p + "Wv"].T), spread_rows(i[p + "Wo"].T)
    d["L3f_rhs"] = i["L3_ffn_rhs"]
    return d


def kernel(**inputs):
    import concourse.bacc as bacc
    from concourse.bass_utils import run_bass_kernel_spmd

    nc = bacc.Bacc("TRN2", target_bir_lowering=False, num_devices=1)
    arrays = {"in_" + k: np.ascontiguousarray(v) for k, v in lay_out({k: np.asarray(v) for k, v in inputs.items()}).items()}
    D = {k[3:]: nc.dram_tensor(k, a.shape, mybir.dt.from_np(a.dtype), kind="ExternalInput").ap() for k, a in arrays.items()}
    D["out"] = nc.dram_tensor("out_0", (128, NB * QT, C), F32, kind="ExternalOutput").ap()
    build(nc, D)
    r = run_bass_kernel_spmd(nc, [arrays], core_ids=[0])
    return np.ascontiguousarray(r.results[0]["out_0"].transpose(1, 0, 2)).reshape(NB, T, C)
```

```python
from contextlib import ExitStack

import concourse.bass as bass
import numpy as np
from concourse import mybir

F32 = mybir.dt.float32
BF16 = mybir.dt.bfloat16
I32 = mybir.dt.int32
ALU = mybir.AluOpType
ACT = mybir.ActivationFunctionType
AX = mybir.AxisListType

NB, T, C = 4, 512, 128
H = 16
LK, KT = 154, 77
QT = T // 128
EPS = 1e-5
BIG = 1e30

PHASES = ["L0x", "L0f", "L1x", "L1f", "L2x", "L2f", "L3x", "L3f"]


class Count:

    def __init__(self, nc, name, per=0, ahead=0):
        self.name, self.per, self.ahead, self.n = name, per, ahead, 0
        self.sem = nc.alloc_semaphore(name)

    def up(self, n=1):
        self.n += n
        return self.sem, n

    def free(self, b, k):
        if isinstance(b, tuple):
            return self.sem, b[0] * self.per + (b[1] * self.per + k)
        return self.sem, b * self.per + k

    def at(self, b, k):
        return self.free(b, k + self.ahead)

    def before(self, eng, b):
        if not (isinstance(b[0], int) and b[0] + b[1] == 0):
            eng.wait_ge(*self.at(b, 0))

    def one_before(self, eng, b):
        if not (isinstance(b[0], int) and b[0] + b[1] == 0):
            eng.wait_ge(*self.free(b, 0))

    def check(self):
        assert self.n in (self.per, 2 * self.per), (self.name, "signals", self.n, "declared", self.per)


class Phase:

    def __init__(self, nc, name):
        self.nc, self.name, self.ctx, self.counts = nc, name, ExitStack(), []

    def sb(self, name, shape, dt=F32):
        return self.ctx.enter_context(self.nc.sbuf_tensor(f"{self.name}_{name}", shape, dt))

    def count(self, name, per=0, ahead=0):
        c = Count(self.nc, f"{self.name}_{name}", per, ahead)
        self.counts.append(c)
        return c

    def done(self):
        for c in self.counts:
            if c.per:
                c.check()
        self.ctx.close()
        self.nc.clear_and_free_semaphores([c.sem for c in self.counts])
        self.nc.all_engine_barrier()


def link(eng, ins, step, b=0):
    ins.then_inc(*step.up())
    eng.wait_ge(*step.at(b, (step.n - 1) % step.per + 1 if step.per else step.n))


def seq(buf, b):
    n = b[0] + b[1] if isinstance(b, tuple) else b
    part = buf[:, n:n + 1, :] if isinstance(n, int) else buf[:, bass.ds(n, 1), :]
    return part.rearrange("p a t -> p (a t)")


def load_all(sp, ld, pairs):
    for dst, src in pairs:
        sp.dma_start(dst, src).then_inc(*ld.up(16))


def phase_input(nc, G, D):
    ph = Phase(nc, "in")
    P = G["P"]
    xt = ph.sb("xt", [128, NB * QT, C])
    ct = ph.sb("ct", [KT, NB * 2, C])
    ld = ph.count("ld")
    x_up = ph.count("x_up")
    c_up = ph.count("c_up")
    x_moved, c_moved = ph.count("x_moved"), ph.count("c_moved")
    loads = [(xt[:], D["x"]), (ct[:], D["ctx"]), (G["ident"][:], D["ident"]), (G["identb"][:], D["identb"]),
             (G["mean"][:], D["mean"]), (G["zero"][:], D["zero"]), (G["eps"][:], D["eps"])]
    with nc.Block() as block:
        @block.sync
        def _(sp):
            load_all(sp, ld, loads)

        @block.tensor
        def _(pe):
            pe.wait_ge(*ld.at(0, 16 * len(loads)))
            for b in range(NB):
                for t in range(QT):
                    m = nc.tensor.transpose(P[:, b, t * 128:(t + 1) * 128], xt[:, b * QT + t, :], G["ident"][:])
                m.then_inc(*x_up.up())
            for i in range(NB * 2):
                m = nc.tensor.transpose(P[:, 4 + i // 6, (i % 6) * KT:(i % 6) * KT + KT], ct[:, i, :],
                                        G["ident"][0:KT, 0:KT])
            m.then_inc(*c_up.up())

        @block.vector
        def _(dve):
            for b in range(NB):
                dve.wait_ge(*x_up.at(0, b + 1))
                nc.vector.tensor_copy(G["X"][:, b, :], P[:, b, :]).then_inc(*x_moved.up())
            dve.wait_ge(*x_moved.at(0, NB))

        @block.scalar
        def _(act):
            act.wait_ge(*c_up.at(0, 1))
            nc.scalar.copy(G["CT"][:, 0:3, :], P[:, 4, 0:3 * LK].rearrange("p (b k) -> p b k", k=LK)).then_inc(*c_moved.up())
            nc.scalar.copy(G["CT"][:, 3, :], P[:, 5, 0:LK]).then_inc(*c_moved.up())
            act.wait_ge(*c_moved.at(0, 2))
    ph.done()


def phase_norm(nc, G, name, src, dst, center=True, gain=None, bias=None):
    ph = Phase(nc, name)
    P = G["P"]
    xc = ph.sb("xc", [128, NB, T]) if center else src
    sq = ph.sb("sq", [128, NB, T])
    rs = ph.sb("rs", [128, NB, T])
    step, ld = ph.count("step"), ph.count("ld")
    given = [v for v in (gain, bias) if v is not None]
    cols = [ph.sb(f"col{n}", [128, 1]) for n in range(len(given))]
    gain, bias = ([c[:, 0:1] for c in cols] + [None, None])[:2]
    mean_up, cent, squared, var_up, ln, rstd, out = (
        ph.count(n) for n in ("mean_up", "cent", "squared", "var_up", "ln", "rstd", "out"))
    with nc.Block() as block:
        @block.sync
        def _(sp):
            load_all(sp, ld, [(c[:], v) for c, v in zip(cols, given)])

        @block.tensor
        def _(pe):
            if center:
                for b in range(NB):
                    nc.tensor.matmul(P[:, b, :], G["mean"][:], src[:, b, :], start=True, stop=True).then_inc(*mean_up.up())
            for b in range(NB):
                pe.wait_ge(*squared.at(0, b + 1))
                nc.tensor.matmul(P[:, 4 + b, :], G["mean"][:], sq[:, b, :], start=True, stop=True).then_inc(*var_up.up())

        @block.vector
        def _(dve):
            if center:
                for b in range(NB):
                    dve.wait_ge(*mean_up.at(0, b + 1))
                    nc.vector.tensor_tensor(xc[:, b, :], src[:, b, :], P[:, b, :], ALU.subtract).then_inc(*cent.up())
            if given:
                dve.wait_ge(*ld.at(0, 16 * len(given)))
            for b in range(NB):
                dve.wait_ge(*rstd.at(0, b + 1))
                if center:
                    dve.wait_ge(*cent.at(0, b + 1))
                if gain is None:
                    nc.vector.tensor_tensor(dst[:, b, :], xc[:, b, :], rs[:, b, :], ALU.mult).then_inc(*out.up())
                elif bias is None:
                    nc.vector.scalar_tensor_tensor(out=dst[:, b, :], in0=xc[:, b, :], scalar=gain, in1=rs[:, b, :],
                                                   op0=ALU.mult, op1=ALU.mult).then_inc(*out.up())
                else:
                    link(dve, nc.vector.scalar_tensor_tensor(out=dst[:, b, :], in0=xc[:, b, :], scalar=gain,
                                                             in1=rs[:, b, :], op0=ALU.mult, op1=ALU.mult), step)
                    nc.vector.tensor_scalar(dst[:, b, :], dst[:, b, :], bias, None, ALU.add).then_inc(*out.up())
            dve.wait_ge(*out.at(0, NB))

        @block.gpsimd
        def _(pool):
            for b in range(0, NB):
                if center:
                    pool.wait_ge(*cent.at(0, b + 1))
                nc.gpsimd.tensor_tensor(sq[:, b, :], xc[:, b, :], xc[:, b, :], ALU.mult).then_inc(*squared.up())

        @block.scalar
        def _(act):
            for b in range(NB):
                act.wait_ge(*var_up.at(0, b + 1))
                nc.scalar.activation(rs[:, b, :], P[:, 4 + b, :], ACT.Ln, bias=G["eps"][:, 0:1]).then_inc(*ln.up())
            for b in range(NB):
                act.wait_ge(*ln.at(0, b + 1))
                nc.scalar.activation(rs[:, b, :], rs[:, b, :], ACT.Exp, scale=-0.5).then_inc(*rstd.up())
    ph.done()


def groups_of(causal):
    out = []
    for g in range(4):
        units = []
        for h in range(4 * g, 4 * g + 4):
            if not causal:
                units += [[(h, kt, 0, T, 0)] for kt in range(2)]
                continue
            units.append([(h, 0, 0, 512, 0)])
            units.append([(h, 1, 128, 384, 0), (h, 3, 384, 128, 384)])
            if h % 2:
                units.append([(h - 1, 2, 256, 256, 0), (h, 2, 256, 256, 256)])
        out.append(units)
    return out


def spread_between(main, extra):
    out, done = [], 0
    for n, step in enumerate(main):
        out.append(step)
        upto = len(extra) * (n + 1) // len(main)
        out += extra[done:upto]
        done = upto
    return out


EARLY = 2


class Attention:

    RING = 3

    def __init__(self, ph, G, causal, parts, den_pass, mask=False, prep=(), late=()):
        self.ph, self.G, self.nc, self.causal, self.parts, self.den_pass, self.mask = (
            ph, G, ph.nc, causal, parts, den_pass, mask)
        self.nk = 128 if causal else KT
        self.nkt = 4 if causal else 2
        self.keys = T if causal else LK
        self.groups = groups_of(causal)
        self.per_group = len(self.groups[0])
        self.kper = 1 if causal else 3
        self.kbanks = -(-H // self.kper)
        self.nsel = 8 + self.kbanks if parts else 0
        self.ns = QT * self.kbanks + (0 if parts else H)
        c = ph.count
        self.ring_full = c("ring_full", self.nsel + 4 * self.per_group)
        self.ring_done = c("ring_done", self.nsel + 4 * self.per_group, self.RING)
        self.s_full, self.s_free = c("s_full", self.ns), c("s_free", self.ns, 2)
        self.parts_ready = c("parts_ready", 2) if parts else None
        self.nm_ready, self.mt_full, self.nmt_ready = c("nm_ready", 1), c("mt_full", 1), c("nmt_ready", 1)
        self.o_full, self.o_free = c("o_full", 4, 2), c("o_free", 4, 1)
        self.d_free = c("d_free", 4, 1) if den_pass else None
        self.den_full, self.rp_ready = c("den_full", 1), c("rp_ready", 1)
        self.rt_full, self.rt_ready = c("rt_full", 1), c("rt_ready", 1)
        self.bc_full, self.on_ready = c("bc_full", 4), c("on_ready", 4)
        self.rec_step = c("rec_step", 4)
        self.out_full, self.out_taken = c("out_full", 1), c("out_taken", 1, 1)
        sb = ph.sb
        if parts:
            self.qp, self.kp = sb("qp", [128, 3, T], BF16), sb("kp", [128, 3, self.keys], BF16)
            self.qs, self.ks = sb("qs", [128, 8, T], BF16), sb("ks", [128, H, self.keys], BF16)
            self.selq, self.selk = sb("selq", [128, 8, 3, 128], BF16), sb("selk", [128, H, 3, 128], BF16)
        else:
            self.qe = sb("qe", [128, H, T])
            self.k_first, self.k_second = sb("k_first", [128, self.keys]), sb("k_second", [128, self.keys])
            self.k_moved = c("k_moved", 1)
        self.selm = sb("selm", [128, H, 128], BF16)
        self.prob = sb("prob", [128, 2 * self.per_group, T])
        self.nm, self.nmr = sb("nm", [128, QT, H]), sb("nmr", [128, QT, H])
        self.nmp = sb("nmp", [128, QT, 128], BF16)
        self.nmt = sb("nmt", [128, T], BF16)
        self.osp, self.on = sb("osp", [128, 4, T]), sb("on", [128, 4, T])
        self.osd = sb("osd", [128, 4, T]) if den_pass else self.osp
        self.rec, self.recr = sb("rec", [128, QT, H]), sb("recr", [128, QT, H])
        self.rp, self.rt_sb = sb("rp", [128, QT, 128], BF16), sb("rt_sb", [128, T], BF16)
        self.seld, self.selr = sb("seld", [128, 4]), sb("selr", [128, 4, 128], BF16)
        self.wo = sb("wo", [128, 4, C])
        self.mt = G["P"][:, 5, 0:256].bitcast(BF16)
        self.den = G["P"][:, 7, 0:QT * H].rearrange("p (t h) -> p t h", h=H)
        self.rt = G["P"][:, 7, 256:512].bitcast(BF16)

        nxt = [[], [], [], []]
        ready = [[] for _ in range(self.kbanks)]
        seen = 0
        for k in range(self.kbanks):
            last = min(H, (k + 1) * self.kper) - 1
            while seen <= last:
                if not parts:
                    ready[k].append(("head", seen))
                elif seen % 2 == 0:
                    ready[k].append(("sel", seen // 2))
                seen += 1
            if parts:
                ready[k].append(("sel", 8 + k))
        nxt[0] += ready[0]
        for k in range(self.kbanks):
            gate = lambda k: (min(H, (k + 1) * self.kper) - 1) // 4
            if k + 1 < self.kbanks:
                nxt[gate(k + 1)] += ready[k + 1]
            nxt[gate(min(k + 1, self.kbanks - 1))] += [("first", (k, qt)) for qt in range(QT)]
        nxt = [[(kind, 1, n) for kind, n in steps] for steps in nxt]
        second = [[("second", 1 if g == 0 or g == 1 and u < EARLY else 0, (g, u)) for u in range(self.per_group)]
                  for g in range(4)]
        values = [[("values", 0, n)] for n in range(4)]
        self.order = [(kind, 1, n) for kind, n in prep] + second[1][EARLY:]
        self.order += spread_between(values[0] + second[2], nxt[0] + nxt[1])
        self.order += spread_between(values[1] + second[3] + values[2], nxt[2])
        half = len(nxt[3]) // 2
        self.order += nxt[3][:half] + values[3] + nxt[3][half:-2] + [("den", 0, 0)] + nxt[3][-2:]
        back = [("rt", 0, 0)] + [("bc", 0, g) for g in range(4)]
        late = [(kind, 1, n) for kind, n in late]
        mixed = spread_between([s for s in back], late)
        self.order += [("mt", 1, 0)] + spread_between(second[0], mixed) + second[1][:EARLY] + [("out", 0, 0)]
        self.ring_ahead = self.nsel + self.per_group + EARLY
        self.bank_of_step = {}
        uses = 0
        for kind, off, n in self.order:
            if kind in ("first", "head"):
                uses += 1
                self.bank_of_step[kind, n] = uses
        self.order_ahead = [s for s in self.order if s[1] == 1]
        self.order_behind = [s for s in self.order if s[1] == 0]

    def run(self, engine, one_step):
        def part(order, t, turn):
            self.unit, self.turn, self.first_use, self.last_unit = 0, turn, {}, {}
            for kind, off, n in order:
                one_step((t, off), kind, n)
        part(self.order_ahead, -1, None)
        with engine.Fori(0, NB - 1) as t:
            part(self.order, t, t)
        part(self.order_behind, NB - 1, NB - 1)

    def ring(self, count, unit, free=False):
        k = unit + (0 if free else count.ahead)
        return count.sem, k if self.turn is None else self.turn * count.per + (self.ring_ahead + k)

    def loads(self, D, seld=None):
        out = [(self.selm[:], D["selm"])]
        if self.parts:
            out += [(self.selq[:], D["selq"]), (self.selk[:], D["selk"])]
        return out + [(self.selr[:], D["selr"]), (self.seld[:], D[seld])]

    def dve_ahead(self, dve):
        self.nc.vector.memset(self.nmp[:], 0.0).then_inc(self.s_free.sem, self.s_free.ahead)
        self.nc.vector.memset(self.nmr[:], 0.0).then_inc(self.o_free.sem, self.o_free.ahead)
        self.nc.vector.memset(self.rp[:], 0.0).then_inc(self.out_taken.sem, self.out_taken.ahead)
        dve.wait_ge(self.s_free.sem, self.s_free.ahead)
        dve.wait_ge(self.o_free.sem, self.o_free.ahead)
        dve.wait_ge(self.out_taken.sem, self.out_taken.ahead)

    def pe_ahead(self, sem, n):
        one = self.G["identb"][0:32, 0:32]
        self.nc.tensor.matmul(self.G["P"][0:32, 7, 0:32], one, one, start=True, stop=True).then_inc(sem, n)

    def act_ahead(self, scratch):
        if self.den_pass:
            self.nc.scalar.copy(self.osd[:, 0, 0:1], self.G["eps"][:, 0:1]).then_inc(self.d_free.sem, self.d_free.ahead)
        self.nc.scalar.copy(scratch, self.G["eps"][:, 0:1]).then_inc(self.ring_done.sem, self.ring_done.ahead)

    def q(self, h, q0, n):
        return self.qs[:, h // 2, q0:q0 + n] if self.parts else self.qe[:, h, q0:q0 + n]

    def ring_bank(self, pe):
        pe.wait_ge(*self.ring(self.ring_done, max(self.unit + 1, self.RING), free=True))
        bank = 2 + self.unit % self.RING
        self.unit += 1
        return bank

    def first_bank(self, pe, b, kind, n):
        use = self.bank_of_step[kind, n]
        pe.wait_ge(*self.s_free.free(b, use))
        return (use - 1) % 2

    def pe(self, pe, b, kind, n):
        nc, G, P = self.nc, self.G, self.G["P"]
        mm = nc.tensor.matmul
        if kind == "sel":
            if n == 0:
                pe.wait_ge(*self.parts_ready.at(b, 2))
            bank = self.ring_bank(pe)
            if n < 8:
                for part in range(3):
                    m = mm(P[:, bank, :], self.selq[:, n, part, :], self.qp[:, part, :], start=part == 0, stop=part == 2)
            else:
                for j, h in enumerate(range((n - 8) * self.kper, min(H, (n - 7) * self.kper))):
                    for part in range(3):
                        m = mm(P[:, bank, j * self.keys:(j + 1) * self.keys], self.selk[:, h, part, :],
                               self.kp[:, part, :], start=part == 0, stop=part == 2)
                self.first_use[n - 8] = self.unit
            m.then_inc(*self.ring_full.up())
        elif kind == "first":
            k, qt = n
            heads = range(k * self.kper, min(H, (k + 1) * self.kper))
            if qt == 0 and self.parts:
                pe.wait_ge(*self.ring(self.ring_done, self.first_use[k]))
            elif qt == 0:
                self.wait_q(pe, b, heads[-1])
            bank = self.first_bank(pe, b, kind, n)
            w = (qt + 1) * 128 if self.causal else LK
            if self.mask:
                mm(P[:, bank, 0:len(heads) * w].rearrange("p (h k) -> p h k", k=w), G["identb"][:],
                   self.mask_of(self.mask_q, b)[:, qt:qt + 1, :].to_broadcast([128, len(heads), w]), start=True, stop=False)
            for j, h in enumerate(heads):
                keys = self.ks[:, h, 0:w] if self.parts else self.k_first[:, 0:w]
                m = mm(P[:, bank, j * w:(j + 1) * w], self.q(h, qt * 128, 128), keys,
                       start=not self.mask, stop=not self.causal and (not self.mask or j == len(heads) - 1))
            if self.causal:
                m = mm(P[:, bank, w - 128:w], G["identb"][:], self.mask_q[:], start=False, stop=True)
            m.then_inc(*self.s_full.up())
        elif kind == "mt":
            self.out_taken.one_before(pe, b)
            pe.wait_ge(*self.nm_ready.at(b, 1))
            for qt in range(QT):
                m = nc.tensor.transpose(self.mt[:, qt * 128:(qt + 1) * 128], self.nmp[:, qt, :], G["identb"][:])
            m.then_inc(*self.mt_full.up())
        elif kind == "second":
            g, u = n
            if g == 0 and u == 0:
                pe.wait_ge(*self.nmt_ready.at(b, 1))
                if not self.parts:
                    pe.wait_ge(*self.k_moved.at(b, 1))
            bank = self.ring_bank(pe)
            for h, kt, q0, w, col in self.groups[g][u]:
                out = P[0:self.nk, bank, col:col + w]
                at = slice(kt * self.nk, (kt + 1) * self.nk)
                mm(out, self.ks[:, h, at] if self.parts else self.k_second[:, at], self.q(h, q0, w), start=True, stop=False)
                if self.causal:
                    mm(out[:, 0:128], G["identb"][:], self.mask_k[:], start=False, stop=False)
                if self.mask:
                    mm(out, G["identb"][0:KT, 0:KT], self.mask_of(self.mask_k, b)[:, kt, :], start=False, stop=False)
                m = mm(out, self.selm[:, h, 0:self.nk], self.nmt[:, q0:q0 + w], start=False, stop=True)
            m.then_inc(*self.ring_full.up())
            self.last_unit[g] = self.unit
        elif kind == "values":
            if n == 0:
                self.wait_values(pe, b)
            pe.wait_ge(*self.ring(self.ring_done, self.last_unit[n] if n else 0))
            pe.wait_ge(*self.o_free.free(b, n + 1))
            if self.den_pass:
                pe.wait_ge(*self.d_free.free(b, n + 1))
            where = {}
            for u, tiles in enumerate(self.groups[n]):
                for h, kt, q0, w, col in tiles:
                    where[h, kt] = ((n % 2) * self.per_group + u, q0, w, col)
            for kt in range(self.nkt):
                for bank in (6, 7)[:2 if self.den_pass else 1]:
                    for j in range(4):
                        slot, q0, w, col = where[4 * n + j, kt]
                        lhs = self.v(kt, 4 * n + j) if bank == 6 else self.ones[0:self.nk, 0:32]
                        m = mm(P[32 * j:32 * j + 32, bank, q0:q0 + w], lhs,
                               self.prob[0:self.nk, slot, col:col + w], start=kt == 0, stop=kt == self.nkt - 1)
            m.then_inc(*self.o_full.up())
        elif kind == "den":
            pe.wait_ge(*(self.d_free if self.den_pass else self.o_free).at(b, 4))
            for qt in range(QT):
                for g in range(4):
                    m = mm(self.den[:, qt, 4 * g:4 * g + 4], self.osd[:, g, qt * 128:(qt + 1) * 128], self.seld[:],
                           start=True, stop=True)
            m.then_inc(*self.den_full.up())
        elif kind == "rt":
            pe.wait_ge(*self.rp_ready.at(b, 1))
            for qt in range(QT):
                m = nc.tensor.transpose(self.rt[:, qt * 128:(qt + 1) * 128], self.rp[:, qt, :], G["identb"][:])
            m.then_inc(*self.rt_full.up())
        elif kind == "bc":
            pe.wait_ge(*(self.on_ready.at(b, n) if n else self.rt_ready.at(b, 1)))
            mm(P[:, 7, :], self.selr[:, n, :], self.rt_sb[:], start=True, stop=True).then_inc(*self.bc_full.up())
        elif kind == "out":
            pe.wait_ge(*self.on_ready.at(b, 4))
            for g in range(4):
                m = mm(P[:, 5, :], self.wo[:, g, :], self.on[:, g, :], start=g == 0, stop=g == 3)
            m.then_inc(*self.out_full.up())

    def act(self, act, b, kind, n):
        nc, P = self.nc, self.G["P"]
        bank = 2 + self.unit % self.RING
        if kind == "sel":
            self.unit += 1
            act.wait_ge(*self.ring(self.ring_full, self.unit))
            if n < 8:
                m = nc.scalar.copy(self.qs[:, n, :], P[:, bank, :])
            else:
                h0 = (n - 8) * self.kper
                w = min(H, h0 + self.kper) - h0
                m = nc.scalar.copy(self.ks[:, h0:h0 + w, :],
                                   P[:, bank, 0:w * self.keys].rearrange("p (h k) -> p h k", k=self.keys))
            m.then_inc(*self.ring_done.up())
        elif kind == "mt" and not self.parts:
            act.wait_ge(*self.k_ready.at(b, 1))
            nc.scalar.copy(self.k_second[:], self.k_first[:]).then_inc(*self.k_moved.up())
        elif kind == "second":
            g, u = n
            if u == 0:
                act.wait_ge(*self.o_full.free(b, g + 1))
            self.unit += 1
            act.wait_ge(*self.ring(self.ring_full, self.unit))
            nc.scalar.activation(self.prob[0:self.nk, (g % 2) * self.per_group + u, :], P[0:self.nk, bank, :],
                                 ACT.Exp).then_inc(*self.ring_done.up())

        elif kind == "values" and self.den_pass:
            act.wait_ge(*self.o_full.at(b, n + 1))
            nc.scalar.copy(self.osd[:, n, :], P[:, 7, :]).then_inc(*self.d_free.up())

    def dve(self, dve, b, kind, n, resid, bias):
        nc, P, step = self.nc, self.G["P"], self.step
        if kind == "first":
            k, qt = n
            w = (qt + 1) * 128 if self.causal else LK
            h0, h1 = k * self.kper, min(H, (k + 1) * self.kper)
            use = self.bank_of_step[kind, n]
            dve.wait_ge(*self.s_full.at(b, use))
            nc.vector.tensor_reduce(self.nm[:, qt, h0:h1], P[:, (use - 1) % 2, 0:(h1 - h0) * w].rearrange("p (h k) -> p h k", k=w),
                                    AX.X, ALU.max, negate=True).then_inc(*self.s_free.up())
            if n == (self.kbanks - 1, QT - 1):
                dve.wait_ge(*self.s_free.at(b, self.ns))
                part = [self.nmp[:, :, p * H:(p + 1) * H] for p in range(3)]
                link(dve, nc.vector.tensor_copy(part[0], self.nm[:]), step, b)
                link(dve, nc.vector.tensor_tensor(self.nmr[:], self.nm[:], part[0], ALU.subtract), step, b)
                link(dve, nc.vector.tensor_copy(part[1], self.nmr[:]), step, b)
                nc.vector.tensor_tensor(part[2], self.nmr[:], part[1], ALU.subtract).then_inc(*self.nm_ready.up())
        elif kind == "mt":
            dve.wait_ge(*self.mt_full.at(b, 1))
            nc.vector.tensor_copy(self.nmt[:], self.mt).then_inc(*self.nmt_ready.up())
        elif kind == "values":
            dve.wait_ge(*self.o_full.at(b, n + 1))
            nc.vector.tensor_copy(self.osp[:, n, :], P[:, 6, :]).then_inc(*self.o_free.up())
        elif kind == "den":
            dve.wait_ge(*self.den_full.at(b, 1))
            link(dve, nc.vector.reciprocal(self.rec[:], self.den), self.rec_step, b)
            part = [self.rp[:, :, p * H:(p + 1) * H] for p in range(3)]
            link(dve, nc.vector.tensor_copy(part[0], self.rec[:]), self.rec_step, b)
            link(dve, nc.vector.tensor_tensor(self.recr[:], self.rec[:], part[0], ALU.subtract), self.rec_step, b)
            link(dve, nc.vector.tensor_copy(part[1], self.recr[:]), self.rec_step, b)
            nc.vector.tensor_tensor(part[2], self.recr[:], part[1], ALU.subtract).then_inc(*self.rp_ready.up())
        elif kind == "rt":
            dve.wait_ge(*self.rt_full.at(b, 1))
            nc.vector.tensor_copy(self.rt_sb[:], self.rt).then_inc(*self.rt_ready.up())
        elif kind == "bc":
            if n == 0:
                dve.wait_ge(*self.o_free.at(b, 4))
            dve.wait_ge(*self.bc_full.at(b, n + 1))
            nc.vector.tensor_tensor(self.on[:, n, :], self.osp[:, n, :], P[:, 7, :], ALU.mult).then_inc(*self.on_ready.up())
        elif kind == "out":
            dve.wait_ge(*self.out_full.at(b, 1))
            at = seq(resid, b)
            nc.vector.scalar_tensor_tensor(out=at, in0=P[:, 5, :], scalar=bias, in1=at,
                                           op0=ALU.add, op1=ALU.add).then_inc(*self.out_taken.up())


def cut(nc, dve, b, step, ps, bias, scale, full, rest, parts, ready):
    if ps is not None:
        link(dve, nc.vector.tensor_scalar(full, ps, bias, scale, ALU.add, ALU.mult), step, b)
    link(dve, nc.vector.tensor_copy(parts[:, 0, :], full), step, b)
    link(dve, nc.vector.tensor_tensor(rest, full, parts[:, 0, :], ALU.subtract), step, b)
    link(dve, nc.vector.tensor_copy(parts[:, 1, :], rest), step, b)
    nc.vector.tensor_tensor(parts[:, 2, :], rest, parts[:, 1, :], ALU.subtract).then_inc(*ready.up())


def phase_cross(nc, G, D, name):
    ph = Phase(nc, name)
    P, sb = G["P"], ph.sb
    A = Attention(ph, G, causal=False, parts=True, den_pass=False, prep=[("q", 0), ("k", 0)], late=[("v", 0), ("v", 1)])
    A.step = step = ph.count("step", 11)
    ld = ph.count("ld")
    wq, wk, wv = sb("wq", [128, C]), sb("wk", [128, C]), sb("wv", [128, 512])
    bqt, bkt, bot, bvt = sb("bq", [128, 1]), sb("bk", [128, 1]), sb("bo", [128, 1]), sb("bv", [KT, 512])
    ctb = sb("ctb", [128, LK])
    qf, qr, kf, kr = sb("qf", [128, T]), sb("qr", [128, T]), sb("kf", [128, LK]), sb("kr", [128, LK])
    va = sb("va", [KT, 2, 512])
    A.v = lambda kt, h: va[:, kt, 32 * h:32 * h + 32]
    ctb_ready, q_full, k_full = (ph.count(n, 1) for n in ("ctb_ready", "q_full", "k_full"))
    v_full, v_ready = ph.count("v_full", 2, 1), ph.count("v_ready", 2)
    A.wait_values = lambda pe, b: pe.wait_ge(*v_ready.at(b, 2))
    loads = [(wq[:], D[name + "_wq"]), (wk[:], D[name + "_wk"]), (wv[:], D[name + "_wv"]), (A.wo[:], D[name + "_wo"]),
             (bqt[:], D[name + "_bq"]), (bkt[:], D[name + "_bk"]), (bot[:], D[name + "_bo"]), (bvt[:], D[name + "_bv"]),
             ] + A.loads(D, "seld8")
    with nc.Block() as block:
        @block.sync
        def _(sp):
            load_all(sp, ld, loads)

        @block.gpsimd
        def _(pool):
            with nc.gpsimd.Fori(0, NB) as b:
                pool.wait_ge(*v_full.free(b, 1))
                nc.gpsimd.tensor_copy(ctb[:], seq(G["CT"], b)).then_inc(*ctb_ready.up())

        @block.tensor
        def _(pe):
            mm = nc.tensor.matmul
            pe.wait_ge(*ld.at((0, 0), 16 * len(loads)))
            A.pe_ahead(A.o_full.sem, 2)
            A.pe_ahead(v_full.sem, 1)

            def one_step(b, kind, n):
                if kind == "q":
                    v_ready.before(pe, b)
                    mm(P[:, 0, :], wq[:], seq(G["Y"], b), start=True, stop=True).then_inc(*q_full.up())
                elif kind == "k":
                    pe.wait_ge(*ctb_ready.at(b, 1))
                    mm(P[:, 1, 0:LK], wk[:], ctb[:], start=True, stop=True).then_inc(*k_full.up())
                elif kind == "v":
                    mm(P[0:KT, n, :], ctb[:, n * KT:(n + 1) * KT], wv[:], start=True, stop=True).then_inc(*v_full.up())
                else:
                    A.pe(pe, b, kind, n)

            A.run(nc.tensor, one_step)

        @block.scalar
        def _(act):
            A.act_ahead(G["scr"][:, 0:1])

            def one_step(b, kind, n):
                A.act(act, b, kind, n)

            A.run(nc.scalar, one_step)

        @block.vector
        def _(dve):
            dve.wait_ge(*ld.at((0, 0), 16 * len(loads)))
            A.dve_ahead(dve)

            def one_step(b, kind, n):
                if kind == "q":
                    dve.wait_ge(*q_full.at(b, 1))
                    cut(nc, dve, b, step, P[:, 0, :], bqt[:, 0:1], 8.0 ** -0.5, qf[:], qr[:], A.qp, A.parts_ready)
                elif kind == "k":
                    dve.wait_ge(*k_full.at(b, 1))
                    cut(nc, dve, b, step, P[:, 1, 0:LK], bkt[:, 0:1], 1.0, kf[:], kr[:], A.kp, A.parts_ready)
                elif kind == "v":
                    dve.wait_ge(*v_full.at(b, n + 1))
                    nc.vector.tensor_tensor(va[:, n, :], P[0:KT, n, :], bvt[:], ALU.add).then_inc(*v_ready.up())
                else:
                    A.dve(dve, b, kind, n, G["X"], bot[:, 0:1])

            A.run(nc.vector, one_step)
    ph.done()


def phase_conv_attention(nc, G, D):
    name = "L0f"
    ph = Phase(nc, name)
    P, sb = G["P"], ph.sb
    A = Attention(ph, G, causal=True, parts=True, den_pass=False, prep=[("conv", 0), ("q", 0), ("k", 0)],
                  late=[("v", n) for n in range(4)])
    A.step = step = ph.count("step", 15)
    ld = ph.count("ld")
    conv = sb("conv", [128, 3])
    wq, wqr, wk, wkr, wv = (sb(n, [128, w]) for n, w in (("wq", C), ("wqr", C), ("wk", C), ("wkr", C), ("wv", 512)))
    bvt = sb("bv", [128, 512])
    cq, sq, ck, sk = (sb(n, [128, T]) for n in ("cq", "sq", "ck", "sk"))
    A.mask_q, A.mask_k = sb("mask_q", [128, 128], BF16), sb("mask_k", [128, 128], BF16)
    hb, full, rest = sb("hb", [128, T]), sb("full", [128, T]), sb("rest", [128, T])
    va = sb("va", [128, 4, 512])
    A.v = lambda kt, h: va[:, kt, 32 * h:32 * h + 32]
    h_ready, q_full, k_full = ph.count("h_ready", 1), ph.count("q_full", 1), ph.count("k_full", 1)
    v_full, v_ready = ph.count("v_full", 4, 1), ph.count("v_ready", 4)
    loads = [(conv[:], D["L0f_conv"]), (wq[:], D["L0f_wq"]), (wqr[:], D["L0f_wqr"]), (wk[:], D["L0f_wk"]),
             (wkr[:], D["L0f_wkr"]), (wv[:], D["L0f_wv"]), (bvt[:], D["L0f_bv"]), (A.wo[:], D["L0f_wo"]),
             (cq[:], D["L0f_cq"]), (sq[:], D["L0f_sq"]), (ck[:], D["L0f_ck"]), (sk[:], D["L0f_sk"]),
             (A.mask_q[:], D["mask_q"]), (A.mask_k[:], D["mask_k"])] + A.loads(D, "seld8")
    A.wait_values = lambda pe, b: pe.wait_ge(*v_ready.at(b, 4))
    with nc.Block() as block:
        @block.sync
        def _(sp):
            load_all(sp, ld, loads)

        @block.tensor
        def _(pe):
            mm = nc.tensor.matmul
            pe.wait_ge(*ld.at((0, 0), 16 * len(loads)))
            A.pe_ahead(A.o_full.sem, 2)
            A.pe_ahead(v_full.sem, 1)

            def one_step(b, kind, n):
                if kind == "q":
                    pe.wait_ge(*h_ready.at(b, 1))
                    v_ready.before(pe, b)
                    mm(P[:, 0, :], wq[:], hb[:], start=True, stop=True)
                    mm(P[:, 1, :], wqr[:], hb[:], start=True, stop=True).then_inc(*q_full.up())
                elif kind == "k":
                    pe.wait_ge(*A.parts_ready.at(b, 1))
                    mm(P[:, 0, :], wk[:], hb[:], start=True, stop=True)
                    mm(P[:, 1, :], wkr[:], hb[:], start=True, stop=True).then_inc(*k_full.up())
                elif kind == "v":
                    if n >= 2:
                        pe.wait_ge(*v_ready.at(b, n - 1))
                    mm(P[:, n % 2, :], hb[:, n * 128:(n + 1) * 128], wv[:], start=True, stop=True).then_inc(*v_full.up())
                elif kind != "conv":
                    A.pe(pe, b, kind, n)

            A.run(nc.tensor, one_step)

        @block.scalar
        def _(act):
            A.act_ahead(G["scr"][:, 0:1])

            def one_step(b, kind, n):
                A.act(act, b, kind, n)

            A.run(nc.scalar, one_step)

        @block.vector
        def _(dve):
            dve.wait_ge(*ld.at((0, 0), 16 * len(loads)))
            A.dve_ahead(dve)

            def one_step(b, kind, n):
                if kind == "conv":
                    z = seq(G["Z"], b)
                    dve.wait_ge(*v_full.free(b, 1))
                    link(dve, nc.vector.tensor_scalar(hb[:], z, conv[:, 2:3], None, ALU.mult), step, b)
                    link(dve, nc.vector.scalar_tensor_tensor(out=hb[:, 1:T], in0=z[:, 0:T - 1], scalar=conv[:, 1:2],
                                                             in1=hb[:, 1:T], op0=ALU.mult, op1=ALU.add), step, b)
                    nc.vector.scalar_tensor_tensor(out=hb[:, 2:T], in0=z[:, 0:T - 2], scalar=conv[:, 0:1],
                                                   in1=hb[:, 2:T], op0=ALU.mult, op1=ALU.add).then_inc(*h_ready.up())
                elif kind in "qk":
                    ready, cos, sin, parts = (q_full, cq, sq, A.qp) if kind == "q" else (k_full, ck, sk, A.kp)
                    dve.wait_ge(*ready.at(b, 1))
                    if kind == "k":
                        dve.wait_ge(*A.parts_ready.at(b, 1))
                    nc.vector.tensor_tensor(full[:], P[:, 0, :], cos[:], ALU.mult)
                    link(dve, nc.vector.tensor_tensor(rest[:], P[:, 1, :], sin[:], ALU.mult), step, b)
                    link(dve, nc.vector.tensor_tensor(full[:], full[:], rest[:], ALU.add), step, b)
                    cut(nc, dve, b, step, None, None, None, full[:], rest[:], parts, A.parts_ready)
                elif kind == "v":
                    dve.wait_ge(*v_full.at(b, n + 1))
                    nc.vector.tensor_tensor(va[:, n, :], P[:, n % 2, :], bvt[:], ALU.add).then_inc(*v_ready.up())
                else:
                    A.dve(dve, b, kind, n, G["Y"], G["zero"][:, 0:1])

            A.run(nc.vector, one_step)
    ph.done()


def phase_latent(nc, G, D, name):
    window = name == "L0x"
    ph = Phase(nc, name)
    P, sb = G["P"], ph.sb
    rot, lat, up_dim = (64, 32, 64) if window else (32, 16, 32)
    per_b = 128 // rot
    prep = [("qc", 0), ("kvc", 0), ("kk", 0)] if window else [("kk", 0)]
    A = Attention(ph, G, causal=not window, parts=False, den_pass=window, mask=window, prep=prep, late=[("lat", 0)])
    A.step = step = ph.count("step", 4)

    ld, pre_full, pre_done = ph.count("ld"), ph.count("pre_full"), ph.count("pre_done")
    keys = A.keys
    nq = 48 if window else 128
    wa, wb = sb("wa", [128, H, 128]), sb("wb", [128, H // per_b, 128])
    wqT = A.prob[0:up_dim, 0:4, :].rearrange("p s (h n) -> p (s h) n", n=128)[:, :, 0:nq]
    woh = A.prob[0:up_dim, 4:8, :].rearrange("p s (h n) -> p (s h) n", n=128)
    wkT = A.prob[0:up_dim, 8, 0:H * lat].rearrange("p (h n) -> p h n", n=lat)
    wvT = A.prob[0:up_dim, 9, :].rearrange("p (h n) -> p h n", n=32)
    wka, wkb, wlat = sb("wka", [128, 128]), sb("wkb", [128, 128]), sb("wlat", [128, 128 if window else lat])
    cq, sq, ck, sk = sb("cq", [128, T]), sb("sq", [128, T]), sb("ck", [128, keys]), sb("sk", [128, keys])
    src = sb("src", [128, keys])
    kf, kt_, tmp = A.k_first, sb("kt", [128, keys]), sb("tmp", [rot, 2, T])
    va = sb("va", [A.nk, A.nkt, 32])
    A.v = lambda kt, h: va[:, kt, :]
    loads = [(t, D[f"{name}_{n}"]) for t, n in ((wa[:], "wa"), (wb[:], "wb"), (wqT, "wqT"), (wkT, "wkT"), (wvT, "wvT"),
             (woh, "woh"), (wka[:], "wka"), (wkb[:], "wkb"), (wlat[:], "wlat"), (cq[:], "cq"), (sq[:], "sq"),
             (ck[:], "ck"), (sk[:], "sk"))]
    loads += A.loads(D, "seld0" if window else "seld16")
    if window:
        wqd, qc, kvc = sb("wqd", [128, 128]), sb("qc", [128, T]), sb("kvc", [128, LK])
        segc_i, segr_i = sb("segc_i", [128, NB * QT], I32), sb("segr_i", [KT, NB, T], I32)
        segc, segr = sb("segc", [128, NB, QT]), sb("segr", [KT, NB, T])
        keyrow, keycol = sb("keyrow", [128, LK]), sb("keycol", [KT, 2])
        A.mask_q, A.mask_k = sb("mask_q", [128, NB, QT, LK], BF16), sb("mask_k", [KT, NB, 2, T], BF16)
        dq, dk = sb("dq", [128, QT, LK]), sb("dk", [KT, 2, T])
        A.ones = sb("ones", [128, 32])
        qc_full, kvc_full, qc_ready, kvc_ready = (ph.count(n, 1) for n in ("qc_full", "kvc_full", "qc_ready", "kvc_ready"))
        masks_ready = ph.count("masks_ready")
        A.mask_of = lambda buf, b: (buf[:, b[0] + b[1], :, :] if isinstance(b[0], int) else
                                    buf[:, bass.ds(b[0] + b[1], 1), :, :].rearrange("p a x y -> p (a x) y"))
        loads += [(wqd[:], D["L0x_wqd"]), (segc_i[:], D["segc"]), (segr_i[:], D["segr"]),
                  (keyrow[:], D["keyrow"]), (keycol[:], D["keycol"])]
        q_in, k_in = qc, kvc
    else:
        A.mask_q, A.mask_k = sb("mask_q", [128, 128], BF16), sb("mask_k", [128, 128], BF16)
        loads += [(A.mask_q[:], D["mask_q"]), (A.mask_k[:], D["mask_k"])]
        q_in, k_in = src, src
    ahead_step, ahead_done = ph.count("ahead_step"), ph.count("ahead_done")
    src_ready = ph.count("src_ready", 1)
    k_full, k_ready, v_ready = (ph.count(n, 1) for n in ("k_full", "k_ready", "v_ready"))
    v_full = ph.count("v_full", 1, 1)
    b_full = ph.count("b_full", H // per_b)
    t_ready, qe_ready = ph.count("t_ready", H), ph.count("qe_ready", H, 2)
    A.k_ready = k_ready
    A.wait_values = lambda pe, b: pe.wait_ge(*v_ready.at(b, 1))

    def wait_q(pe, b, h):
        pe.wait_ge(*qe_ready.at(b, h + 1))
        if window:
            pe.wait_ge(*masks_ready.at(0, 2 * NB))

    A.wait_q = wait_q
    with nc.Block() as block:
        @block.sync
        def _(sp):
            load_all(sp, ld, loads)

        @block.gpsimd
        def _(pool):
            nc.gpsimd.memset(tmp[:], 0.0).then_inc(qe_ready.sem, 2)
            with nc.gpsimd.Fori(0, NB) as b:
                pool.wait_ge(*v_full.free(b, 1))
                nc.gpsimd.tensor_copy(src[:], seq(G["CT"] if window else G["Z"], b)).then_inc(*src_ready.up())
                for h in range(H):
                    pool.wait_ge(*t_ready.at(b, h + 1))
                    nc.gpsimd.tensor_tensor(A.qe[0:rot, h, :], A.qe[0:rot, h, :], tmp[:, h % 2, :], ALU.add)\
                        .then_inc(*qe_ready.up())

        @block.tensor
        def _(pe):
            mm = nc.tensor.matmul
            pe.wait_ge(*ld.at((0, 0), 16 * len(loads)))
            for h in range(H):
                mm(P[0:nq, 0, h * lat:(h + 1) * lat], wqT[:, h, :], wkT[:, h, :], start=True, stop=True)
            for h in range(H):
                m = mm(P[32 * (h % 4):32 * (h % 4) + 32, 1, (h // 4) * C:(h // 4 + 1) * C], wvT[:, h, :], woh[:, h, :],
                       start=True, stop=True)
            m.then_inc(*pre_full.up())
            A.pe_ahead(A.o_full.sem, 2)
            A.pe_ahead(v_full.sem, 1)
            pe.wait_ge(*pre_done.at((0, 0), 2))
            pe.wait_ge(*ahead_done.at((0, 0), 1))

            def one_step(b, kind, n):
                if kind == "qc":
                    A.out_taken.one_before(pe, b)
                    mm(P[:, 5, :], wqd[:], seq(G["Y"], b), start=True, stop=True).then_inc(*qc_full.up())
                elif kind == "kvc":
                    pe.wait_ge(*src_ready.at(b, 1))
                    pe.wait_ge(*qc_ready.at(b, 1))
                    mm(P[:, 5, 0:LK], wlat[:], src[:], start=True, stop=True).then_inc(*kvc_full.up())
                elif kind == "lat":
                    for kt in range(A.nkt):
                        m = mm(P[0:A.nk, 0, 32 * kt:32 * kt + lat], src[:, kt * A.nk:(kt + 1) * A.nk], wlat[:, 0:lat],
                               start=True, stop=True)
                    m.then_inc(*v_full.up())
                elif kind == "kk":
                    pe.wait_ge(*(kvc_ready if window else src_ready).at(b, 1))
                    v_ready.before(pe, b)
                    mm(P[:, 0, 0:keys], wka[:], k_in[:], start=True, stop=True)
                    mm(P[:, 1, 0:keys], wkb[:], k_in[:], start=True, stop=True).then_inc(*k_full.up())
                elif kind == "head":
                    if n == 0:
                        A.out_taken.one_before(pe, b)
                        pe.wait_ge(*k_ready.at(b, 1))
                    if n % per_b == 0:
                        if n:
                            pe.wait_ge(*t_ready.at(b, n))
                        mm(P[:, 5, :], wb[:, n // per_b, :], q_in[:], start=True, stop=True).then_inc(*b_full.up())
                    bank = A.first_bank(pe, b, kind, n)
                    mm(P[:, bank, :], wa[:, n, :], q_in[:], start=True, stop=True).then_inc(*A.s_full.up())
                else:
                    A.pe(pe, b, kind, n)

            A.run(nc.tensor, one_step)

        @block.scalar
        def _(act):
            A.act_ahead(G["scr"][:, 0:1])
            act.wait_ge(*pre_full.at((0, 0), 1))
            nc.scalar.copy(wa[0:nq, :, rot:rot + lat], P[0:nq, 0, 0:H * lat].rearrange("p (h r) -> p h r", r=lat))\
                .then_inc(*pre_done.up())
            nc.scalar.copy(A.wo[:], P[:, 1, :].rearrange("p (g c) -> p g c", c=C)).then_inc(*pre_done.up())

            def one_step(b, kind, n):
                if kind == "qc":
                    act.wait_ge(*qc_full.at(b, 1))
                    nc.scalar.copy(qc[:], P[:, 5, :]).then_inc(*qc_ready.up())
                elif kind == "kvc":
                    act.wait_ge(*kvc_full.at(b, 1))
                    nc.scalar.copy(kvc[:], P[:, 5, 0:LK]).then_inc(*kvc_ready.up())
                elif kind == "lat":
                    act.wait_ge(*v_full.at(b, 1))
                    nc.scalar.copy(va[:, :, 0:lat], P[0:A.nk, 0, 0:32 * A.nkt].rearrange("p (k r) -> p k r", r=32)[:, :, 0:lat])\
                        .then_inc(*v_ready.up())
                else:
                    A.act(act, b, kind, n)

            A.run(nc.scalar, one_step)

        @block.vector
        def _(dve):
            dve.wait_ge(*ld.at((0, 0), 16 * len(loads)))
            A.dve_ahead(dve)
            if window:
                link(dve, nc.vector.tensor_copy(segc[:].rearrange("p b t -> p (b t)"), segc_i[:]), ahead_step, (0, 0))
                link(dve, nc.vector.tensor_copy(segr[:], segr_i[:]), ahead_step, (0, 0))
                nc.vector.memset(A.ones[:], 1.0).then_inc(*ahead_done.up())
                for s in range(NB):
                    for qt in range(QT):
                        m = nc.vector.tensor_scalar(dq[:, qt, :], keyrow[:], segc[:, s, qt:qt + 1], None, ALU.subtract)
                    link(dve, m, ahead_step, (0, 0))
                    link(dve, nc.vector.tensor_tensor(dq[:], dq[:], dq[:], ALU.mult), ahead_step, (0, 0))
                    nc.vector.tensor_scalar(A.mask_q[:, s, :, :], dq[:], 1.5, -BIG, ALU.is_gt, ALU.mult).then_inc(*masks_ready.up())
                    for kt in range(2):
                        m = nc.vector.tensor_scalar(dk[:, kt, :], segr[:, s, :], keycol[:, kt:kt + 1], None, ALU.subtract)
                    link(dve, m, ahead_step, (0, 0))
                    link(dve, nc.vector.tensor_tensor(dk[:], dk[:], dk[:], ALU.mult), ahead_step, (0, 0))
                    nc.vector.tensor_scalar(A.mask_k[:, s, :, :], dk[:], 1.5, -BIG, ALU.is_gt, ALU.mult).then_inc(*masks_ready.up())
                    dve.wait_ge(*masks_ready.at(0, 2 * (s + 1)))
            else:
                link(dve, nc.vector.memset(va[:, :, lat:32], 0.0), ahead_step, (0, 0))
                nc.vector.memset(va[:, :, lat:lat + 1], 1.0).then_inc(*ahead_done.up())

            def one_step(b, kind, n):
                if kind == "kk":
                    A.k_moved.before(dve, b)
                    dve.wait_ge(*k_full.at(b, 1))
                    nc.vector.tensor_tensor(kf[:], P[:, 0, 0:keys], ck[:], ALU.mult)
                    link(dve, nc.vector.tensor_tensor(kt_[:], P[:, 1, 0:keys], sk[:], ALU.mult), step, b)
                    nc.vector.tensor_tensor(kf[:], kf[:], kt_[:], ALU.add).then_inc(*k_ready.up())
                elif kind == "head":
                    if n % per_b == 0:
                        dve.wait_ge(*b_full.at(b, n // per_b + 1))
                    use = A.bank_of_step[kind, n]
                    dve.wait_ge(*A.s_full.at(b, use))
                    nc.vector.tensor_tensor(A.qe[:, n, :], P[:, (use - 1) % 2, :], cq[:], ALU.mult).then_inc(*A.s_free.up())
                    dve.wait_ge(*qe_ready.free(b, n + 1))
                    j = n % per_b
                    nc.vector.tensor_tensor(tmp[:, n % 2, :], P[rot * j:rot * j + rot, 5, :],
                                            sq[rot * j:rot * j + rot, :], ALU.mult).then_inc(*t_ready.up())
                elif kind not in ("qc", "kvc", "lat"):
                    A.dve(dve, b, kind, n, G["X"] if window else G["Y"], G["zero"][:, 0:1])

            A.run(nc.vector, one_step)
    ph.done()


def one_hot_of_max(nc, dve, b, step, logits, mx, eq, prio, top, hot, E):
    wide = [128, QT, E]
    link(dve, nc.vector.tensor_reduce(mx, logits, AX.X, ALU.max), step, b)
    link(dve, nc.vector.tensor_tensor(eq, logits, mx.unsqueeze(2).to_broadcast(wide), ALU.is_ge), step, b)
    link(dve, nc.vector.tensor_tensor(eq, eq, prio, ALU.mult), step, b)
    link(dve, nc.vector.tensor_reduce(top, eq, AX.X, ALU.max), step, b)
    return nc.vector.tensor_tensor(hot, eq, top.unsqueeze(2).to_broadcast(wide), ALU.is_equal)


def phase_experts(nc, G, D, name):
    one = name == "L0m"
    ph = Phase(nc, name)
    P, sb = G["P"], ph.sb
    E = 4 if one else 8
    NM = 4
    NC = 4 if one else 5
    step = ph.count("step", 17 if one else 26)
    ld = ph.count("ld")
    router, prio, sel = sb("router", [128, E]), sb("prio", [128, QT, E]), sb("sel", [E, NM, 128])
    if one:
        w1, w2 = sb("w1", [128, E, 1024]), sb("w2", [128, E, 4, C])
        hm = sb("hm", [128, E, T])
    else:
        w1, w2 = sb("w1", [128, NC, 2, 128]), sb("w2", [128, NC, C])
        ebias = sb("ebias", [128, QT, E])
    loads = [(router[:], D[name + "_router"]), (prio[:], D[name + "_prio"]), (sel[:], D[name + "_sel"]),
             (w1[:], D[name + "_w1"]), (w2[:], D[name + "_w2"])] + ([] if one else [(ebias[:], D["L2m_ebias"])])
    zb = sb("zb", [128, T])
    lg, eq, hot = (sb(n, [128, QT, E]) for n in ("lg", "eq", "hot"))
    lg2, hot2, e2, r2 = sb("lg2", [128, QT, E]), sb("hot2", [128, QT, E]), sb("e2", [128, QT]), sb("r2", [128, QT])
    mx, top, mx2 = sb("mx", [128, QT]), sb("top", [128, QT]), sb("mx2", [128, QT])
    hott = sb("hott", [E, T])
    me = sb("me", [128, NM, T])
    ex, rc, act_ = sb("ex", [128, 2, T]), sb("rc", [128, T]), sb("act", [128, NC, T])
    acc, prod = sb("acc", [128, T]), sb("prod", [128, T])
    n_out = E if one else 1
    zb_ready, lg_full, hot_ready, ht_full, hott_ready = (
        ph.count(n, 1, a) for n, a in (("zb_ready", 0), ("lg_full", 0), ("hot_ready", 0), ("ht_full", 0), ("hott_ready", 0)))
    gap, gap_done = ph.count("gap", 0 if one else 1), ph.count("gap_done", 0 if one else 1)
    masks_full, me_ready, hm_ready = ph.count("masks_full", NM), ph.count("me_ready", NM), ph.count("hm_ready", NM if one else 0)
    gv_full, gv_free = ph.count("gv_full", NC), ph.count("gv_free", NC, 2)
    exp_ready, act_ready = ph.count("exp_ready", NC), gv_free
    out_full, x_done = ph.count("out_full", n_out, 1), ph.count("x_done", 1, 1)
    with nc.Block() as block:
        @block.sync
        def _(sp):
            load_all(sp, ld, loads)

        @block.gpsimd
        def _(pool):
            with nc.gpsimd.Fori(0, NB) as b:
                pool.wait_ge(*out_full.free(b, 1))
                nc.gpsimd.tensor_copy(zb[:], seq(G["Z"], b)).then_inc(*zb_ready.up())
                if one:
                    pool.wait_ge(*zb_ready.at(b, 1))
                    for e in range(E):
                        pool.wait_ge(*me_ready.at(b, e + 1))
                        nc.gpsimd.tensor_tensor(hm[:, e, :], zb[:], me[:, e, :], ALU.mult).then_inc(*hm_ready.up())

        @block.tensor
        def _(pe):
            mm = nc.tensor.matmul
            pe.wait_ge(*ld.at(0, 16 * len(loads)))
            one_ = G["identb"][0:32, 0:32]
            mm(P[0:32, 7, 0:32], one_, one_, start=True, stop=True).then_inc(out_full.sem, 1)
            with nc.tensor.Fori(0, NB) as b:
                pe.wait_ge(*gv_free.free(b, 2))
                pe.wait_ge(*zb_ready.at(b, 1))
                for t in range(QT):
                    m = mm(P[:, 0, t * E:(t + 1) * E], zb[:, t * 128:(t + 1) * 128], router[:], start=True, stop=True)
                m.then_inc(*lg_full.up())
                pe.wait_ge(*hot_ready.at(b, 1))
                for t in range(QT):
                    m = nc.tensor.transpose(P[0:E, 1, t * 128:(t + 1) * 128], hot[:, t, :], G["ident"][:])
                m.then_inc(*ht_full.up())
                pe.wait_ge(*hott_ready.at(b, 1))
                pe.wait_ge(*x_done.free(b, 1))
                for n in range(NM):
                    mm(P[:, 2 + n, :], sel[:, n, :], hott[:], start=True, stop=True).then_inc(*masks_full.up())
                if not one:
                    pe.wait_ge(*me_ready.at(b, NM))
                for c in range(NC):
                    pe.wait_ge(*gv_free.free(b, c + 1))
                    for half in range(2):
                        bank = 2 * (c % 2) + half
                        if one:
                            for e in range(E):
                                if c == half == 0:
                                    pe.wait_ge(*hm_ready.at(b, e + 1))
                                lhs = w1[:, e, half * 512 + c * 128:half * 512 + c * 128 + 128]
                                m = mm(P[:, bank, :], lhs, hm[:, e, :], start=e == 0, stop=e == E - 1)
                        else:
                            m = mm(P[:, bank, :], w1[:, c, half, :], zb[:], start=True, stop=True)
                    m.then_inc(*gv_full.up())
                pe.wait_ge(*gv_free.at(b, NC))
                for e in range(n_out):
                    for c in range(NC):
                        m = mm(P[:, 4 + e, :], w2[:, e, c, :] if one else w2[:, c, :], act_[:, c, :],
                               start=c == 0, stop=c == NC - 1)
                    m.then_inc(*out_full.up())

        @block.scalar
        def _(act):
            with nc.scalar.Fori(0, NB) as b:
                if not one:
                    act.wait_ge(*gap.at(b, 1))
                    nc.scalar.activation(e2[:], mx2[:], ACT.Exp).then_inc(*gap_done.up())
                for n in range(NM):
                    act.wait_ge(*masks_full.at(b, n + 1))
                    nc.scalar.copy(me[:, n, :], P[:, 2 + n, :]).then_inc(*me_ready.up())
                for c in range(NC):
                    act.wait_ge(*gv_full.at(b, c + 1))
                    act.wait_ge(*gv_free.free(b, c + 1))
                    nc.scalar.activation(ex[:, c % 2, :], P[:, 2 * (c % 2), :], ACT.Tanh, scale=0.5).then_inc(*exp_ready.up())

        @block.vector
        def _(dve):
            dve.wait_ge(*ld.at(0, 16 * len(loads)))
            nc.vector.memset(acc[:, 0:1], 0.0).then_inc(gv_free.sem, 2)
            dve.wait_ge(gv_free.sem, 2)
            nc.vector.memset(acc[:, 0:1], 0.0).then_inc(x_done.sem, 1)
            dve.wait_ge(x_done.sem, 1)
            with nc.vector.Fori(0, NB) as b:
                dve.wait_ge(*lg_full.at(b, 1))
                ps = P[:, 0, 0:QT * E].rearrange("p (t e) -> p t e", e=E)
                if one:
                    link(dve, nc.vector.tensor_copy(lg[:], ps), step, b)
                    one_hot_of_max(nc, dve, b, step, lg[:], mx[:], eq[:], prio[:], top[:], hot[:], E)\
                        .then_inc(*hot_ready.up())
                else:
                    link(dve, nc.vector.tensor_tensor(lg[:], ps, ebias[:], ALU.add), step, b)
                    link(dve, one_hot_of_max(nc, dve, b, step, lg[:], mx[:], eq[:], prio[:], top[:], hot[:], E), step, b)
                    link(dve, nc.vector.scalar_tensor_tensor(out=lg2[:], in0=hot[:], scalar=-BIG, in1=lg[:],
                                                             op0=ALU.mult, op1=ALU.add), step, b)
                    link(dve, one_hot_of_max(nc, dve, b, step, lg2[:], mx2[:], eq[:], prio[:], top[:], hot2[:], E), step, b)
                    nc.vector.tensor_tensor(mx2[:], mx2[:], mx[:], ALU.subtract).then_inc(*gap.up())
                    dve.wait_ge(*gap_done.at(b, 1))
                    link(dve, nc.vector.tensor_scalar(r2[:], e2[:], 1.0, None, ALU.add), step, b)
                    link(dve, nc.vector.reciprocal(r2[:], r2[:]), step, b)
                    wide = [128, QT, E]
                    link(dve, nc.vector.tensor_tensor(hot2[:], hot2[:], e2[:].unsqueeze(2).to_broadcast(wide), ALU.mult), step, b)
                    link(dve, nc.vector.tensor_tensor(hot2[:], hot2[:], hot[:], ALU.add), step, b)
                    nc.vector.tensor_tensor(hot[:], hot2[:], r2[:].unsqueeze(2).to_broadcast(wide), ALU.mult).then_inc(*hot_ready.up())
                dve.wait_ge(*ht_full.at(b, 1))
                nc.vector.tensor_copy(hott[:], P[0:E, 1, :]).then_inc(*hott_ready.up())
                for c in range(NC):
                    dve.wait_ge(*exp_ready.at(b, c + 1))
                    g, v, e = P[:, 2 * (c % 2), :], P[:, 2 * (c % 2) + 1, :], ex[:, c % 2, :]
                    dve.wait_ge(*gv_free.free(b, c + 2))
                    link(dve, nc.vector.scalar_tensor_tensor(out=rc[:], in0=e, scalar=1.0, in1=g, op0=ALU.add, op1=ALU.mult), step, b)
                    if not one and c < NM:
                        link(dve, nc.vector.tensor_tensor(rc[:], rc[:], me[:, c, :], ALU.mult), step, b)
                    nc.vector.scalar_tensor_tensor(out=act_[:, c, :], in0=v, scalar=0.5, in1=rc[:], op0=ALU.mult, op1=ALU.mult)\
                        .then_inc(*gv_free.up())
                x = seq(G["X"], b)
                link(dve, nc.vector.tensor_tensor(x, x, seq(G["Y"], b), ALU.add), step, b)
                if one:
                    for e in range(E):
                        dve.wait_ge(*out_full.at(b, e + 1))
                        link(dve, nc.vector.tensor_tensor(prod[:], P[:, 4 + e, :], me[:, e, :], ALU.mult), step, b)
                        ins = nc.vector.tensor_tensor(x, x, prod[:], ALU.add)
                        if e < E - 1:
                            link(dve, ins, step, b)
                        else:
                            ins.then_inc(*x_done.up())
                else:
                    dve.wait_ge(*out_full.at(b, 1))
                    nc.vector.tensor_tensor(x, x, P[:, 4, :], ALU.add).then_inc(*x_done.up())
    ph.done()


def phase_tree(nc, G, D):
    ph = Phase(nc, "L1f")
    P, sb = G["P"], ph.sb
    N = 255
    step = ph.count("step", 10)
    ld, pre_full, pre_done = ph.count("ld"), ph.count("pre_full"), ph.count("pre_done")
    wq, rt, lvT, woT, bias = sb("wq", [128, C]), sb("rt", [128, N]), sb("lvT", [128, 256]), sb("woT", [128, C]), sb("bias", [128, 1])
    gw, lw = sb("gw", [128, N]), sb("lw", [128, 2, C])
    yb, ex, g, og = sb("yb", [128, T]), sb("ex", [128, QT, 256]), sb("g", [128, QT, 256]), sb("og", [128, QT, 256])
    lp = [sb("lp0", [128, QT, 256]), sb("lp1", [128, QT, 256])]
    lt = sb("lt", [128, 2, T])
    loads = [(wq[:], D["L1f_wq"]), (rt[:], D["L1f_rt"]), (lvT[:], D["L1f_lvT"]), (woT[:], D["L1f_woT"]), (bias[:], D["L1f_bias"])]
    yb_ready, z_full, e_ready, lp_ready, lt_full, lt_ready = (
        ph.count(n, k, a) for n, k, a in (("yb_ready", 1, 0), ("z_full", 1, 1), ("e_ready", 1, 0), ("lp_ready", 1, 0),
                                          ("lt_full", 1, 0), ("lt_ready", 1, 0)))
    y_full = ph.count("y_full", 1)
    z = P[:, 0:2, :].rearrange("p b (t n) -> p (b t) n", n=256)
    with nc.Block() as block:
        @block.sync
        def _(sp):
            load_all(sp, ld, loads)

        @block.gpsimd
        def _(pool):
            with nc.gpsimd.Fori(0, NB) as b:
                pool.wait_ge(*z_full.free(b, 1))
                nc.gpsimd.tensor_copy(yb[:], seq(G["Y"], b)).then_inc(*yb_ready.up())

        @block.tensor
        def _(pe):
            mm = nc.tensor.matmul
            pe.wait_ge(*ld.at(0, 16 * len(loads)))
            mm(P[:, 0, 0:N], wq[:], rt[:], start=True, stop=True)
            for c in range(2):
                m = mm(P[:, 1, c * C:(c + 1) * C], lvT[:, c * 128:(c + 1) * 128], woT[:], start=True, stop=True)
            m.then_inc(*pre_full.up())
            mm(P[0:32, 7, 0:32], G["identb"][0:32, 0:32], G["identb"][0:32, 0:32], start=True, stop=True).then_inc(z_full.sem, 1)
            pe.wait_ge(*pre_done.at(0, 2))
            with nc.tensor.Fori(0, NB) as b:
                pe.wait_ge(*yb_ready.at(b, 1))
                for t in range(QT):
                    m = mm(z[:, t, 0:N], yb[:, t * 128:(t + 1) * 128], gw[:], start=True, stop=True)
                m.then_inc(*z_full.up())
                pe.wait_ge(*lp_ready.at(b, 1))
                for t in range(QT):
                    for c in range(2):
                        m = nc.tensor.transpose(P[:, 2 + c, t * 128:(t + 1) * 128], lp[1][:, t, c * 128:(c + 1) * 128], G["ident"][:])
                m.then_inc(*lt_full.up())
                pe.wait_ge(*lt_ready.at(b, 1))
                for c in range(2):
                    m = mm(P[:, 4, :], lw[:, c, :], lt[:, c, :], start=c == 0, stop=c == 1)
                m.then_inc(*y_full.up())

        @block.scalar
        def _(act):
            act.wait_ge(*pre_full.at(0, 1))
            nc.scalar.copy(gw[:], P[:, 0, 0:N]).then_inc(*pre_done.up())
            nc.scalar.copy(lw[:], P[:, 1, 0:2 * C].rearrange("p (c n) -> p c n", c=2)).then_inc(*pre_done.up())
            with nc.scalar.Fori(0, NB) as b:
                act.wait_ge(*z_full.at(b, 1))
                nc.scalar.activation(ex[:, :, 0:N], z[:, :, 0:N], ACT.Tanh, scale=0.5).then_inc(*e_ready.up())
                act.wait_ge(*lt_full.at(b, 1))
                nc.scalar.copy(lt[:], P[:, 2:4, :]).then_inc(*lt_ready.up())

        @block.vector
        def _(dve):
            dve.wait_ge(*ld.at(0, 16 * len(loads)))
            with nc.vector.Fori(0, NB) as b:
                dve.wait_ge(*e_ready.at(b, 1))
                link(dve, nc.vector.tensor_scalar(g[:, :, 0:N], ex[:, :, 0:N], 0.5, 0.5, ALU.mult, ALU.add), step, b)
                link(dve, nc.vector.tensor_scalar(og[:, :, 0:N], g[:, :, 0:N], -1.0, 1.0, ALU.mult, ALU.add), step, b)
                nc.vector.tensor_copy(lp[0][:, :, 0:1], og[:, :, 0:1])
                link(dve, nc.vector.tensor_copy(lp[0][:, :, 1:2], g[:, :, 0:1]), step, b)
                for level in range(1, 8):
                    n = 2 ** level
                    old, new = lp[(level - 1) % 2][:, :, 0:n], lp[level % 2][:, :, 0:2 * n].rearrange("p t (n s) -> p t n s", s=2)
                    nc.vector.tensor_tensor(new[:, :, :, 0], old, og[:, :, n - 1:2 * n - 1], ALU.mult)
                    ins = nc.vector.tensor_tensor(new[:, :, :, 1], old, g[:, :, n - 1:2 * n - 1], ALU.mult)
                    if level < 7:
                        link(dve, ins, step, b)
                    else:
                        ins.then_inc(*lp_ready.up())
                dve.wait_ge(*y_full.at(b, 1))
                x = seq(G["X"], b)
                link(dve, nc.vector.scalar_tensor_tensor(out=x, in0=P[:, 4, :], scalar=bias[:, 0:1], in1=x,
                                                         op0=ALU.add, op1=ALU.add), step, b)
    ph.done()


def phase_over_heads(nc, G, D):
    ph = Phase(nc, "L3x")
    P, sb = G["P"], ph.sb
    NSEL, KPER = 14, 3
    step = ph.count("step", 2 * 4 + 8 * 2)
    ld = ph.count("ld")
    wq, wk, wv, wo = sb("wq", [128, C]), sb("wk", [128, C]), sb("wv", [128, 512]), sb("wo", [128, 4, C])
    selq, selk = sb("selq", [128, 8, 3, 128], BF16), sb("selk", [128, H, 3, 128], BF16)
    loads = [(wq[:], D["L3x_wq"]), (wk[:], D["L3x_wk"]), (wv[:], D["L3x_wv"]), (wo[:], D["L3x_wo"]),
             (selq[:], D["selq"]), (selk[:], D["selk"])]
    ctb = sb("ctb", [128, LK])
    qf, qr, kf, kr = sb("qf", [128, T]), sb("qr", [128, T]), sb("kf", [128, LK]), sb("kr", [128, LK])
    qp, kp = sb("qp", [128, 3, T], BF16), sb("kp", [128, 3, LK], BF16)
    qs, ks = sb("qs", [128, 8, T], BF16), sb("ks", [128, H, LK], BF16)
    va = sb("va", [KT, 2, 512])
    mx, sm = sb("mx", [KT, 128]), sb("sm", [KT, 2, 128])
    ex = sb("ex", [KT, 2, H, 128])
    pall = sb("pall", [KT, 2, H, T])
    on = sb("on", [128, 4, T])
    ctb_ready, q_full, k_full = (ph.count(n, 1) for n in ("ctb_ready", "q_full", "k_full"))
    v_full, v_ready, parts_ready = ph.count("v_full", 2, 1), ph.count("v_ready", 2), ph.count("parts_ready", 2)
    ring_full, ring_done = ph.count("ring_full", NSEL), ph.count("ring_done", NSEL, 4)
    st_full, sub_done, exp_done, sum_ready = (ph.count(n, 8) for n in ("st_full", "sub_done", "exp_done", "sum_ready"))
    p_ready = ph.count("p_ready", 8, 2)
    o_full, on_ready, out_full, x_done = ph.count("o_full", 4), ph.count("on_ready", 4), ph.count("out_full", 1), ph.count("x_done", 1, 1)
    with nc.Block() as block:
        @block.sync
        def _(sp):
            load_all(sp, ld, loads)

        @block.gpsimd
        def _(pool):
            nc.gpsimd.memset(ctb[:, 0:1], 0.0).then_inc(p_ready.sem, 2)
            pool.wait_ge(p_ready.sem, 2)
            with nc.gpsimd.Fori(0, NB) as b:
                pool.wait_ge(*v_full.free(b, 1))
                nc.gpsimd.tensor_copy(ctb[:], seq(G["CT"], b)).then_inc(*ctb_ready.up())
                for u in range(8):
                    kt, qt = divmod(u, QT)
                    pool.wait_ge(*sum_ready.at(b, u + 1))
                    nc.gpsimd.tensor_tensor(pall[:, kt, :, qt * 128:(qt + 1) * 128], ex[:, u % 2, :, :],
                                            sm[:, u % 2, :].unsqueeze(1).to_broadcast([KT, H, 128]), ALU.mult)\
                        .then_inc(*p_ready.up())

        @block.tensor
        def _(pe):
            mm = nc.tensor.matmul
            pe.wait_ge(*ld.at(0, 16 * len(loads)))
            mm(P[0:32, 7, 0:32], G["identb"][0:32, 0:32], G["identb"][0:32, 0:32], start=True, stop=True).then_inc(v_full.sem, 1)
            with nc.tensor.Fori(0, NB) as b:
                pe.wait_ge(*x_done.free(b, 1))
                mm(P[:, 0, :], wq[:], seq(G["Y"], b), start=True, stop=True).then_inc(*q_full.up())
                pe.wait_ge(*ctb_ready.at(b, 1))
                mm(P[:, 1, 0:LK], wk[:], ctb[:], start=True, stop=True).then_inc(*k_full.up())
                for kt in range(2):
                    mm(P[0:KT, 2 + kt, :], ctb[:, kt * KT:(kt + 1) * KT], wv[:], start=True, stop=True).then_inc(*v_full.up())
                pe.wait_ge(*parts_ready.at(b, 2))
                for i in range(NSEL):
                    bank = 4 + i % 4
                    pe.wait_ge(*ring_done.free(b, i + 1))
                    if i < 8:
                        for part in range(3):
                            m = mm(P[:, bank, :], selq[:, i, part, :], qp[:, part, :], start=part == 0, stop=part == 2)
                    else:
                        for j, h in enumerate(range((i - 8) * KPER, min(H, (i - 7) * KPER))):
                            for part in range(3):
                                m = mm(P[:, bank, j * LK:(j + 1) * LK], selk[:, h, part, :], kp[:, part, :],
                                       start=part == 0, stop=part == 2)
                    m.then_inc(*ring_full.up())
                pe.wait_ge(*ring_done.at(b, NSEL))
                pe.wait_ge(*v_ready.at(b, 2))
                for u in range(8):
                    kt, qt = divmod(u, QT)
                    if u:
                        pe.wait_ge(*sub_done.at(b, u))
                    for h in range(H):
                        m = mm(P[0:KT, h // 4, (h % 4) * 128:(h % 4) * 128 + 128], ks[:, h, kt * KT:(kt + 1) * KT],
                               qs[:, h // 2, qt * 128:(qt + 1) * 128], start=True, stop=True)
                    m.then_inc(*st_full.up())
                pe.wait_ge(*p_ready.at(b, 8))
                for g in range(4):
                    for kt in range(2):
                        for j in range(4):
                            h = 4 * g + j
                            m = mm(P[32 * j:32 * j + 32, 4 + g, :], va[:, kt, 32 * h:32 * h + 32], pall[:, kt, h, :],
                                   start=kt == 0, stop=kt == 1)
                    m.then_inc(*o_full.up())
                pe.wait_ge(*sub_done.at(b, 8))
                for g in range(4):
                    pe.wait_ge(*on_ready.at(b, g + 1))
                    m = mm(P[:, 0, :], wo[:, g, :], on[:, g, :], start=g == 0, stop=g == 3)
                m.then_inc(*out_full.up())

        @block.scalar
        def _(act):
            nc.scalar.copy(G["scr"][:, 0:1], G["eps"][:, 0:1]).then_inc(ring_done.sem, 4)
            with nc.scalar.Fori(0, NB) as b:
                for i in range(NSEL):
                    act.wait_ge(*ring_full.at(b, i + 1))
                    if i < 8:
                        m = nc.scalar.copy(qs[:, i, :], P[:, 4 + i % 4, :])
                    else:
                        h0, n = (i - 8) * KPER, min(H, (i - 7) * KPER) - (i - 8) * KPER
                        m = nc.scalar.copy(ks[:, h0:h0 + n, :], P[:, 4 + i % 4, 0:n * LK].rearrange("p (h k) -> p h k", k=LK))
                    m.then_inc(*ring_done.up())
                for u in range(8):
                    act.wait_ge(*sub_done.at(b, u + 1))
                    nc.scalar.activation(ex[:, u % 2, :, :], ex[:, u % 2, :, :], ACT.Exp).then_inc(*exp_done.up())
                for g in range(4):
                    act.wait_ge(*o_full.at(b, g + 1))
                    nc.scalar.copy(on[:, g, :], P[:, 4 + g, :]).then_inc(*on_ready.up())

        @block.vector
        def _(dve):
            dve.wait_ge(*ld.at(0, 16 * len(loads)))
            nc.vector.memset(mx[:, 0:1], 0.0).then_inc(x_done.sem, 1)
            dve.wait_ge(x_done.sem, 1)
            scores = P[0:KT, 0:4, :].rearrange("p b (j q) -> p (b j) q", q=128)

            def total(b, u):
                dve.wait_ge(*exp_done.at(b, u + 1))
                dve.wait_ge(*p_ready.free(b, u + 1))
                link(dve, nc.vector.tensor_reduce(sm[:, u % 2, :], ex[:, u % 2, :, :].rearrange("p h q -> p q h"), AX.X, ALU.add), step, b)
                nc.vector.reciprocal(sm[:, u % 2, :], sm[:, u % 2, :]).then_inc(*sum_ready.up())

            with nc.vector.Fori(0, NB) as b:
                dve.wait_ge(*q_full.at(b, 1))
                cut(nc, dve, b, step, P[:, 0, :], G["zero"][:, 0:1], 8.0 ** -0.5, qf[:], qr[:], qp, parts_ready)
                dve.wait_ge(*k_full.at(b, 1))
                cut(nc, dve, b, step, P[:, 1, 0:LK], G["zero"][:, 0:1], 1.0, kf[:], kr[:], kp, parts_ready)
                for kt in range(2):
                    dve.wait_ge(*v_full.at(b, kt + 1))
                    nc.vector.tensor_copy(va[:, kt, :], P[0:KT, 2 + kt, :]).then_inc(*v_ready.up())
                for u in range(8):
                    dve.wait_ge(*st_full.at(b, u + 1))
                    link(dve, nc.vector.tensor_reduce(mx[:], scores.rearrange("p h q -> p q h"), AX.X, ALU.max), step, b)
                    dve.wait_ge(*p_ready.free(b, u + 1))
                    nc.vector.tensor_tensor(ex[:, u % 2, :, :], scores, mx[:].unsqueeze(1).to_broadcast([KT, H, 128]),
                                            ALU.subtract).then_inc(*sub_done.up())
                    if u:
                        total(b, u - 1)
                    dve.wait_ge(*sub_done.at(b, u + 1))
                total(b, 7)
                dve.wait_ge(*out_full.at(b, 1))
                x = seq(G["X"], b)
                nc.vector.tensor_tensor(x, x, P[:, 0, :], ALU.add).then_inc(*x_done.up())
    ph.done()


def phase_output(nc, G, D):
    ph = Phase(nc, "out")
    P, sb = G["P"], ph.sb
    ROUND = 1.5 * 2.0 ** 23
    ld = ph.count("ld")
    rhs, rt, rs, ri, rqT, rq = (sb("rhs", [128, C]), sb("rt", [128, C]), sb("rs", [128, 1]), sb("ri", [128, 1]),
                                sb("rqT", [128, C], BF16), sb("rq", [128, C], BF16))
    diag, rsb = sb("diag", [128, 128]), sb("rsb", [128, 128])
    zb, xb = sb("zb", [128, T]), sb("xb", [128, T])
    amax, sc, inv = sb("amax", [128, QT]), sb("sc", [128, QT]), sb("inv", [128, QT])
    qz, qb, qt_ = sb("qz", [128, QT, 128]), sb("qb", [128, QT, 128], BF16), sb("qt", [128, T], BF16)
    o = sb("o", [128, NB * QT, C])
    pre, pre_pe, pstep = ph.count("pre"), ph.count("pre_pe"), ph.count("pstep")
    step = ph.count("step", 7)
    b_ready, z_full, q_ready, qt_full, qt_done = (ph.count(n, k, a) for n, k, a in (
        ("b_ready", 2, 0), ("z_full", 1, 0), ("q_ready", 1, 0), ("qt_full", 1, 0), ("qt_done", 1, 0)))
    y_full, o_ready, stored = ph.count("y_full", 1, 1), ph.count("o_ready", 1), ph.count("stored", 16)
    loads = [(rhs[:], D["L3f_rhs"])]
    qview = P[:, 1, 0:256].bitcast(BF16)
    wide = [128, QT, 128]
    with nc.Block() as block:
        @block.sync
        def _(sp):
            load_all(sp, ld, loads)
            with nc.sync.Fori(0, NB) as b:
                sp.wait_ge(*o_ready.at(b, 1))
                sp.dma_start(D["out"][:, bass.ds(b * QT, QT), :], o[:, bass.ds(b * QT, QT), :]).then_inc(*stored.up(16))
            sp.wait_ge(stored.sem, 16 * NB)

        @block.gpsimd
        def _(pool):
            with nc.gpsimd.Fori(0, NB) as b:
                pool.wait_ge(*y_full.free(b, 1))
                nc.gpsimd.tensor_copy(zb[:], seq(G["Z"], b)).then_inc(*b_ready.up())
                nc.gpsimd.tensor_copy(xb[:], seq(G["X"], b)).then_inc(*b_ready.up())

        @block.tensor
        def _(pe):
            mm = nc.tensor.matmul
            pe.wait_ge(*ld.at(0, 16 * len(loads)))
            nc.tensor.transpose(P[:, 0, 0:128], rhs[:], G["ident"][:]).then_inc(*pre_pe.up())
            pe.wait_ge(*pre.at(0, 1))
            nc.tensor.transpose(qview[:, 0:128], rqT[:], G["identb"][:])
            mm(P[:, 2, 0:128], G["mean"][:], diag[:], start=True, stop=True).then_inc(*pre_pe.up())
            mm(P[0:32, 7, 0:32], G["identb"][0:32, 0:32], G["identb"][0:32, 0:32], start=True, stop=True).then_inc(y_full.sem, 1)
            pe.wait_ge(*pre.at(0, 2))
            with nc.tensor.Fori(0, NB) as b:
                pe.wait_ge(*b_ready.at(b, 1))
                for t in range(QT):
                    m = nc.tensor.transpose(P[:, 0, t * 128:(t + 1) * 128], zb[:, t * 128:(t + 1) * 128], G["ident"][:])
                m.then_inc(*z_full.up())
                pe.wait_ge(*q_ready.at(b, 1))
                for t in range(QT):
                    m = nc.tensor.transpose(qview[:, t * 128:(t + 1) * 128], qb[:, t, :], G["identb"][:])
                m.then_inc(*qt_full.up())
                pe.wait_ge(*qt_done.at(b, 1))
                pe.wait_ge(*b_ready.at(b, 2))
                for t in range(QT):
                    mm(P[:, 2, t * 128:(t + 1) * 128], qt_[:, t * 128:(t + 1) * 128], rq[:], start=True, stop=True)
                for t in range(QT):
                    m = nc.tensor.transpose(P[:, 3, t * 128:(t + 1) * 128], xb[:, t * 128:(t + 1) * 128], G["ident"][:])
                m.then_inc(*y_full.up())

        @block.scalar
        def _(act):
            with nc.scalar.Fori(0, NB) as b:
                act.wait_ge(*qt_full.at(b, 1))
                nc.scalar.copy(qt_[:], qview).then_inc(*qt_done.up())

        @block.vector
        def _(dve):
            def plink(ins):
                link(dve, ins, pstep)
            dve.wait_ge(*pre_pe.at(0, 1))
            plink(nc.vector.tensor_reduce(rs[:], P[:, 0, 0:128], AX.X, ALU.max, apply_absolute_value=True))
            plink(nc.vector.tensor_scalar(rs[:], rs[:], 1e-12, 1.0 / 127.0, ALU.max, ALU.mult))
            plink(nc.vector.reciprocal(ri[:], rs[:]))
            plink(nc.vector.tensor_scalar(rt[:], P[:, 0, 0:128], ri[:, 0:1], None, ALU.mult))
            plink(nc.vector.tensor_scalar(rt[:], rt[:], ROUND, ROUND, ALU.add, ALU.subtract))
            plink(nc.vector.tensor_scalar(diag[:], G["ident"][:], rs[:, 0:1], 128.0, ALU.mult, ALU.mult))
            nc.vector.tensor_scalar(rqT[:], rt[:], 127.0, -127.0, ALU.min, ALU.max).then_inc(*pre.up())
            dve.wait_ge(*pre_pe.at(0, 2))
            plink(nc.vector.tensor_copy(rq[:], qview[:, 0:128]))
            nc.vector.tensor_copy(rsb[:], P[:, 2, 0:128]).then_inc(*pre.up())
            dve.wait_ge(*pre.at(0, 2))
            with nc.vector.Fori(0, NB) as b:
                dve.wait_ge(*z_full.at(b, 1))
                zt = P[:, 0, :].rearrange("p (t c) -> p t c", c=128)
                link(dve, nc.vector.tensor_reduce(amax[:], zt, AX.X, ALU.max, apply_absolute_value=True), step, b)
                link(dve, nc.vector.tensor_scalar(sc[:], amax[:], 1e-12, 1.0 / 127.0, ALU.max, ALU.mult), step, b)
                link(dve, nc.vector.reciprocal(inv[:], sc[:]), step, b)
                link(dve, nc.vector.tensor_tensor(qz[:], zt, inv[:].unsqueeze(2).to_broadcast(wide), ALU.mult), step, b)
                link(dve, nc.vector.tensor_scalar(qz[:], qz[:], ROUND, ROUND, ALU.add, ALU.subtract), step, b)
                nc.vector.tensor_scalar(qb[:], qz[:], 127.0, -127.0, ALU.min, ALU.max).then_inc(*q_ready.up())
                dve.wait_ge(*y_full.at(b, 1))
                y = P[:, 2, :].rearrange("p (t c) -> p t c", c=128)
                link(dve, nc.vector.tensor_tensor(qz[:], y, sc[:].unsqueeze(2).to_broadcast(wide), ALU.mult), step, b)
                link(dve, nc.vector.tensor_tensor(qz[:], qz[:], rsb[:].unsqueeze(1).to_broadcast(wide), ALU.mult), step, b)
                nc.vector.tensor_tensor(o[:, bass.ds(b * QT, QT), :], qz[:], P[:, 3, :].rearrange("p (t c) -> p t c", c=128),
                                        ALU.add).then_inc(*o_ready.up())
    ph.done()


def phase_output_plain(nc, G, D):
    ph = Phase(nc, "out")
    P = G["P"]
    xt = ph.sb("xt", [128, NB * QT, C])
    up, moved, st = ph.count("up"), ph.count("moved"), ph.count("st")
    with nc.Block() as block:
        @block.tensor
        def _(pe):
            for b in range(NB):
                for t in range(QT):
                    m = nc.tensor.transpose(P[:, b, t * 128:(t + 1) * 128], G["X"][:, b, t * 128:(t + 1) * 128], G["ident"][:])
                m.then_inc(*up.up())

        @block.vector
        def _(dve):
            for b in range(NB):
                dve.wait_ge(*up.at(0, b + 1))
                nc.vector.tensor_copy(xt[:, b * QT:(b + 1) * QT, :], P[:, b, :].rearrange("p (t c) -> p t c", c=C)).then_inc(*moved.up())

        @block.sync
        def _(sp):
            for b in range(NB):
                sp.wait_ge(*moved.at(0, b + 1))
                sp.dma_start(D["out"][:, b * QT:(b + 1) * QT, :], xt[:, b * QT:(b + 1) * QT, :]).then_inc(*st.up(16))
            sp.wait_ge(*st.at(0, 16 * NB))
    ph.done()


def build(nc, D):
    ctx = ExitStack()
    with ctx:
        def sb(name, shape, dt=F32):
            return ctx.enter_context(nc.sbuf_tensor(name, shape, dt))
        G = {"X": sb("X", [128, NB, T]), "Y": sb("Y", [128, NB, T]), "Z": sb("Z", [128, NB, T]),
             "CT": sb("CT", [128, NB, LK]), "ident": sb("ident", [128, 128]), "identb": sb("identb", [128, 128], BF16),
             "mean": sb("mean", [128, 128]), "eps": sb("eps", [128, 2]), "zero": sb("zero", [128, 1]), "scr": sb("scr", [128, 2]),
             "P": ctx.enter_context(nc.psum_tensor("P", [128, 8, 512], F32))}
        phase_input(nc, G, D)
        X, Y, Z = G["X"], G["Y"], G["Z"]
        if "L0x" in PHASES:
            phase_norm(nc, G, "n0x", X, Y)
            phase_latent(nc, G, D, "L0x")
        if "L0f" in PHASES:
            phase_norm(nc, G, "n0f", X, Y)
            phase_norm(nc, G, "n0a", Y, Z, gain=D["L0_ln1_w"], bias=D["L0_ln1_b"])
            phase_conv_attention(nc, G, D)
            phase_norm(nc, G, "n0m", Y, Z, gain=D["L0_ln2_w"], bias=D["L0_ln2_b"])
            phase_experts(nc, G, D, "L0m")
        if "L1x" in PHASES:
            phase_norm(nc, G, "n1x", X, Y)
            phase_cross(nc, G, D, "L1x")
        if "L1f" in PHASES:
            phase_norm(nc, G, "n1f", X, Y)
            phase_tree(nc, G, D)
        if "L2x" in PHASES:
            phase_norm(nc, G, "n2x", X, Y)
            phase_cross(nc, G, D, "L2x")
        if "L2f" in PHASES:
            phase_norm(nc, G, "n2f", X, Y)
            phase_norm(nc, G, "n2a", Y, Z, center=False, gain=D["L2_w_ln1"])
            phase_latent(nc, G, D, "L2f")
            phase_norm(nc, G, "n2m", Y, Z, center=False, gain=D["L2_w_ln2"])
            phase_experts(nc, G, D, "L2m")
        if "L3x" in PHASES:
            phase_norm(nc, G, "n3x", X, Y)
            phase_over_heads(nc, G, D)
        if "L3f" in PHASES:
            phase_norm(nc, G, "n3f", X, Z)
            phase_output(nc, G, D)
        else:
            phase_output_plain(nc, G, D)


def lay_out(i):
    f32, bf = np.float32, mybir.dt.np(BF16)
    d = {}
    tok = lambda a: np.ascontiguousarray(a.reshape(-1, 128, a.shape[-1]).transpose(1, 0, 2))
    col = lambda a: np.ascontiguousarray(a.reshape(-1, 1))
    d["x"] = tok(i["x"])
    d["ctx"] = np.ascontiguousarray(i["ctx_1024"].reshape(NB * 2, KT, C).transpose(1, 0, 2))
    d["ident"] = np.eye(128, dtype=f32)
    d["identb"] = np.eye(128).astype(bf)
    d["mean"] = np.full((128, 128), 1 / 128, f32)
    d["eps"] = np.full((128, 2), EPS, f32)

    qpart, kpart = (0, 0, 1, 0, 2, 1), (0, 1, 0, 2, 0, 1)
    selq, selk = np.zeros((128, 8, 3, 128), f32), np.zeros((128, H, 3, 128), f32)
    selm = np.zeros((128, H, 128), f32)
    seld = {first: np.zeros((128, 4), f32) for first in (0, 8, 16)}
    selr = np.zeros((128, 4, 4, 32), f32)
    for h in range(H):
        for c in range(6):
            for e in range(8):
                row = 64 * (h % 2) + 8 * c + e
                selq[8 * h + e, h // 2, qpart[c], row] = 1
                selk[8 * h + e, h, kpart[c], row] = 1
        for p in range(3):
            selm[16 * p + h, h, :] = 1
            selr[16 * p + h, h // 4, h % 4, :] = 1
    for j in range(4):
        for first in seld:
            seld[first][32 * j + first, j] = 1
    d["selq"], d["selk"], d["selm"] = selq.astype(bf), selk.astype(bf), selm.astype(bf)
    d["selr"] = selr.reshape(128, 4, 128).astype(bf)
    d["seld0"], d["seld8"], d["seld16"] = seld[0], seld[8], seld[16]

    def spread_cols(w):
        n, e = w.shape[0], w.shape[1] // H
        out = np.zeros((n, H, 32), w.dtype)
        out[:, :, :e] = w.reshape(n, H, e)
        return out.reshape(n, H * 32)

    def spread_rows(w):
        return np.ascontiguousarray(spread_cols(w.T).T.reshape(4, 128, C).transpose(1, 0, 2))

    def values_bias(b):
        out = spread_cols(b.reshape(1, -1)).reshape(H, 32)
        out[:, 8] = 1
        return np.ascontiguousarray(np.broadcast_to(out.reshape(1, -1), (KT, 512)))

    def block_diagonal(w):
        out = np.zeros((H, 8, H, 8), w.dtype)
        for h in range(H):
            out[h, :, h, :] = w[h]
        return out.reshape(C, C)

    p = "L1_xattn_"
    d["L1x_wq"], d["L1x_wk"] = (np.ascontiguousarray(i[p + w].T) for w in ("w_q", "w_k"))
    d["L1x_wv"], d["L1x_wo"] = spread_cols(i[p + "w_v"].T), spread_rows(np.ascontiguousarray(i[p + "w_o"].T))
    d["L1x_bq"], d["L1x_bk"], d["L1x_bo"] = (col(i[p + b]) for b in ("b_q", "b_k", "b_o"))
    d["L1x_bv"] = values_bias(i[p + "b_v"])

    d["zero"] = np.zeros((128, 1), f32)
    k, q = np.arange(128)[:, None], np.arange(128)[None, :]
    d["mask_k"] = np.where(k > q, -BIG, 0).astype(f32).astype(bf)
    d["mask_q"] = np.ascontiguousarray(d["mask_k"].T)

    def rope(n, half, base, pos_exp):
        inv = (1.0 / np.float32(base) ** pos_exp.astype(f32)).astype(f32)
        ang = (np.arange(n, dtype=f32)[None, :] * inv[:, None]).astype(f32)
        return np.cos(ang).astype(f32), np.sin(ang).astype(f32)

    cos, sin = rope(T, 4, 10000.0, np.arange(0, 8, 2) / 8)
    cos8, sin8 = np.tile(cos, (32, 1)), np.tile(np.concatenate([-sin, sin]), (16, 1))
    s8 = f32(8.0) ** f32(-0.5)
    d["L0f_cq"], d["L0f_sq"], d["L0f_ck"], d["L0f_sk"] = cos8 * s8, sin8 * s8, cos8, sin8
    p = "L0_ffn_"
    d["L0f_conv"] = np.ascontiguousarray(i[p + "conv_w"][:, 0, :])
    wq, wk, wv = np.split(i[p + "attn_w"], 3, axis=1)
    swap = np.arange(C).reshape(16, 2, 4)[:, ::-1].reshape(-1)
    d["L0f_wq"], d["L0f_wqr"], d["L0f_wk"], d["L0f_wkr"] = wq, wq[:, swap], wk, wk[:, swap]
    d["L0f_wv"], d["L0f_wo"] = spread_cols(wv), spread_rows(i[p + "proj_w"])
    d["L0f_bv"] = np.ascontiguousarray(np.broadcast_to(values_bias(np.zeros(C, f32))[0:1], (128, 512)))
    for n in ("ln1_w", "ln1_b", "ln2_w", "ln2_b"):
        d["L0_" + n] = col(i[p + n])

    def padded(a, shape, at=(0, 0)):
        out = np.zeros(shape, a.dtype)
        out[tuple(slice(o, o + n) for o, n in zip(at, a.shape))] = a
        return out

    p = "L0_xattn_"
    wa, wb = np.zeros((128, H, 128), f32), np.zeros((128, 8, 128), f32)
    qr = i[p + "w_q_rope"].reshape(48, H, 64)
    wa[:48, :, :64] = qr
    wb[:48] = qr.reshape(48, H, 2, 32)[:, :, ::-1].reshape(48, 8, 128)
    d["L0x_wa"], d["L0x_wb"] = wa, wb
    d["L0x_wqd"] = padded(i[p + "w_q_down"], (128, 128))
    d["L0x_wqT"] = i[p + "w_q_up"].reshape(48, H, 64).transpose(2, 1, 0)
    d["L0x_wkT"] = i[p + "w_k_up"].reshape(32, H, 64).transpose(2, 1, 0)
    d["L0x_wvT"] = i[p + "w_v_up"].reshape(32, H, 64).transpose(2, 1, 0)
    d["L0x_woh"] = i[p + "w_out"].reshape(H, 64, C).transpose(1, 0, 2)
    wka = padded(i[p + "w_k_rope"], (128, 128))
    wka[:32, 64:96] = np.eye(32)
    d["L0x_wka"] = wka
    d["L0x_wkb"] = padded(i[p + "w_k_rope"].reshape(32, 2, 32)[:, ::-1].reshape(32, 64), (128, 128))
    d["L0x_wlat"] = padded(i[p + "w_kv_comp"], (128, 128))
    cos, sin = rope(T, 32, 10000.0, np.arange(32) / 32)
    s128 = f32(1.0) / np.sqrt(128).astype(f32)
    rc, rs = np.tile(cos, (2, 1)), np.concatenate([-sin, sin])
    one = np.ones((32, T), f32)
    d["L0x_cq"] = padded(np.concatenate([rc, one]) * s128, (128, T))
    d["L0x_sq"] = np.tile(rs, (2, 1)) * s128
    d["L0x_ck"] = padded(np.concatenate([rc, one])[:, :LK], (128, LK))
    d["L0x_sk"] = padded(rs[:, :LK], (128, LK))
    seg = i["itok_BxS_0_511"]
    d["segc"] = np.ascontiguousarray(seg.reshape(NB * QT, 128).T)
    d["segr"] = np.ascontiguousarray(np.broadcast_to(seg[None], (KT, NB, T)))
    d["keyrow"] = np.ascontiguousarray(np.broadcast_to(np.arange(1, LK + 1, dtype=f32), (128, LK)))
    d["keycol"] = np.ascontiguousarray(np.arange(1, LK + 1, dtype=f32).reshape(2, KT).T)

    p = "L2_ffn_"
    wq = i[p + "Wq"].reshape(C, H, 64)
    flip = np.arange(32).reshape(16, 2)[:, ::-1].reshape(-1)
    wa = np.zeros((128, H, 128), f32)
    wa[:, :, :32] = wq[:, :, 32:]
    d["L2f_wa"], d["L2f_wb"] = wa, wq[:, :, 32:][:, :, flip].reshape(C, 4, 128)
    d["L2f_wqT"] = wq[:, :, :32].transpose(2, 1, 0)
    kvb = i[p + "Wkvb"].reshape(16, H, 32).transpose(2, 1, 0)
    d["L2f_wkT"] = kvb
    d["L2f_wvT"] = padded(kvb, (32, H, 32), (0, 0, 0))
    d["L2f_woh"] = i[p + "Wo"].reshape(H, 64, C)[:, :32].transpose(1, 0, 2)
    kva = i[p + "Wkva"]
    d["L2f_wka"] = padded(np.concatenate([kva[:, 16:], kva[:, :16]], 1), (128, 128))
    d["L2f_wkb"] = padded(kva[:, 16:][:, flip], (128, 128))
    d["L2f_wlat"] = kva[:, :16]
    cos, sin = rope(T, 16, 100000.0, np.arange(0, 32, 2) / 32)
    rc = np.repeat(cos, 2, axis=0)
    rs = np.stack([-sin, sin], 1).reshape(32, T)
    one = np.ones((16, T), f32)
    d["L2f_cq"] = padded(np.concatenate([rc, one]) * f32(0.125), (128, T))
    d["L2f_sq"] = np.tile(rs, (4, 1)) * f32(0.125)
    d["L2f_ck"] = padded(np.concatenate([rc, one]), (128, T))
    d["L2f_sk"] = padded(rs, (128, T))
    d["L2_w_ln1"], d["L2_w_ln2"] = col(i[p + "w_ln1"]), col(i[p + "w_ln2"])

    p = "L2_xattn_"
    d["L2x_wq"], d["L2x_wk"] = (block_diagonal(i[p + w]) for w in ("Wq", "Wk"))
    d["L2x_wv"], d["L2x_wo"] = spread_cols(block_diagonal(i[p + "Wv"])), spread_rows(i[p + "Wo"])
    d["L2x_bq"], d["L2x_bk"], d["L2x_bo"] = (col(i[p + b]) for b in ("bq", "bk", "bo"))
    d["L2x_bv"] = values_bias(i[p + "bv"].reshape(-1))

    p = "L0_ffn_"
    d["L0m_router"] = i[p + "router_w"]
    d["L0m_w1"] = i[p + "expert_wv"].transpose(1, 0, 2)
    d["L0m_w2"] = i[p + "expert_proj"].reshape(4, 4, 128, C).transpose(2, 0, 1, 3)
    p = "L2_ffn_"
    d["L2m_router"] = i[p + "Wgate"]
    w1, w2 = np.zeros((128, 5, 2, 2, 64), f32), np.zeros((2, 64, 5, C), f32)
    for e in range(8):
        w1[:, e // 2, 0, e % 2], w1[:, e // 2, 1, e % 2] = i[p + "Wg"][e], i[p + "Wu"][e]
        w2[e % 2, :, e // 2] = i[p + "Wd"][e]
    w1[:, 4, 0, 0], w1[:, 4, 1, 0], w2[0, :, 4] = i[p + "sWg"][0], i[p + "sWu"][0], i[p + "sWd"][0]
    d["L2m_w1"], d["L2m_w2"] = w1.reshape(128, 5, 2, 128), w2.reshape(128, 5, C)
    d["L2m_ebias"] = np.broadcast_to(i[p + "expert_bias"], (128, QT, 8))
    for n, e in (("L0m", 4), ("L2m", 8)):
        d[n + "_prio"] = np.broadcast_to(np.arange(e, 0, -1, dtype=f32), (128, QT, e))
        d[n + "_sel"] = np.repeat(np.eye(e, dtype=f32), 128 if e == 4 else 64, axis=1).reshape(e, 4, 128)

    p = "L1_ffn_"
    d["L1f_wq"], d["L1f_rt"], d["L1f_lvT"], d["L1f_woT"] = (
        i[p + "Wq"], i[p + "routers"].T, i[p + "leaf_values"].T, i[p + "Wout_w"].T)
    d["L1f_bias"] = col(i[p + "Wout_b"])
    p = "L3_xattn_"
    d["L3x_wq"], d["L3x_wk"] = i[p + "Wq"].T, i[p + "Wk"].T
    d["L3x_wv"], d["L3x_wo"] = spread_cols(i[p + "Wv"].T), spread_rows(i[p + "Wo"].T)
    d["L3f_rhs"] = i["L3_ffn_rhs"]
    return d


def kernel(**inputs):
    import concourse.bacc as bacc
    from concourse.bass_utils import run_bass_kernel_spmd

    nc = bacc.Bacc("TRN2", target_bir_lowering=False, num_devices=1)
    arrays = {"in_" + k: np.ascontiguousarray(v) for k, v in lay_out({k: np.asarray(v) for k, v in inputs.items()}).items()}
    D = {k[3:]: nc.dram_tensor(k, a.shape, mybir.dt.from_np(a.dtype), kind="ExternalInput").ap() for k, a in arrays.items()}
    D["out"] = nc.dram_tensor("out_0", (128, NB * QT, C), F32, kind="ExternalOutput").ap()
    build(nc, D)
    r = run_bass_kernel_spmd(nc, [arrays], core_ids=[0])
    return np.ascontiguousarray(r.results[0]["out_0"].transpose(1, 0, 2)).reshape(NB, T, C)
```

```python
from contextlib import ExitStack

import concourse.bass as bass
import numpy as np
from concourse import mybir

F32 = mybir.dt.float32
BF16 = mybir.dt.bfloat16
I32 = mybir.dt.int32
ALU = mybir.AluOpType
ACT = mybir.ActivationFunctionType
AX = mybir.AxisListType

NB, T, C = 4, 512, 128
H = 16
LK, KT = 154, 77
QT = T // 128
EPS = 1e-5
BIG = 1e30



class Count:

    def __init__(self, nc, name, per=0, ahead=0):
        self.name, self.per, self.ahead, self.n = name, per, ahead, 0
        self.sem = nc.alloc_semaphore(name)

    def up(self, n=1):
        self.n += n
        return self.sem, n

    def free(self, b, k):
        if isinstance(b, tuple):
            known = b[1] * self.per + k
            assert known > 0 or isinstance(b[0], int), (self.name, "a wait against zero")
            return self.sem, b[0] * self.per + known
        assert k > 0, (self.name, "a wait against zero")
        return self.sem, b * self.per + k

    def at(self, b, k):
        return self.free(b, k + self.ahead)

    def before(self, eng, b):
        if not (isinstance(b[0], int) and b[0] + b[1] == 0):
            eng.wait_ge(*self.at(b, 0))

    def one_before(self, eng, b):
        if not (isinstance(b[0], int) and b[0] + b[1] == 0):
            eng.wait_ge(*self.free(b, 0))

    def check(self):
        assert self.n in (self.per, 2 * self.per), (self.name, "signals", self.n, "declared", self.per)


class Phase:

    def __init__(self, nc, name):
        self.nc, self.name, self.ctx, self.counts = nc, name, ExitStack(), []

    def sb(self, name, shape, dt=F32):
        return self.ctx.enter_context(self.nc.sbuf_tensor(f"{self.name}_{name}", shape, dt))

    def count(self, name, per=0, ahead=0):
        c = Count(self.nc, f"{self.name}_{name}", per, ahead)
        self.counts.append(c)
        return c

    def done(self):
        for c in self.counts:
            if c.per:
                c.check()
        self.ctx.close()
        self.nc.clear_and_free_semaphores([c.sem for c in self.counts])
        self.nc.all_engine_barrier()


def link(eng, ins, step, b=0):
    ins.then_inc(*step.up())
    eng.wait_ge(*step.at(b, (step.n - 1) % step.per + 1 if step.per else step.n))


def seq(buf, b):
    n = b[0] + b[1] if isinstance(b, tuple) else b
    part = buf[:, n:n + 1, :] if isinstance(n, int) else buf[:, bass.ds(n, 1), :]
    return part.rearrange("p a t -> p (a t)")


def load_all(sp, ld, pairs):
    for dst, src in pairs:
        sp.dma_start(dst, src).then_inc(*ld.up(16))


def phase_input(nc, G, D):
    ph = Phase(nc, "in")
    P = G["P"]
    xt = ph.sb("xt", [128, NB * QT, C])
    ct = ph.sb("ct", [KT, NB * 2, C])
    ld = ph.count("ld")
    x_up = ph.count("x_up")
    c_up = ph.count("c_up")
    x_moved, c_moved = ph.count("x_moved"), ph.count("c_moved")
    loads = [(xt[:], D["x"]), (ct[:], D["ctx"]), (G["ident"][:], D["ident"]), (G["identb"][:], D["identb"]),
             (G["mean"][:], D["mean"]), (G["zero"][:], D["zero"]), (G["eps"][:], D["eps"])]
    with nc.Block() as block:
        @block.sync
        def _(sp):
            load_all(sp, ld, loads)

        @block.tensor
        def _(pe):
            pe.wait_ge(*ld.at(0, 16 * len(loads)))
            for b in range(NB):
                for t in range(QT):
                    m = nc.tensor.transpose(P[:, b, t * 128:(t + 1) * 128], xt[:, b * QT + t, :], G["ident"][:])
                m.then_inc(*x_up.up())
            for i in range(NB * 2):
                m = nc.tensor.transpose(P[:, 4 + i // 6, (i % 6) * KT:(i % 6) * KT + KT], ct[:, i, :],
                                        G["ident"][0:KT, 0:KT])
            m.then_inc(*c_up.up())

        @block.vector
        def _(dve):
            for b in range(NB):
                dve.wait_ge(*x_up.at(0, b + 1))
                nc.vector.tensor_copy(G["X"][:, b, :], P[:, b, :]).then_inc(*x_moved.up())
            dve.wait_ge(*x_moved.at(0, NB))

        @block.scalar
        def _(act):
            act.wait_ge(*c_up.at(0, 1))
            nc.scalar.copy(G["CT"][:, 0:3, :], P[:, 4, 0:3 * LK].rearrange("p (b k) -> p b k", k=LK)).then_inc(*c_moved.up())
            nc.scalar.copy(G["CT"][:, 3, :], P[:, 5, 0:LK]).then_inc(*c_moved.up())
            act.wait_ge(*c_moved.at(0, 2))
    ph.done()


def phase_norm(nc, G, name, src, dst, center=True, gain=None, bias=None, fetch=None):
    ph = Phase(nc, name)
    P = G["P"]
    xc = dst if center else src
    sq = rs = ph.sb("sq", [128, NB, T])
    step, ld = ph.count("step"), ph.count("ld")
    given = [v for v in (gain, bias) if v is not None]
    cols = [ph.sb(f"col{n}", [128, 1]) for n in range(len(given))]
    gain, bias = ([c[:, 0:1] for c in cols] + [None, None])[:2]
    mean_up, cent, squared, squared_by_dve, var_up, ln, rstd, out = (
        ph.count(n) for n in ("mean_up", "cent", "squared", "squared_by_dve", "var_up", "ln", "rstd", "out"))
    with nc.Block() as block:
        @block.sync
        def _(sp):
            load_all(sp, ld, [(c[:], v) for c, v in zip(cols, given)])
            if fetch:
                load_all(sp, *fetch)

        @block.tensor
        def _(pe):
            if center:
                for b in range(NB):
                    nc.tensor.matmul(P[:, b, :], G["mean"][:], src[:, b, :], start=True, stop=True).then_inc(*mean_up.up())
            for b in range(NB):
                pe.wait_ge(*(squared_by_dve if b % 2 else squared).at(0, b // 2 + 1))
                nc.tensor.matmul(P[:, 4 + b, :], G["mean"][:], sq[:, b, :], start=True, stop=True).then_inc(*var_up.up())

        @block.vector
        def _(dve):
            if center:
                for b in range(NB):
                    dve.wait_ge(*mean_up.at(0, b + 1))
                    nc.vector.tensor_tensor(xc[:, b, :], src[:, b, :], P[:, b, :], ALU.subtract).then_inc(*cent.up())
                    if b % 2:
                        dve.wait_ge(*cent.at(0, b + 1))
                        nc.vector.tensor_tensor(sq[:, b, :], xc[:, b, :], xc[:, b, :], ALU.mult).then_inc(*squared_by_dve.up())
            else:
                for b in range(1, NB, 2):
                    nc.vector.tensor_tensor(sq[:, b, :], xc[:, b, :], xc[:, b, :], ALU.mult).then_inc(*squared_by_dve.up())
            if given:
                dve.wait_ge(*ld.at(0, 16 * len(given)))
            for b in range(NB):
                dve.wait_ge(*rstd.at(0, b + 1))
                if center:
                    dve.wait_ge(*cent.at(0, b + 1))
                if gain is None:
                    nc.vector.tensor_tensor(dst[:, b, :], xc[:, b, :], rs[:, b, :], ALU.mult).then_inc(*out.up())
                elif bias is None:
                    nc.vector.scalar_tensor_tensor(out=dst[:, b, :], in0=xc[:, b, :], scalar=gain, in1=rs[:, b, :],
                                                   op0=ALU.mult, op1=ALU.mult).then_inc(*out.up())
                else:
                    link(dve, nc.vector.scalar_tensor_tensor(out=dst[:, b, :], in0=xc[:, b, :], scalar=gain,
                                                             in1=rs[:, b, :], op0=ALU.mult, op1=ALU.mult), step)
                    nc.vector.tensor_scalar(dst[:, b, :], dst[:, b, :], bias, None, ALU.add).then_inc(*out.up())
            dve.wait_ge(*out.at(0, NB))

        @block.gpsimd
        def _(pool):
            for b in range(0, NB, 2):
                if center:
                    pool.wait_ge(*cent.at(0, b + 1))
                nc.gpsimd.tensor_tensor(sq[:, b, :], xc[:, b, :], xc[:, b, :], ALU.mult).then_inc(*squared.up())

        @block.scalar
        def _(act):
            for b in range(NB):
                act.wait_ge(*var_up.at(0, b + 1))
                nc.scalar.activation(rs[:, b, :], P[:, 4 + b, :], ACT.Ln, bias=G["eps"][:, 0:1]).then_inc(*ln.up())
            for b in range(NB):
                act.wait_ge(*ln.at(0, b + 1))
                nc.scalar.activation(rs[:, b, :], rs[:, b, :], ACT.Exp, scale=-0.5).then_inc(*rstd.up())
    ph.done()


def groups_of(causal):
    out = []
    for g in range(4):
        units = []
        for h in range(4 * g, 4 * g + 4):
            if not causal:
                units += [[(h, kt, 0, T, 0)] for kt in range(2)]
                continue
            units.append([(h, 0, 0, 512, 0)])
            units.append([(h, 1, 128, 384, 0), (h, 3, 384, 128, 384)])
            if h % 2:
                units.append([(h - 1, 2, 256, 256, 0), (h, 2, 256, 256, 256)])
        out.append(units)
    return out


def spread_between(main, extra):
    out, done = [], 0
    for n, step in enumerate(main):
        out.append(step)
        upto = len(extra) * (n + 1) // len(main)
        out += extra[done:upto]
        done = upto
    return out


EARLY = 1


class Attention:

    RING = 3

    def __init__(self, ph, G, causal, prep, late):
        self.ph, self.G, self.nc, self.causal = ph, G, ph.nc, causal
        self.nk = 128 if causal else KT
        self.nkt = 4 if causal else 2
        self.keys = T if causal else LK
        self.groups = groups_of(causal)
        self.per_group = len(self.groups[0])
        self.kper = 1 if causal else 3
        self.kbanks = -(-H // self.kper)
        self.nsel = 8 + self.kbanks
        self.ns = QT * self.kbanks
        c = ph.count
        self.ring_full = c("ring_full", self.nsel + 4 * self.per_group)
        self.ring_done = c("ring_done", self.nsel + 4 * self.per_group, self.RING)
        self.s_full, self.s_free = c("s_full", self.ns), c("s_free", self.ns, 2)
        self.parts_ready = c("parts_ready", 2)
        self.nm_ready, self.mt_full, self.nmt_ready = c("nm_ready", 1), c("mt_full", 1), c("nmt_ready", 1)
        self.o_full, self.o_free = c("o_full", 4, 2), c("o_free", 4, 1)
        self.den_full, self.rp_ready = c("den_full", 1), c("rp_ready", 1)
        self.rt_full, self.rt_ready = c("rt_full", 1), c("rt_ready", 1)
        self.bc_full, self.on_ready = c("bc_full", 4), c("on_ready", 4)
        self.rec_step = c("rec_step", 4)
        self.out_full, self.out_taken = c("out_full", 1), c("out_taken", 1, 1)
        sb = ph.sb
        self.qp, self.kp = sb("qp", [128, 3, T], BF16), sb("kp", [128, 3, self.keys], BF16)
        self.qs, self.ks = sb("qs", [128, 8, T], BF16), sb("ks", [128, H, self.keys], BF16)
        self.selq, self.selk = sb("selq", [128, 8, 3, 128], BF16), sb("selk", [128, H, 3, 128], BF16)
        self.selm = sb("selm", [128, H, 128], BF16)
        self.prob = sb("prob", [128, 2 * self.per_group, T])
        self.nm, self.nmr = sb("nm", [128, QT, H]), sb("nmr", [128, QT, H])
        self.nmp = sb("nmp", [128, QT, 128], BF16)
        self.nmt = sb("nmt", [128, T], BF16)
        self.osp, self.on = sb("osp", [128, 4, T]), sb("on", [128, 4, T])
        self.rec, self.recr = sb("rec", [128, QT, H]), sb("recr", [128, QT, H])
        self.rp, self.rt_sb = sb("rp", [128, QT, 128], BF16), sb("rt_sb", [128, T], BF16)
        self.seld, self.selr = sb("seld", [128, 4]), sb("selr", [128, 4, 128], BF16)
        self.wo = sb("wo", [128, 4, C])
        self.mt = G["P"][:, 5, 0:256].bitcast(BF16)
        self.den = G["P"][:, 7, 0:QT * H].rearrange("p (t h) -> p t h", h=H)
        self.rt = G["P"][:, 7, 256:512].bitcast(BF16)

        nxt = [[], [], [], []]
        ready = [[] for _ in range(self.kbanks)]
        for pair in range(8):
            ready[2 * pair // self.kper].append(("sel", pair))
        for k in range(self.kbanks):
            ready[k].append(("sel", 8 + k))
        nxt[0] += ready[0]
        gate = lambda k: (min(H, (k + 1) * self.kper) - 1) // 4
        for k in range(self.kbanks):
            if k + 1 < self.kbanks:
                nxt[gate(k + 1)] += ready[k + 1]
            nxt[gate(min(k + 1, self.kbanks - 1))] += [("first", (k, qt)) for qt in range(QT)]
        nxt = [[(kind, 1, n) for kind, n in steps] for steps in nxt]
        second = [[("second", 1 if g == 0 or g == 1 and u < EARLY else 0, (g, u)) for u in range(self.per_group)]
                  for g in range(4)]
        values = [[("values", 0, n)] for n in range(4)]
        self.order = []
        for i, unit in enumerate(second[1][EARLY:]):
            if i % 3 == 0:
                self.order += [(kind, 1, n) for kind, n in prep[i // 3:i // 3 + 1]]
            self.order.append(unit)
        self.order += spread_between(values[0] + second[2], nxt[0] + nxt[1])
        self.order += spread_between(values[1] + second[3] + values[2], nxt[2])
        half = len(nxt[3]) // 2
        self.order += nxt[3][:half] + values[3] + nxt[3][half:-2] + [("den", 0, 0)] + nxt[3][-2:]
        back = [("rt", 0, 0)] + [("bc", 0, g) for g in range(4)]
        late = [(kind, 1, n) for kind, n in late]
        mixed = spread_between(back, late)
        self.order += [("mt", 1, 0)] + spread_between(second[0], mixed) + second[1][:EARLY] + [("out", 0, 0)]
        self.ring_ahead = self.nsel + self.per_group + EARLY
        self.use_of_step = {}
        uses = 0
        for kind, off, n in self.order:
            if kind == "first":
                uses += 1
                self.use_of_step[n] = uses
        self.order_ahead = [s for s in self.order if s[1] == 1]
        self.order_behind = [s for s in self.order if s[1] == 0]

    def run(self, engine, one_step):
        def part(order, t, turn):
            self.unit, self.turn, self.first_use, self.last_unit = 0, turn, {}, {}
            for kind, off, n in order:
                one_step((t, off), kind, n)
        part(self.order_ahead, -1, None)
        with engine.Fori(0, NB - 1) as t:
            part(self.order, t, t)
        part(self.order_behind, NB - 1, NB - 1)

    def ring(self, count, unit, free=False):
        k = unit + (0 if free else count.ahead)
        return count.sem, k if self.turn is None else self.turn * count.per + (self.ring_ahead + k)

    def loads(self, D):
        return [(t[:], D[n]) for t, n in ((self.selq, "selq"), (self.selk, "selk"), (self.selm, "selm"),
                                          (self.selr, "selr"), (self.seld, "seld"))]

    def dve_ahead(self, dve):
        self.nc.vector.memset(self.nmp[:], 0.0).then_inc(self.s_free.sem, self.s_free.ahead)
        self.nc.vector.memset(self.nmr[:], 0.0).then_inc(self.o_free.sem, self.o_free.ahead)
        self.nc.vector.memset(self.rp[:], 0.0).then_inc(self.out_taken.sem, self.out_taken.ahead)
        dve.wait_ge(self.s_free.sem, self.s_free.ahead)
        dve.wait_ge(self.o_free.sem, self.o_free.ahead)
        dve.wait_ge(self.out_taken.sem, self.out_taken.ahead)

    def pe_ahead(self, sem, n):
        one = self.G["identb"][0:32, 0:32]
        self.nc.tensor.matmul(self.G["P"][0:32, 7, 0:32], one, one, start=True, stop=True).then_inc(sem, n)

    def act_ahead(self, scratch):
        self.nc.scalar.copy(scratch, self.G["eps"][:, 0:1]).then_inc(self.ring_done.sem, self.ring_done.ahead)

    def q(self, h, q0, n):
        return self.qs[:, h // 2, q0:q0 + n]

    def ring_bank(self, pe):
        pe.wait_ge(*self.ring(self.ring_done, max(self.unit + 1, self.RING), free=True))
        bank = 2 + self.unit % self.RING
        self.unit += 1
        return bank

    def first_bank(self, pe, b, n):
        use = self.use_of_step[n]
        pe.wait_ge(*self.s_free.free(b, use))
        return (use - 1) % 2

    def pe(self, pe, b, kind, n):
        nc, G, P = self.nc, self.G, self.G["P"]
        mm = nc.tensor.matmul
        if kind == "sel":
            if n == 0:
                pe.wait_ge(*self.parts_ready.at(b, 2))
            bank = self.ring_bank(pe)
            if n < 8:
                for part in range(3):
                    m = mm(P[:, bank, :], self.selq[:, n, part, :], self.qp[:, part, :], start=part == 0, stop=part == 2)
            else:
                for j, h in enumerate(range((n - 8) * self.kper, min(H, (n - 7) * self.kper))):
                    for part in range(3):
                        m = mm(P[:, bank, j * self.keys:(j + 1) * self.keys], self.selk[:, h, part, :],
                               self.kp[:, part, :], start=part == 0, stop=part == 2)
                self.first_use[n - 8] = self.unit
            m.then_inc(*self.ring_full.up())
        elif kind == "first":
            k, qt = n
            heads = range(k * self.kper, min(H, (k + 1) * self.kper))
            if qt == 0:
                pe.wait_ge(*self.ring(self.ring_done, self.first_use[k]))
            bank = self.first_bank(pe, b, n)
            w = (qt + 1) * 128 if self.causal else LK
            for j, h in enumerate(heads):
                m = mm(P[:, bank, j * w:(j + 1) * w], self.q(h, qt * 128, 128), self.ks[:, h, 0:w],
                       start=True, stop=not self.causal)
            if self.causal:
                m = mm(P[:, bank, w - 128:w], G["identb"][:], self.mask_q[:], start=False, stop=True)
            m.then_inc(*self.s_full.up())
        elif kind == "mt":
            self.out_taken.one_before(pe, b)
            pe.wait_ge(*self.nm_ready.at(b, 1))
            for qt in range(QT):
                m = nc.tensor.transpose(self.mt[:, qt * 128:(qt + 1) * 128], self.nmp[:, qt, :], G["identb"][:])
            m.then_inc(*self.mt_full.up())
        elif kind == "second":
            g, u = n
            if g == 0 and u == 0:
                pe.wait_ge(*self.nmt_ready.at(b, 1))
            bank = self.ring_bank(pe)
            for h, kt, q0, w, col in self.groups[g][u]:
                out = P[0:self.nk, bank, col:col + w]
                at = slice(kt * self.nk, (kt + 1) * self.nk)
                mm(out, self.ks[:, h, at], self.q(h, q0, w), start=True, stop=False)
                if self.causal:
                    mm(out[:, 0:128], G["identb"][:], self.mask_k[:], start=False, stop=False)
                m = mm(out, self.selm[:, h, 0:self.nk], self.nmt[:, q0:q0 + w], start=False, stop=True)
            m.then_inc(*self.ring_full.up())
            self.last_unit[g] = self.unit
        elif kind == "values":
            if n == 0:
                self.wait_values(pe, b)
            pe.wait_ge(*self.ring(self.ring_done, self.last_unit[n] if n else 0))
            pe.wait_ge(*self.o_free.free(b, n + 1))
            where = {}
            for u, tiles in enumerate(self.groups[n]):
                for h, kt, q0, w, col in tiles:
                    where[h, kt] = ((n % 2) * self.per_group + u, q0, w, col)
            for kt in range(self.nkt):
                for j in range(4):
                    slot, q0, w, col = where[4 * n + j, kt]
                    m = mm(P[32 * j:32 * j + 32, 6, q0:q0 + w], self.v(kt, 4 * n + j),
                           self.prob[0:self.nk, slot, col:col + w], start=kt == 0, stop=kt == self.nkt - 1)
            m.then_inc(*self.o_full.up())
        elif kind == "den":
            pe.wait_ge(*self.o_free.at(b, 4))
            for qt in range(QT):
                for g in range(4):
                    m = mm(self.den[:, qt, 4 * g:4 * g + 4], self.osp[:, g, qt * 128:(qt + 1) * 128], self.seld[:],
                           start=True, stop=True)
            m.then_inc(*self.den_full.up())
        elif kind == "rt":
            pe.wait_ge(*self.rp_ready.at(b, 1))
            for qt in range(QT):
                m = nc.tensor.transpose(self.rt[:, qt * 128:(qt + 1) * 128], self.rp[:, qt, :], G["identb"][:])
            m.then_inc(*self.rt_full.up())
        elif kind == "bc":
            pe.wait_ge(*(self.on_ready.at(b, n) if n else self.rt_ready.at(b, 1)))
            mm(P[:, 7, :], self.selr[:, n, :], self.rt_sb[:], start=True, stop=True).then_inc(*self.bc_full.up())
        elif kind == "out":
            pe.wait_ge(*self.on_ready.at(b, 4))
            for g in range(4):
                m = mm(P[:, 5, :], self.wo[:, g, :], self.on[:, g, :], start=g == 0, stop=g == 3)
            m.then_inc(*self.out_full.up())

    def act(self, act, b, kind, n):
        nc, P = self.nc, self.G["P"]
        bank = 2 + self.unit % self.RING
        if kind == "sel":
            self.unit += 1
            act.wait_ge(*self.ring(self.ring_full, self.unit))
            if n < 8:
                m = nc.scalar.copy(self.qs[:, n, :], P[:, bank, :])
            else:
                h0 = (n - 8) * self.kper
                w = min(H, h0 + self.kper) - h0
                m = nc.scalar.copy(self.ks[:, h0:h0 + w, :],
                                   P[:, bank, 0:w * self.keys].rearrange("p (h k) -> p h k", k=self.keys))
            m.then_inc(*self.ring_done.up())
        elif kind == "second":
            g, u = n
            if u == 0:
                act.wait_ge(*self.o_full.free(b, g + 1))
            self.unit += 1
            act.wait_ge(*self.ring(self.ring_full, self.unit))
            nc.scalar.activation(self.prob[0:self.nk, (g % 2) * self.per_group + u, :], P[0:self.nk, bank, :],
                                 ACT.Exp).then_inc(*self.ring_done.up())


    def dve(self, dve, b, kind, n, resid, bias):
        nc, P, step = self.nc, self.G["P"], self.step
        if kind == "first":
            k, qt = n
            w = (qt + 1) * 128 if self.causal else LK
            h0, h1 = k * self.kper, min(H, (k + 1) * self.kper)
            use = self.use_of_step[n]
            dve.wait_ge(*self.s_full.at(b, use))
            nc.vector.tensor_reduce(self.nm[:, qt, h0:h1], P[:, (use - 1) % 2, 0:(h1 - h0) * w].rearrange("p (h k) -> p h k", k=w),
                                    AX.X, ALU.max, negate=True).then_inc(*self.s_free.up())
            if n == (self.kbanks - 1, QT - 1):
                dve.wait_ge(*self.s_free.at(b, self.ns))
                part = [self.nmp[:, :, p * H:(p + 1) * H] for p in range(3)]
                link(dve, nc.vector.tensor_copy(part[0], self.nm[:]), step, b)
                link(dve, nc.vector.tensor_tensor(self.nmr[:], self.nm[:], part[0], ALU.subtract), step, b)
                link(dve, nc.vector.tensor_copy(part[1], self.nmr[:]), step, b)
                nc.vector.tensor_tensor(part[2], self.nmr[:], part[1], ALU.subtract).then_inc(*self.nm_ready.up())
        elif kind == "mt":
            dve.wait_ge(*self.mt_full.at(b, 1))
            nc.vector.tensor_copy(self.nmt[:], self.mt).then_inc(*self.nmt_ready.up())
        elif kind == "values":
            dve.wait_ge(*self.o_full.at(b, n + 1))
            nc.vector.tensor_copy(self.osp[:, n, :], P[:, 6, :]).then_inc(*self.o_free.up())
        elif kind == "den":
            dve.wait_ge(*self.den_full.at(b, 1))
            link(dve, nc.vector.reciprocal(self.rec[:], self.den), self.rec_step, b)
            part = [self.rp[:, :, p * H:(p + 1) * H] for p in range(3)]
            link(dve, nc.vector.tensor_copy(part[0], self.rec[:]), self.rec_step, b)
            link(dve, nc.vector.tensor_tensor(self.recr[:], self.rec[:], part[0], ALU.subtract), self.rec_step, b)
            link(dve, nc.vector.tensor_copy(part[1], self.recr[:]), self.rec_step, b)
            nc.vector.tensor_tensor(part[2], self.recr[:], part[1], ALU.subtract).then_inc(*self.rp_ready.up())
        elif kind == "rt":
            dve.wait_ge(*self.rt_full.at(b, 1))
            nc.vector.tensor_copy(self.rt_sb[:], self.rt).then_inc(*self.rt_ready.up())
        elif kind == "bc":
            if n == 0:
                dve.wait_ge(*self.o_free.at(b, 4))
            dve.wait_ge(*self.bc_full.at(b, n + 1))
            nc.vector.tensor_tensor(self.on[:, n, :], self.osp[:, n, :], P[:, 7, :], ALU.mult).then_inc(*self.on_ready.up())
        elif kind == "out":
            dve.wait_ge(*self.out_full.at(b, 1))
            at = seq(resid, b)
            nc.vector.scalar_tensor_tensor(out=at, in0=P[:, 5, :], scalar=bias, in1=at,
                                           op0=ALU.add, op1=ALU.add).then_inc(*self.out_taken.up())


def cut(nc, dve, b, step, ps, bias, scale, full, rest, parts, ready):
    if ps is not None:
        link(dve, nc.vector.tensor_scalar(full, ps, bias, scale, ALU.add, ALU.mult), step, b)
    link(dve, nc.vector.tensor_copy(parts[:, 0, :], full), step, b)
    link(dve, nc.vector.tensor_tensor(rest, full, parts[:, 0, :], ALU.subtract), step, b)
    link(dve, nc.vector.tensor_copy(parts[:, 1, :], rest), step, b)
    nc.vector.tensor_tensor(parts[:, 2, :], rest, parts[:, 1, :], ALU.subtract).then_inc(*ready.up())


def phase_cross(nc, G, D, name, norm):
    ph = Phase(nc, name)
    P, sb = G["P"], ph.sb
    A = Attention(ph, G, causal=False, prep=[("q", 0), ("k", 0)], late=[("v", 0), ("v", 1)])
    A.step = step = ph.count("step", 11)
    ld = ph.count("ld")
    wq, wk, wv = sb("wq", [128, C]), sb("wk", [128, C]), sb("wv", [128, 512])
    bqt, bkt, bot, bvt = sb("bq", [128, 1]), sb("bk", [128, 1]), sb("bo", [128, 1]), sb("bv", [KT, 512])
    ctb = sb("ctb", [128, LK])
    qf, qr, kf, kr = sb("qf", [128, T]), sb("qr", [128, T]), sb("kf", [128, LK]), sb("kr", [128, LK])
    va = sb("va", [KT, 2, 512])
    A.v = lambda kt, h: va[:, kt, 32 * h:32 * h + 32]
    ctb_ready, q_full, k_full = (ph.count(n, 1) for n in ("ctb_ready", "q_full", "k_full"))
    v_full, v_ready = ph.count("v_full", 2, 1), ph.count("v_ready", 2)
    A.wait_values = lambda pe, b: pe.wait_ge(*v_ready.at(b, 2))
    loads = [(wq[:], D[name + "_wq"]), (wk[:], D[name + "_wk"]), (wv[:], D[name + "_wv"]), (A.wo[:], D[name + "_wo"]),
             (bqt[:], D[name + "_bq"]), (bkt[:], D[name + "_bk"]), (bot[:], D[name + "_bo"]), (bvt[:], D[name + "_bv"]),
             ] + A.loads(D)
    norm((ld, loads))
    with nc.Block() as block:
        @block.gpsimd
        def _(pool):
            with nc.gpsimd.Fori(0, NB) as b:
                pool.wait_ge(*v_full.free(b, 1))
                nc.gpsimd.tensor_copy(ctb[:], seq(G["CT"], b)).then_inc(*ctb_ready.up())

        @block.tensor
        def _(pe):
            mm = nc.tensor.matmul
            pe.wait_ge(*ld.at((0, 0), 16 * len(loads)))
            A.pe_ahead(A.o_full.sem, 2)
            A.pe_ahead(v_full.sem, 1)

            def one_step(b, kind, n):
                if kind == "q":
                    v_ready.before(pe, b)
                    mm(P[:, 0, :], wq[:], seq(G["Y"], b), start=True, stop=True).then_inc(*q_full.up())
                elif kind == "k":
                    pe.wait_ge(*ctb_ready.at(b, 1))
                    mm(P[:, 1, 0:LK], wk[:], ctb[:], start=True, stop=True).then_inc(*k_full.up())
                elif kind == "v":
                    mm(P[0:KT, n, :], ctb[:, n * KT:(n + 1) * KT], wv[:], start=True, stop=True).then_inc(*v_full.up())
                else:
                    A.pe(pe, b, kind, n)

            A.run(nc.tensor, one_step)

        @block.scalar
        def _(act):
            A.act_ahead(G["scr"][:, 0:1])

            def one_step(b, kind, n):
                A.act(act, b, kind, n)

            A.run(nc.scalar, one_step)

        @block.vector
        def _(dve):
            dve.wait_ge(*ld.at((0, 0), 16 * len(loads)))
            A.dve_ahead(dve)

            def one_step(b, kind, n):
                if kind == "q":
                    dve.wait_ge(*q_full.at(b, 1))
                    cut(nc, dve, b, step, P[:, 0, :], bqt[:, 0:1], 8.0 ** -0.5, qf[:], qr[:], A.qp, A.parts_ready)
                elif kind == "k":
                    dve.wait_ge(*k_full.at(b, 1))
                    cut(nc, dve, b, step, P[:, 1, 0:LK], bkt[:, 0:1], 1.0, kf[:], kr[:], A.kp, A.parts_ready)
                elif kind == "v":
                    dve.wait_ge(*v_full.at(b, n + 1))
                    nc.vector.tensor_tensor(va[:, n, :], P[0:KT, n, :], bvt[:], ALU.add).then_inc(*v_ready.up())
                else:
                    A.dve(dve, b, kind, n, G["X"], bot[:, 0:1])

            A.run(nc.vector, one_step)
    ph.done()


def phase_conv_attention(nc, G, D, norm):
    name = "L0f"
    ph = Phase(nc, name)
    P, sb = G["P"], ph.sb
    A = Attention(ph, G, causal=True, prep=[("conv", 0), ("q", 0), ("k", 0)],
                  late=[("v", n) for n in range(4)])
    A.step = step = ph.count("step", 15)
    ld = ph.count("ld")
    conv = sb("conv", [128, 3])
    wq, wqr, wk, wkr, wv = (sb(n, [128, w]) for n, w in (("wq", C), ("wqr", C), ("wk", C), ("wkr", C), ("wv", 512)))
    bvt = sb("bv", [128, 512])
    cq, sq, ck, sk = (sb(n, [128, T]) for n in ("cq", "sq", "ck", "sk"))
    A.mask_q, A.mask_k = sb("mask_q", [128, 128], BF16), sb("mask_k", [128, 128], BF16)
    hb, full, rest = sb("hb", [128, T]), sb("full", [128, T]), sb("rest", [128, T])
    va = sb("va", [128, 4, 512])
    A.v = lambda kt, h: va[:, kt, 32 * h:32 * h + 32]
    h_ready, q_full, k_full = ph.count("h_ready", 1), ph.count("q_full", 1), ph.count("k_full", 1)
    v_full, v_ready = ph.count("v_full", 4, 1), ph.count("v_ready", 4)
    loads = [(conv[:], D["L0f_conv"]), (wq[:], D["L0f_wq"]), (wqr[:], D["L0f_wqr"]), (wk[:], D["L0f_wk"]),
             (wkr[:], D["L0f_wkr"]), (wv[:], D["L0f_wv"]), (bvt[:], D["L0f_bv"]), (A.wo[:], D["L0f_wo"]),
             (cq[:], D["L0f_cq"]), (sq[:], D["L0f_sq"]), (ck[:], D["L0f_ck"]), (sk[:], D["L0f_sk"]),
             (A.mask_q[:], D["mask_q"]), (A.mask_k[:], D["mask_k"])] + A.loads(D)
    A.wait_values = lambda pe, b: pe.wait_ge(*v_ready.at(b, 4))
    norm((ld, loads))
    with nc.Block() as block:
        @block.tensor
        def _(pe):
            mm = nc.tensor.matmul
            pe.wait_ge(*ld.at((0, 0), 16 * len(loads)))
            A.pe_ahead(A.o_full.sem, 2)
            A.pe_ahead(v_full.sem, 1)

            def one_step(b, kind, n):
                if kind == "q":
                    pe.wait_ge(*h_ready.at(b, 1))
                    v_ready.before(pe, b)
                    mm(P[:, 0, :], wq[:], hb[:], start=True, stop=True)
                    mm(P[:, 1, :], wqr[:], hb[:], start=True, stop=True).then_inc(*q_full.up())
                elif kind == "k":
                    pe.wait_ge(*A.parts_ready.at(b, 1))
                    mm(P[:, 0, :], wk[:], hb[:], start=True, stop=True)
                    mm(P[:, 1, :], wkr[:], hb[:], start=True, stop=True).then_inc(*k_full.up())
                elif kind == "v":
                    if n >= 2:
                        pe.wait_ge(*v_ready.at(b, n - 1))
                    mm(P[:, n % 2, :], hb[:, n * 128:(n + 1) * 128], wv[:], start=True, stop=True).then_inc(*v_full.up())
                elif kind != "conv":
                    A.pe(pe, b, kind, n)

            A.run(nc.tensor, one_step)

        @block.scalar
        def _(act):
            A.act_ahead(G["scr"][:, 0:1])

            def one_step(b, kind, n):
                A.act(act, b, kind, n)

            A.run(nc.scalar, one_step)

        @block.vector
        def _(dve):
            dve.wait_ge(*ld.at((0, 0), 16 * len(loads)))
            A.dve_ahead(dve)

            def one_step(b, kind, n):
                if kind == "conv":
                    z = seq(G["Z"], b)
                    dve.wait_ge(*v_full.free(b, 1))
                    link(dve, nc.vector.tensor_scalar(hb[:], z, conv[:, 2:3], None, ALU.mult), step, b)
                    link(dve, nc.vector.scalar_tensor_tensor(out=hb[:, 1:T], in0=z[:, 0:T - 1], scalar=conv[:, 1:2],
                                                             in1=hb[:, 1:T], op0=ALU.mult, op1=ALU.add), step, b)
                    nc.vector.scalar_tensor_tensor(out=hb[:, 2:T], in0=z[:, 0:T - 2], scalar=conv[:, 0:1],
                                                   in1=hb[:, 2:T], op0=ALU.mult, op1=ALU.add).then_inc(*h_ready.up())
                elif kind in "qk":
                    ready, cos, sin, parts = (q_full, cq, sq, A.qp) if kind == "q" else (k_full, ck, sk, A.kp)
                    dve.wait_ge(*ready.at(b, 1))
                    if kind == "k":
                        dve.wait_ge(*A.parts_ready.at(b, 1))
                    nc.vector.tensor_tensor(full[:], P[:, 0, :], cos[:], ALU.mult)
                    link(dve, nc.vector.tensor_tensor(rest[:], P[:, 1, :], sin[:], ALU.mult), step, b)
                    link(dve, nc.vector.tensor_tensor(full[:], full[:], rest[:], ALU.add), step, b)
                    cut(nc, dve, b, step, None, None, None, full[:], rest[:], parts, A.parts_ready)
                elif kind == "v":
                    dve.wait_ge(*v_full.at(b, n + 1))
                    nc.vector.tensor_tensor(va[:, n, :], P[:, n % 2, :], bvt[:], ALU.add).then_inc(*v_ready.up())
                else:
                    A.dve(dve, b, kind, n, G["Y"], G["zero"][:, 0:1])

            A.run(nc.vector, one_step)
    ph.done()


def phase_latent(nc, G, D, name, norm):
    window = name == "L0x"
    ph = Phase(nc, name)
    P, sb, mm = G["P"], ph.sb, nc.tensor.matmul
    rot, lat, up_dim = (64, 32, 64) if window else (32, 16, 32)
    per_b = 128 // rot
    keys, nk, nkt = (LK, KT, 2) if window else (T, 128, 4)
    per_k = 3 if window else 1
    KB = -(-H // per_k)
    groups = groups_of(not window)
    UNITS = len(groups[0])
    EB = 2 if window else 4
    nq = 48 if window else 128
    heads_of = lambda k: range(k * per_k, min(H, (k + 1) * per_k))
    width = lambda qt: LK if window else (qt + 1) * 128

    wa, wb = sb("wa", [128, H, 128]), sb("wb", [128, H // per_b, 128])
    wka, wkb, wlat, wo = sb("wka", [128, 128]), sb("wkb", [128, 128]), sb("wlat", [128, 128 if window else lat]), sb("wo", [128, 4, C])
    cq, sq, ck, sk = sb("cq", [128, T]), sb("sq", [128, T]), sb("ck", [128, keys]), sb("sk", [128, keys])
    src = sb("src", [128, keys])
    kf, kt_, tmp = sb("kf", [128, NB, keys]), sb("kt", [128, keys]), sb("tmp", [rot, 2, T])
    va, qe = sb("va", [nk, nkt, 32]), sb("qe", [128, H, T])
    ex = sb("ex", [128, EB, QT, per_k * keys])
    prob = sb("prob", [128, 2 * UNITS, T])
    nm, den = sb("nm", [128, QT, H]), sb("den", [128, QT, H])
    rec, recr = sb("rec", [128, QT, H]), sb("recr", [128, QT, H])
    rp, rt_sb = sb("rp", [128, QT, 128], BF16), sb("rt_sb", [128, T], BF16)
    selr = sb("selr", [128, 4, 128], BF16)
    osp, on = sb("osp", [128, 4, T]), sb("on", [128, 4, T])
    rt = P[:, 7, 0:256].bitcast(BF16)
    wqT = prob[0:up_dim, 0:4, :].rearrange("p s (h n) -> p (s h) n", n=128)[:, :, 0:nq]
    woh = prob[0:up_dim, 4:8, :].rearrange("p s (h n) -> p (s h) n", n=128)
    wkT = prob[0:up_dim, 8, 0:H * lat].rearrange("p (h n) -> p h n", n=lat)
    wvT = prob[0:up_dim, 9, :].rearrange("p (h n) -> p h n", n=32)
    loads = [(t, D[f"{name}_{n}"]) for t, n in ((wqT, "wqT"), (wkT, "wkT"), (wvT, "wvT"), (woh, "woh"), (wa[:], "wa"),
             (wb[:], "wb"), (wka[:], "wka"), (wkb[:], "wkb"), (wlat[:], "wlat"), (cq[:], "cq"), (sq[:], "sq"),
             (ck[:], "ck"), (sk[:], "sk"))] + [(selr[:], D["selr"])]
    c = ph.count
    if window:
        wqd, qc, kvc = sb("wqd", [128, 128]), sb("qc", [128, T]), sb("kvc", [128, LK])
        segc_i, segc, keyrow = sb("segc_i", [128, NB * QT], I32), sb("segc", [128, NB, QT]), sb("keyrow", [128, LK])
        mask, dq = sb("mask", [128, NB, QT, LK], BF16), sb("dq", [128, QT, LK])
        qc_full, kvc_full, qc_ready, kvc_ready = (c(n, 1) for n in ("qc_full", "kvc_full", "qc_ready", "kvc_ready"))
        masks_ready = c("masks_ready")
        loads += [(wqd[:], D["L0x_wqd"]), (segc_i[:], D["segc"]), (keyrow[:], D["keyrow"])]
    else:
        mask = sb("mask", [128, 128], BF16)
        loads += [(mask[:], D["mask_q"])]
    ld, pre_full, pre_done, ahead_step, ahead_done = (c(n) for n in ("ld", "pre_full", "pre_done", "ahead_step", "ahead_done"))
    src_ready, k_full, k_ready, v_ready = (c(n, 1) for n in ("src_ready", "k_full", "k_ready", "v_ready"))
    v_full = c("v_full", 1, 1)
    a_full, a_free, b_full = c("a_full", H), c("a_free", H, 1), c("b_full", H // per_b)
    t_ready, qe_ready = c("t_ready", H), c("qe_ready", H, 2)
    s_full, max_ready, s_free = c("s_full", KB * QT), c("max_ready", KB * QT), c("s_free", KB * QT, 2)
    t_full, t_free = c("t_full", 4 * UNITS), c("t_free", 4 * UNITS, 2)
    o_full, o_free = c("o_full", 4, 2), c("o_free", 4, 1)
    rp_ready, rt_full, rt_ready, out_full, out_taken = (c(n, 1, a) for n, a in (
        ("rp_ready", 0), ("rt_full", 0), ("rt_ready", 0), ("out_full", 0), ("out_taken", 1)))
    bc_full, on_ready, k_step, r_step = c("bc_full", 4), c("on_ready", 4), c("k_step", 1), c("r_step", 4)

    done_at = [max(h for h, *_ in tiles) // per_k for units in groups for tiles in units]
    assert done_at == sorted(done_at)
    slots = {}

    def put(slot, *steps):
        slots.setdefault(slot, []).append(list(steps))

    for k in range(KB):
        heads = [("head", h) for h in heads_of(k)]
        put(k - 1, *heads)
        put(k, *[("scores", (k, qt)) for qt in range(QT)])
        put(k + 1, *[("turn", u) for u in range(4 * UNITS) if done_at[u] == k])
    for g in range(4):
        put((4 * g + 3) // per_k + 2, ("values", g))
    put(KB, ("rp", 0))
    put(2, ("lat", 0))
    if window:
        put(-2, ("qc", 0), ("kvc", 0))
        put(-1, ("kk", 0))
    else:
        put(-1, ("kk", 0))
    put(KB + 1, ("rt", 0))
    put(KB + 2, *[("bc", g) for g in range(4)])
    put(KB + 2, ("out", 0))
    FIRST = 3
    before = ("rp", "kk")
    after = ("qc", "kvc", "rt", "lat", "out")
    order = []
    for at in range(FIRST, FIRST + KB):
        found = [[(kind, off, n) for kind, n in steps] for off in (0, 1) for steps in slots.get(at - off * KB, [])]
        assert all(s - FIRST < KB for s in slots)
        first = [s for steps in found for s in steps if s[0] in before]
        last = [s for steps in found for s in steps if s[0] in after]
        main = [s for steps in found for s in steps if s[0] == "scores"]
        rest = [s for kind in ("head", "values", "bc", "turn") for steps in found for s in steps if s[0] == kind]
        last.sort(key=lambda s: after.index(s[0]) if s[0] != "lat" else 9)
        first.sort(key=lambda s: before.index(s[0]))
        order += first + spread_between(main, rest) + last

    def run(engine, one_step):
        for kind, off, n in order:
            if off == 1:
                one_step((-1, 1), kind, n)
        with engine.Fori(0, NB - 1) as t:
            for kind, off, n in order:
                one_step((t, off), kind, n)
        for kind, off, n in order:
            if off == 0:
                one_step((NB - 1, 0), kind, n)

    norm((ld, loads))
    with nc.Block() as block:
        @block.gpsimd
        def _(pool):
            nc.gpsimd.memset(tmp[:], 0.0).then_inc(qe_ready.sem, 2)
            with nc.gpsimd.Fori(0, NB) as b:
                pool.wait_ge(*v_full.free(b, 1))
                nc.gpsimd.tensor_copy(src[:], seq(G["CT"] if window else G["Z"], b)).then_inc(*src_ready.up())
                for h in range(H):
                    pool.wait_ge(*t_ready.at(b, h + 1))
                    nc.gpsimd.tensor_tensor(qe[0:rot, h, :], qe[0:rot, h, :], tmp[:, h % 2, :], ALU.add)\
                        .then_inc(*qe_ready.up())

        @block.tensor
        def _(pe):
            pe.wait_ge(*ld.at(0, 16 * len(loads)))
            for h in range(H):
                mm(P[0:nq, 0, h * lat:(h + 1) * lat], wqT[:, h, :], wkT[:, h, :], start=True, stop=True)
            for h in range(H):
                m = mm(P[32 * (h % 4):32 * (h % 4) + 32, 1, (h // 4) * C:(h // 4 + 1) * C], wvT[:, h, :], woh[:, h, :],
                       start=True, stop=True)
            m.then_inc(*pre_full.up())
            one = G["identb"][0:32, 0:32]
            for sem, n in ((o_full.sem, 2), (v_full.sem, 1)):
                mm(P[0:32, 7, 0:32], one, one, start=True, stop=True).then_inc(sem, n)
            pe.wait_ge(*pre_done.at(0, 2))
            pe.wait_ge(*ahead_done.at(0, 1))

            def one_step(b, kind, n):
                q_in = qc[:] if window else seq(G["Z"], b)
                if kind == "qc":
                    t_ready.before(pe, b)
                    mm(P[:, 5, :], wqd[:], seq(G["Y"], b), start=True, stop=True).then_inc(*qc_full.up())
                elif kind == "kvc":
                    v_ready.before(pe, b)
                    out_taken.one_before(pe, b)
                    mm(P[:, 7, 0:LK], wlat[:], seq(G["CT"], b), start=True, stop=True).then_inc(*kvc_full.up())
                elif kind == "kk":
                    pe.wait_ge(*a_free.free(b, 1))
                    t_ready.before(pe, b)
                    if window:
                        pe.wait_ge(*qc_ready.at(b, 1))
                        pe.wait_ge(*kvc_ready.at(b, 1))
                    k_in = kvc[:] if window else seq(G["Z"], b)
                    mm(P[:, 0, 0:keys], wka[:], k_in, start=True, stop=True)
                    mm(P[:, 5, 0:keys], wkb[:], k_in, start=True, stop=True).then_inc(*k_full.up())
                elif kind == "lat":
                    pe.wait_ge(*src_ready.at(b, 1))
                    pe.wait_ge(*out_taken.free(b, 1))
                    for kt in range(nkt):
                        m = mm(P[0:nk, 7, 32 * kt:32 * kt + lat], src[:, kt * nk:(kt + 1) * nk], wlat[:, 0:lat],
                               start=True, stop=True)
                    m.then_inc(*v_full.up())
                elif kind == "head":
                    if n == 0:
                        pe.wait_ge(*k_ready.at(b, 1))
                    if n % per_b == 0:
                        if n:
                            pe.wait_ge(*t_ready.at(b, n))
                        mm(P[:, 5, :], wb[:, n // per_b, :], q_in, start=True, stop=True).then_inc(*b_full.up())
                    pe.wait_ge(*a_free.free(b, n + 1))
                    mm(P[:, 0, :], wa[:, n, :], q_in, start=True, stop=True).then_inc(*a_full.up())
                elif kind == "scores":
                    k, qt = n
                    heads, w = heads_of(k), width(qt)
                    if qt == 0:
                        pe.wait_ge(*qe_ready.at(b, heads[-1] + 1))
                    if window and n == (0, 0):
                        pe.wait_ge(*masks_ready.at(0, NB))
                    pe.wait_ge(*s_free.free(b, k * QT + qt + 1))
                    bank = 1 + qt % 2
                    if window:
                        part = (mask[:, b[0] + b[1], qt:qt + 1, :] if isinstance(b[0], int) else
                                mask[:, bass.ds(b[0] + b[1], 1), qt:qt + 1, :].rearrange("p a x y -> p (a x) y"))
                        mm(P[:, bank, 0:len(heads) * w].rearrange("p (h k) -> p h k", k=w), G["identb"][:],
                           part.to_broadcast([128, len(heads), w]), start=True, stop=False)
                    for j, h in enumerate(heads):
                        m = mm(P[:, bank, j * w:(j + 1) * w], qe[:, h, qt * 128:(qt + 1) * 128], seq(kf, b)[:, 0:w],
                               start=not window, stop=window and j == len(heads) - 1)
                    if not window:
                        m = mm(P[:, bank, w - 128:w], G["identb"][:], mask[:], start=False, stop=True)
                    m.then_inc(*s_full.up())
                elif kind == "turn":
                    g, u = divmod(n, UNITS)
                    pe.wait_ge(*s_free.at(b, (done_at[n] + 1) * QT))
                    pe.wait_ge(*t_free.free(b, n + 1))
                    for h, kt, q0, w, col in groups[g][u]:
                        for q in range(0, w, 128):
                            qt = (q0 + q) // 128
                            at = (h % per_k) * LK + kt * nk if window else kt * 128
                            m = nc.tensor.transpose(P[0:nk, 3 + n % 2, col + q:col + q + 128],
                                                    ex[:, (h // per_k) % EB, qt, at:at + nk], G["ident"][:])
                    m.then_inc(*t_full.up())
                elif kind == "values":
                    if n == 0:
                        pe.wait_ge(*v_ready.at(b, 1))
                    pe.wait_ge(*t_free.at(b, (n + 1) * UNITS))
                    pe.wait_ge(*o_free.free(b, n + 1))
                    where = {}
                    for u, tiles in enumerate(groups[n]):
                        for h, kt, q0, w, col in tiles:
                            where[h, kt] = ((n % 2) * UNITS + u, q0, w, col)
                    for kt in range(nkt):
                        for j in range(4):
                            slot, q0, w, col = where[4 * n + j, kt]
                            m = mm(P[32 * j:32 * j + 32, 6, q0:q0 + w], va[:, kt, :], prob[0:nk, slot, col:col + w],
                                   start=kt == 0, stop=kt == nkt - 1)
                    m.then_inc(*o_full.up())
                elif kind == "rt":
                    pe.wait_ge(*rp_ready.at(b, 1))
                    for qt in range(QT):
                        m = nc.tensor.transpose(rt[:, qt * 128:(qt + 1) * 128], rp[:, qt, :], G["identb"][:])
                    m.then_inc(*rt_full.up())
                elif kind == "bc":
                    pe.wait_ge(*(on_ready.at(b, n) if n else rt_ready.at(b, 1)))
                    mm(P[:, 7, :], selr[:, n, :], rt_sb[:], start=True, stop=True).then_inc(*bc_full.up())
                elif kind == "out":
                    pe.wait_ge(*on_ready.at(b, 4))
                    for g in range(4):
                        m = mm(P[:, 7, :], wo[:, g, :], on[:, g, :], start=g == 0, stop=g == 3)
                    m.then_inc(*out_full.up())

            run(nc.tensor, one_step)

        @block.scalar
        def _(act):
            act.wait_ge(*pre_full.at(0, 1))
            nc.scalar.copy(wa[0:nq, :, rot:rot + lat], P[0:nq, 0, 0:H * lat].rearrange("p (h r) -> p h r", r=lat))\
                .then_inc(*pre_done.up())
            nc.scalar.copy(wo[:], P[:, 1, :].rearrange("p (g c) -> p g c", c=C)).then_inc(*pre_done.up())
            act.wait_ge(*pre_done.at(0, 2))
            nc.scalar.copy(G["scr"][:, 0:1], G["eps"][:, 0:1]).then_inc(s_free.sem, 2)
            act.wait_ge(s_free.sem, 2)
            nc.scalar.copy(G["scr"][:, 0:1], G["eps"][:, 0:1]).then_inc(t_free.sem, 2)

            def one_step(b, kind, n):
                if kind == "qc":
                    act.wait_ge(*qc_full.at(b, 1))
                    nc.scalar.copy(qc[:], P[:, 5, :]).then_inc(*qc_ready.up())
                elif kind == "kvc":
                    act.wait_ge(*kvc_full.at(b, 1))
                    nc.scalar.copy(kvc[:], P[:, 7, 0:LK]).then_inc(*kvc_ready.up())
                elif kind == "lat":
                    act.wait_ge(*v_full.at(b, 1))
                    nc.scalar.copy(va[:, :, 0:lat], P[0:nk, 7, 0:32 * nkt].rearrange("p (k r) -> p k r", r=32)[:, :, 0:lat])\
                        .then_inc(*v_ready.up())
                elif kind == "scores":
                    k, qt = n
                    w = width(qt)
                    act.wait_ge(*max_ready.at(b, k * QT + qt + 1))
                    for j, h in enumerate(heads_of(k)):
                        m = nc.scalar.activation(ex[:, k % EB, qt, j * w:(j + 1) * w], P[:, 1 + qt % 2, j * w:(j + 1) * w],
                                                 ACT.Exp, bias=nm[:, qt, h:h + 1], accum_out=den[:, qt, h:h + 1])
                    m.then_inc(*s_free.up())
                elif kind == "turn":
                    g, u = divmod(n, UNITS)
                    act.wait_ge(*o_full.free(b, g + 1))
                    act.wait_ge(*t_full.at(b, n + 1))
                    nc.scalar.copy(prob[0:nk, (g % 2) * UNITS + u, :], P[0:nk, 3 + n % 2, :]).then_inc(*t_free.up())

            run(nc.scalar, one_step)

        @block.vector
        def _(dve):
            dve.wait_ge(*ld.at(0, 16 * len(loads)))
            nc.vector.memset(kt_[:, 0:1], 0.0).then_inc(a_free.sem, 1)
            nc.vector.memset(nm[:], 0.0).then_inc(o_free.sem, 1)
            nc.vector.memset(rp[:], 0.0).then_inc(out_taken.sem, 1)
            for count in (a_free, o_free, out_taken):
                dve.wait_ge(count.sem, 1)
            nc.vector.memset(va[:], 0.0).then_inc(*ahead_done.up())
            if window:
                link(dve, nc.vector.tensor_copy(segc[:].rearrange("p b t -> p (b t)"), segc_i[:]), ahead_step)
                for s in range(NB):
                    for qt in range(QT):
                        m = nc.vector.tensor_scalar(dq[:, qt, :], keyrow[:], segc[:, s, qt:qt + 1], None, ALU.subtract)
                    link(dve, m, ahead_step)
                    link(dve, nc.vector.tensor_tensor(dq[:], dq[:], dq[:], ALU.mult), ahead_step)
                    nc.vector.tensor_scalar(mask[:, s, :, :], dq[:], 1.5, -BIG, ALU.is_gt, ALU.mult).then_inc(*masks_ready.up())
                    dve.wait_ge(*masks_ready.at(0, s + 1))

            def one_step(b, kind, n):
                if kind == "kk":
                    dve.wait_ge(*k_full.at(b, 1))
                    k_b = seq(kf, b)
                    nc.vector.tensor_tensor(k_b, P[:, 0, 0:keys], ck[:], ALU.mult)
                    link(dve, nc.vector.tensor_tensor(kt_[:], P[:, 5, 0:keys], sk[:], ALU.mult), k_step, b)
                    nc.vector.tensor_tensor(k_b, k_b, kt_[:], ALU.add).then_inc(*k_ready.up())
                elif kind == "head":
                    if n % per_b == 0:
                        dve.wait_ge(*b_full.at(b, n // per_b + 1))
                    dve.wait_ge(*a_full.at(b, n + 1))
                    nc.vector.tensor_tensor(qe[:, n, :], P[:, 0, :], cq[:], ALU.mult).then_inc(*a_free.up())
                    dve.wait_ge(*qe_ready.free(b, n + 1))
                    j = n % per_b
                    nc.vector.tensor_tensor(tmp[:, n % 2, :], P[rot * j:rot * j + rot, 5, :],
                                            sq[rot * j:rot * j + rot, :], ALU.mult).then_inc(*t_ready.up())
                elif kind == "scores":
                    k, qt = n
                    w, heads = width(qt), heads_of(k)
                    dve.wait_ge(*s_full.at(b, k * QT + qt + 1))
                    nc.vector.tensor_reduce(nm[:, qt, heads[0]:heads[-1] + 1],
                                            P[:, 1 + qt % 2, 0:len(heads) * w].rearrange("p (h k) -> p h k", k=w),
                                            AX.X, ALU.max, negate=True).then_inc(*max_ready.up())
                elif kind == "values":
                    dve.wait_ge(*o_full.at(b, n + 1))
                    nc.vector.tensor_copy(osp[:, n, :], P[:, 6, :]).then_inc(*o_free.up())
                elif kind == "rp":
                    dve.wait_ge(*s_free.at(b, KB * QT))
                    link(dve, nc.vector.reciprocal(rec[:], den[:]), r_step, b)
                    part = [rp[:, :, p * H:(p + 1) * H] for p in range(3)]
                    link(dve, nc.vector.tensor_copy(part[0], rec[:]), r_step, b)
                    link(dve, nc.vector.tensor_tensor(recr[:], rec[:], part[0], ALU.subtract), r_step, b)
                    link(dve, nc.vector.tensor_copy(part[1], recr[:]), r_step, b)
                    nc.vector.tensor_tensor(part[2], recr[:], part[1], ALU.subtract).then_inc(*rp_ready.up())
                elif kind == "rt":
                    dve.wait_ge(*rt_full.at(b, 1))
                    nc.vector.tensor_copy(rt_sb[:], rt).then_inc(*rt_ready.up())
                elif kind == "bc":
                    if n == 0:
                        dve.wait_ge(*o_free.at(b, 4))
                    dve.wait_ge(*bc_full.at(b, n + 1))
                    nc.vector.tensor_tensor(on[:, n, :], osp[:, n, :], P[:, 7, :], ALU.mult).then_inc(*on_ready.up())
                elif kind == "out":
                    dve.wait_ge(*out_full.at(b, 1))
                    x = seq(G["X"] if window else G["Y"], b)
                    nc.vector.tensor_tensor(x, x, P[:, 7, :], ALU.add).then_inc(*out_taken.up())

            run(nc.vector, one_step)
    ph.done()


def one_hot_of_max(nc, dve, b, step, logits, mx, eq, prio, top, hot, E):
    wide = [128, NB * QT, E]
    link(dve, nc.vector.tensor_reduce(mx, logits, AX.X, ALU.max), step, b)
    link(dve, nc.vector.tensor_tensor(eq, logits, mx.unsqueeze(2).to_broadcast(wide), ALU.is_ge), step, b)
    link(dve, nc.vector.tensor_tensor(eq, eq, prio, ALU.mult), step, b)
    link(dve, nc.vector.tensor_reduce(top, eq, AX.X, ALU.max), step, b)
    return nc.vector.tensor_tensor(hot, eq, top.unsqueeze(2).to_broadcast(wide), ALU.is_equal)


def phase_experts(nc, G, D, name, norm):
    one = name == "L0m"
    ph = Phase(nc, name)
    P, sb = G["P"], ph.sb
    E = 4 if one else 8
    NM = 4
    NC = 4 if one else 5
    step, ahead_step = ph.count("step", NC + 1 + 2 * E - 1 if one else NC + NM + 1), ph.count("ahead_step")
    ld = ph.count("ld")
    TILES = NB * QT
    router, prio, sel = sb("router", [128, E]), sb("prio", [128, TILES, E]), sb("sel", [128, NM, 128], BF16)
    if one:
        w1, w2 = sb("w1", [128, E, 1024]), sb("w2", [128, E, 4, C])
        hm = sb("hm", [128, E, T])
    else:
        w1, w2 = sb("w1", [128, NC, 2, 128]), sb("w2", [128, NC, C])
        ebias = sb("ebias", [128, TILES, E])
    loads = [(router[:], D[name + "_router"]), (prio[:], D[name + "_prio"]), (sel[:], D[name + "_sel"]),
             (w1[:], D[name + "_w1"]), (w2[:], D[name + "_w2"])] + ([] if one else [(ebias[:], D["L2m_ebias"])])
    lg, eq, hot = (sb(n, [128, TILES, E]) for n in ("lg", "eq", "hot"))
    lg2, hot2, e2, r2 = sb("lg2", [128, TILES, E]), sb("hot2", [128, TILES, E]), sb("e2", [128, TILES]), sb("r2", [128, TILES])
    mx, top, mx2 = sb("mx", [128, TILES]), sb("top", [128, TILES]), sb("mx2", [128, TILES])
    hp, hott = sb("hp", [128, TILES, 128], BF16), sb("hott", [128, NB, T], BF16)
    me = sb("me", [128, NB, NM * T])
    ex, rc, act_ = sb("ex", [128, 2, T]), sb("rc", [128, T]), sb("act", [128, NC, T])
    acc, prod = sb("acc", [128, T]), sb("prod", [128, T])
    n_out = E if one else 1
    lg_full, hot_ready, ht_full, hott_ready, gap, gap_done = (
        ph.count(n) for n in ("lg_full", "hot_ready", "ht_full", "hott_ready", "gap", "gap_done"))
    masks_full, me_by_act, me_by_dve = (ph.count(n) for n in ("masks_full", "me_by_act", "me_by_dve"))
    hm_ready = ph.count("hm_ready", NM if one else 0)
    gv_full, gv_free = ph.count("gv_full", NC), ph.count("gv_free", NC, 2)
    exp_ready, act_ready = ph.count("exp_ready", NC), gv_free
    out_full, x_done = ph.count("out_full", n_out, 1), ph.count("x_done", 1, 1)
    hott_ps = [P[:, 1 + i, :].bitcast(BF16) for i in range(2)]
    norm((ld, loads))
    with nc.Block() as block:
        @block.gpsimd
        def _(pool):
            if one:
                pool.wait_ge(*me_by_act.at(0, NB * NM // 2))
                pool.wait_ge(*me_by_dve.at(0, NB * NM // 2))
                with nc.gpsimd.Fori(0, NB) as b:
                    pool.wait_ge(*gv_free.free(b, 2))
                    for e in range(E):
                        nc.gpsimd.tensor_tensor(hm[:, e, :], seq(G["Z"], b), seq(me, b)[:, e * T:(e + 1) * T], ALU.mult)\
                            .then_inc(*hm_ready.up())

        @block.tensor
        def _(pe):
            mm = nc.tensor.matmul
            pe.wait_ge(*ld.at(0, 16 * len(loads)))
            one_ = G["identb"][0:32, 0:32]
            mm(P[0:32, 7, 0:32], one_, one_, start=True, stop=True).then_inc(out_full.sem, 1)
            for i in range(TILES):
                m = mm(P[:, 0, i * E:(i + 1) * E], G["Z"][:, i // QT, (i % QT) * 128:(i % QT + 1) * 128], router[:],
                       start=True, stop=True)
            m.then_inc(*lg_full.up())
            pe.wait_ge(*hot_ready.at(0, 1))
            for i in range(TILES):
                m = nc.tensor.transpose(hott_ps[i // 8][:, (i % 8) * 128:(i % 8 + 1) * 128], hp[:, i, :], G["identb"][:])
                if i % 8 == 7:
                    m.then_inc(*ht_full.up())
            for i in range(NB * NM):
                if i % (2 * NM) == 0:
                    pe.wait_ge(*hott_ready.at(0, i // (2 * NM) + 1))
                if i >= 4:
                    pe.wait_ge(*(me_by_dve if i % 2 else me_by_act).at(0, (i - 4) // 2 + 1))
                mm(P[:, 4 + i % 4, :], sel[:, i % NM, :], hott[:, i // NM, :], start=True, stop=True).then_inc(*masks_full.up())
            pe.wait_ge(*me_by_act.at(0, NB * NM // 2))
            pe.wait_ge(*me_by_dve.at(0, NB * NM // 2))
            with nc.tensor.Fori(0, NB) as b:
                for c in range(NC):
                    pe.wait_ge(*gv_free.free(b, c + 1))
                    for half in range(2):
                        bank = 2 * (c % 2) + half
                        if one:
                            for e in range(E):
                                if c == half == 0:
                                    pe.wait_ge(*hm_ready.at(b, e + 1))
                                lhs = w1[:, e, half * 512 + c * 128:half * 512 + c * 128 + 128]
                                m = mm(P[:, bank, :], lhs, hm[:, e, :], start=e == 0, stop=e == E - 1)
                        else:
                            m = mm(P[:, bank, :], w1[:, c, half, :], seq(G["Z"], b), start=True, stop=True)
                    m.then_inc(*gv_full.up())
                pe.wait_ge(*gv_free.at(b, NC))
                pe.wait_ge(*x_done.free(b, 1))
                for e in range(n_out):
                    for c in range(NC):
                        m = mm(P[:, 4 + e, :], w2[:, e, c, :] if one else w2[:, c, :], act_[:, c, :],
                               start=c == 0, stop=c == NC - 1)
                    m.then_inc(*out_full.up())

        @block.scalar
        def _(act):
            if not one:
                act.wait_ge(*gap.at(0, 1))
                nc.scalar.activation(e2[:], mx2[:], ACT.Exp).then_inc(*gap_done.up())
            for i in range(0, NB * NM, 2):
                act.wait_ge(*masks_full.at(0, i + 1))
                nc.scalar.copy(me[:, i // NM, (i % NM) * T:(i % NM + 1) * T], P[:, 4 + i % 4, :]).then_inc(*me_by_act.up())
            with nc.scalar.Fori(0, NB) as b:
                for c in range(NC):
                    act.wait_ge(*gv_full.at(b, c + 1))
                    act.wait_ge(*gv_free.free(b, c + 1))
                    nc.scalar.activation(ex[:, c % 2, :], P[:, 2 * (c % 2), :], ACT.Tanh, scale=0.5).then_inc(*exp_ready.up())

        @block.vector
        def _(dve):
            dve.wait_ge(*ld.at(0, 16 * len(loads)))
            nc.vector.memset(acc[:, 0:1], 0.0).then_inc(gv_free.sem, 2)
            dve.wait_ge(gv_free.sem, 2)
            nc.vector.memset(acc[:, 0:1], 0.0).then_inc(x_done.sem, 1)
            dve.wait_ge(x_done.sem, 1)
            dve.wait_ge(*lg_full.at(0, 1))
            ps = P[:, 0, 0:TILES * E].rearrange("p (t e) -> p t e", e=E)
            link(dve, nc.vector.memset(hp[:], 0.0), ahead_step)
            if one:
                link(dve, nc.vector.tensor_copy(lg[:], ps), ahead_step)
                link(dve, one_hot_of_max(nc, dve, 0, ahead_step, lg[:], mx[:], eq[:], prio[:], top[:], hot[:], E), ahead_step)
                nc.vector.tensor_copy(hp[:, :, 0:E], hot[:]).then_inc(*hot_ready.up())
            else:
                link(dve, nc.vector.tensor_tensor(lg[:], ps, ebias[:], ALU.add), ahead_step)
                link(dve, one_hot_of_max(nc, dve, 0, ahead_step, lg[:], mx[:], eq[:], prio[:], top[:], hot[:], E), ahead_step)
                link(dve, nc.vector.scalar_tensor_tensor(out=lg2[:], in0=hot[:], scalar=-BIG, in1=lg[:],
                                                         op0=ALU.mult, op1=ALU.add), ahead_step)
                link(dve, one_hot_of_max(nc, dve, 0, ahead_step, lg2[:], mx2[:], eq[:], prio[:], top[:], hot2[:], E), ahead_step)
                nc.vector.tensor_tensor(mx2[:], mx2[:], mx[:], ALU.subtract).then_inc(*gap.up())
                dve.wait_ge(*gap_done.at(0, 1))
                link(dve, nc.vector.tensor_scalar(r2[:], e2[:], 1.0, None, ALU.add), ahead_step)
                link(dve, nc.vector.reciprocal(r2[:], r2[:]), ahead_step)
                wide = [128, TILES, E]
                link(dve, nc.vector.tensor_tensor(hot2[:], hot2[:], e2[:].unsqueeze(2).to_broadcast(wide), ALU.mult), ahead_step)
                link(dve, nc.vector.tensor_tensor(hot2[:], hot2[:], hot[:], ALU.add), ahead_step)
                link(dve, nc.vector.tensor_tensor(hot[:], hot2[:], r2[:].unsqueeze(2).to_broadcast(wide), ALU.mult), ahead_step)
                part = [hp[:, :, p * E:(p + 1) * E] for p in range(3)]
                link(dve, nc.vector.tensor_copy(part[0], hot[:]), ahead_step)
                link(dve, nc.vector.tensor_tensor(lg[:], hot[:], part[0], ALU.subtract), ahead_step)
                link(dve, nc.vector.tensor_copy(part[1], lg[:]), ahead_step)
                nc.vector.tensor_tensor(part[2], lg[:], part[1], ALU.subtract).then_inc(*hot_ready.up())
            for i in range(2):
                dve.wait_ge(*ht_full.at(0, i + 1))
                nc.vector.tensor_copy(hott[:, 2 * i:2 * i + 2, :].rearrange("p b t -> p (b t)"), hott_ps[i]).then_inc(*hott_ready.up())
            for i in range(1, NB * NM, 2):
                dve.wait_ge(*masks_full.at(0, i + 1))
                nc.vector.tensor_copy(me[:, i // NM, (i % NM) * T:(i % NM + 1) * T], P[:, 4 + i % 4, :]).then_inc(*me_by_dve.up())
            dve.wait_ge(*me_by_act.at(0, NB * NM // 2))
            dve.wait_ge(*me_by_dve.at(0, NB * NM // 2))
            with nc.vector.Fori(0, NB) as b:
                m_b = seq(me, b)
                for c in range(NC):
                    dve.wait_ge(*exp_ready.at(b, c + 1))
                    g, v, e = P[:, 2 * (c % 2), :], P[:, 2 * (c % 2) + 1, :], ex[:, c % 2, :]
                    dve.wait_ge(*gv_free.free(b, c + 2))
                    link(dve, nc.vector.scalar_tensor_tensor(out=rc[:], in0=e, scalar=1.0, in1=g, op0=ALU.add, op1=ALU.mult), step, b)
                    if not one and c < NM:
                        link(dve, nc.vector.tensor_tensor(rc[:], rc[:], m_b[:, c * T:(c + 1) * T], ALU.mult), step, b)
                    nc.vector.scalar_tensor_tensor(out=act_[:, c, :], in0=v, scalar=0.5, in1=rc[:], op0=ALU.mult, op1=ALU.mult)\
                        .then_inc(*gv_free.up())
                x = seq(G["X"], b)
                link(dve, nc.vector.tensor_tensor(x, x, seq(G["Y"], b), ALU.add), step, b)
                if one:
                    for e in range(E):
                        dve.wait_ge(*out_full.at(b, e + 1))
                        link(dve, nc.vector.tensor_tensor(prod[:], P[:, 4 + e, :], m_b[:, e * T:(e + 1) * T], ALU.mult), step, b)
                        ins = nc.vector.tensor_tensor(x, x, prod[:], ALU.add)
                        if e < E - 1:
                            link(dve, ins, step, b)
                        else:
                            ins.then_inc(*x_done.up())
                else:
                    dve.wait_ge(*out_full.at(b, 1))
                    nc.vector.tensor_tensor(x, x, P[:, 4, :], ALU.add).then_inc(*x_done.up())
    ph.done()


def phase_tree(nc, G, D, norm):
    ph = Phase(nc, "L1f")
    P, sb = G["P"], ph.sb
    N = 255
    step = ph.count("step", 10)
    ld, pre_full, pre_done = ph.count("ld"), ph.count("pre_full"), ph.count("pre_done")
    wq, rt, lvT, woT, bias = sb("wq", [128, C]), sb("rt", [128, N]), sb("lvT", [128, 256]), sb("woT", [128, C]), sb("bias", [128, 1])
    gw, lw = sb("gw", [128, N]), sb("lw", [128, 2, C])
    yb, ex, g, og = sb("yb", [128, T]), sb("ex", [128, QT, 256]), sb("g", [128, QT, 256]), sb("og", [128, QT, 256])
    lp = [sb("lp0", [128, QT, 256]), sb("lp1", [128, QT, 256])]
    lt = sb("lt", [128, 2, T])
    loads = [(wq[:], D["L1f_wq"]), (rt[:], D["L1f_rt"]), (lvT[:], D["L1f_lvT"]), (woT[:], D["L1f_woT"]), (bias[:], D["L1f_bias"])]
    yb_ready, z_full, e_ready, lp_ready, lt_full, lt_ready = (
        ph.count(n, k, a) for n, k, a in (("yb_ready", 1, 0), ("z_full", 1, 1), ("e_ready", 1, 0), ("lp_ready", 1, 0),
                                          ("lt_full", 1, 0), ("lt_ready", 1, 0)))
    y_full = ph.count("y_full", 1)
    z = P[:, 0:2, :].rearrange("p b (t n) -> p (b t) n", n=256)
    norm((ld, loads))
    with nc.Block() as block:
        @block.gpsimd
        def _(pool):
            with nc.gpsimd.Fori(0, NB) as b:
                pool.wait_ge(*z_full.free(b, 1))
                nc.gpsimd.tensor_copy(yb[:], seq(G["Y"], b)).then_inc(*yb_ready.up())

        @block.tensor
        def _(pe):
            mm = nc.tensor.matmul
            pe.wait_ge(*ld.at(0, 16 * len(loads)))
            mm(P[:, 0, 0:N], wq[:], rt[:], start=True, stop=True)
            for c in range(2):
                m = mm(P[:, 1, c * C:(c + 1) * C], lvT[:, c * 128:(c + 1) * 128], woT[:], start=True, stop=True)
            m.then_inc(*pre_full.up())
            mm(P[0:32, 7, 0:32], G["identb"][0:32, 0:32], G["identb"][0:32, 0:32], start=True, stop=True).then_inc(z_full.sem, 1)
            pe.wait_ge(*pre_done.at(0, 2))
            with nc.tensor.Fori(0, NB) as b:
                pe.wait_ge(*yb_ready.at(b, 1))
                for t in range(QT):
                    m = mm(z[:, t, 0:N], yb[:, t * 128:(t + 1) * 128], gw[:], start=True, stop=True)
                m.then_inc(*z_full.up())
                pe.wait_ge(*lp_ready.at(b, 1))
                for t in range(QT):
                    for c in range(2):
                        m = nc.tensor.transpose(P[:, 2 + c, t * 128:(t + 1) * 128], lp[1][:, t, c * 128:(c + 1) * 128], G["ident"][:])
                m.then_inc(*lt_full.up())
                pe.wait_ge(*lt_ready.at(b, 1))
                for c in range(2):
                    m = mm(P[:, 4, :], lw[:, c, :], lt[:, c, :], start=c == 0, stop=c == 1)
                m.then_inc(*y_full.up())

        @block.scalar
        def _(act):
            act.wait_ge(*pre_full.at(0, 1))
            nc.scalar.copy(gw[:], P[:, 0, 0:N]).then_inc(*pre_done.up())
            nc.scalar.copy(lw[:], P[:, 1, 0:2 * C].rearrange("p (c n) -> p c n", c=2)).then_inc(*pre_done.up())
            with nc.scalar.Fori(0, NB) as b:
                act.wait_ge(*z_full.at(b, 1))
                nc.scalar.activation(ex[:, :, 0:N], z[:, :, 0:N], ACT.Tanh, scale=0.5).then_inc(*e_ready.up())
                act.wait_ge(*lt_full.at(b, 1))
                nc.scalar.copy(lt[:], P[:, 2:4, :]).then_inc(*lt_ready.up())

        @block.vector
        def _(dve):
            dve.wait_ge(*ld.at(0, 16 * len(loads)))
            with nc.vector.Fori(0, NB) as b:
                dve.wait_ge(*e_ready.at(b, 1))
                link(dve, nc.vector.tensor_scalar(g[:, :, 0:N], ex[:, :, 0:N], 0.5, 0.5, ALU.mult, ALU.add), step, b)
                link(dve, nc.vector.tensor_scalar(og[:, :, 0:N], g[:, :, 0:N], -1.0, 1.0, ALU.mult, ALU.add), step, b)
                nc.vector.tensor_copy(lp[0][:, :, 0:1], og[:, :, 0:1])
                link(dve, nc.vector.tensor_copy(lp[0][:, :, 1:2], g[:, :, 0:1]), step, b)
                for level in range(1, 8):
                    n = 2 ** level
                    old, new = lp[(level - 1) % 2][:, :, 0:n], lp[level % 2][:, :, 0:2 * n].rearrange("p t (n s) -> p t n s", s=2)
                    nc.vector.tensor_tensor(new[:, :, :, 0], old, og[:, :, n - 1:2 * n - 1], ALU.mult)
                    ins = nc.vector.tensor_tensor(new[:, :, :, 1], old, g[:, :, n - 1:2 * n - 1], ALU.mult)
                    if level < 7:
                        link(dve, ins, step, b)
                    else:
                        ins.then_inc(*lp_ready.up())
                dve.wait_ge(*y_full.at(b, 1))
                x = seq(G["X"], b)
                link(dve, nc.vector.scalar_tensor_tensor(out=x, in0=P[:, 4, :], scalar=bias[:, 0:1], in1=x,
                                                         op0=ALU.add, op1=ALU.add), step, b)
    ph.done()


def phase_over_heads(nc, G, D, norm):
    ph = Phase(nc, "L3x")
    P, sb = G["P"], ph.sb
    NSEL, KPER, UNITS = 14, 3, 2 * QT
    ld = ph.count("ld")
    wq, wk, wv, wo = sb("wq", [128, C]), sb("wk", [128, C]), sb("wv", [128, 512]), sb("wo", [128, 4, C])
    selq, selk = sb("selq", [128, 8, 3, 128], BF16), sb("selk", [128, H, 3, 128], BF16)
    loads = [(wq[:], D["L3x_wq"]), (wk[:], D["L3x_wk"]), (wv[:], D["L3x_wv"]), (wo[:], D["L3x_wo"]),
             (selq[:], D["selq"]), (selk[:], D["selk"])]
    ctb = sb("ctb", [128, LK])
    qf, qr, kf, kr = sb("qf", [128, T]), sb("qr", [128, T]), sb("kf", [128, LK]), sb("kr", [128, LK])
    qp, kp = sb("qp", [128, 3, T], BF16), sb("kp", [128, 3, LK], BF16)
    qs, ks = sb("qs", [128, NB, 8 * T], BF16), sb("ks", [128, NB, H * LK], BF16)
    va = sb("va", [KT, 2, 512])
    mx, sm = sb("mx", [KT, 128]), sb("sm", [KT, UNITS, 128])
    ex = sb("ex", [KT, UNITS, H, 128])
    on = sb("on", [128, 4, T])
    ctb_ready, qf_ready, kf_ready = ph.count("ctb_ready", 1), ph.count("qf_ready", 2), ph.count("kf_ready", 2)
    q_full, k_full = (ph.count(n, 1) for n in ("q_full", "k_full"))
    v_full, v_ready, parts_ready = ph.count("v_full", 2, 1), ph.count("v_ready", 2), ph.count("parts_ready", 2)
    ring_full, ring_done = ph.count("ring_full", NSEL), ph.count("ring_done", NSEL, 2)
    step, mx_step, sm_step = ph.count("step", 2), ph.count("mx_step", UNITS), ph.count("sm_step", UNITS)
    st_full, sub_done, exp_done, sum_ready = (ph.count(n, UNITS) for n in ("st_full", "sub_done", "exp_done", "sum_ready"))
    p_ready = ph.count("p_ready", UNITS)
    o_full, on_ready = ph.count("o_full", QT, QT), ph.count("on_ready", QT, 1)
    out_full, x_done = ph.count("out_full", 1), ph.count("x_done", 1, 1)

    sels, order = [("sel", 1, i) for i in range(NSEL)], []
    for u in range(4, UNITS + 4):
        off, v = divmod(u, UNITS)
        before = divmod(u - 1, UNITS)
        aside = {4: [("q", 1, 0), ("k", 1, 0), ("values", 0, 0)], 5: sels[:4], 6: sels[4:5] + [("values", 0, 1)],
                 7: sels[5:], 8: [("values", 0, 2)], 9: [], 10: [("values", 0, 3)],
                 11: [("v", 1, 0), ("v", 1, 1), ("out", 0, 0)]}[u]
        order += [("scores", off, v)] + [s for s in aside if s[0] != "out"] + [("unit", off, v), ("total", *before)]
        order += [s for s in aside if s[0] == "out"]

    def run(engine, one_step):
        for kind, off, n in order:
            if off == 1:
                one_step((-1, 1), kind, n)
        with engine.Fori(0, NB - 1) as t:
            for kind, off, n in order:
                one_step((t, off), kind, n)
        for kind, off, n in order:
            if off == 0:
                one_step((NB - 1, 0), kind, n)

    norm((ld, loads))
    with nc.Block() as block:
        @block.gpsimd
        def _(pool):
            def one_step(b, kind, n):
                if kind == "q":
                    pool.wait_ge(*v_full.free(b, 1))
                    nc.gpsimd.tensor_copy(ctb[:], seq(G["CT"], b)).then_inc(*ctb_ready.up())
                if kind in ("q", "k"):
                    ready, full, rest, part = (qf_ready, qf, qr, qp) if kind == "q" else (kf_ready, kf, kr, kp)
                    pool.wait_ge(*ready.at(b, 2))
                    nc.gpsimd.tensor_tensor(rest[:], full[:], part[:, 0, :], ALU.subtract)
                    link(pool, nc.gpsimd.tensor_tensor(part[:, 1, :], full[:], part[:, 0, :], ALU.subtract), step, b)
                    nc.gpsimd.tensor_tensor(part[:, 2, :], rest[:], part[:, 1, :], ALU.subtract).then_inc(*parts_ready.up())
                elif kind == "total":
                    pool.wait_ge(*sum_ready.at(b, n + 1))
                    nc.gpsimd.tensor_tensor(ex[:, n, :, :], ex[:, n, :, :], sm[:, n, :].unsqueeze(1).to_broadcast([KT, H, 128]),
                                            ALU.mult).then_inc(*p_ready.up())

            run(nc.gpsimd, one_step)

        @block.tensor
        def _(pe):
            mm = nc.tensor.matmul
            pe.wait_ge(*ld.at(0, 16 * len(loads)))
            mm(P[0:32, 7, 0:32], G["identb"][0:32, 0:32], G["identb"][0:32, 0:32], start=True, stop=True).then_inc(v_full.sem, 1)
            mm(P[0:32, 7, 0:32], G["identb"][0:32, 0:32], G["identb"][0:32, 0:32], start=True, stop=True).then_inc(o_full.sem, QT)

            def one_step(b, kind, n):
                if kind == "v":
                    mm(P[0:KT, 5 + n, :], ctb[:, n * KT:(n + 1) * KT], wv[:], start=True, stop=True).then_inc(*v_full.up())
                elif kind == "q":
                    x_done.one_before(pe, b)
                    mm(P[:, 7, :], wq[:], seq(G["Y"], b), start=True, stop=True).then_inc(*q_full.up())
                elif kind == "k":
                    pe.wait_ge(*ctb_ready.at(b, 1))
                    pe.wait_ge(*qf_ready.at(b, 2))
                    mm(P[:, 7, 0:LK], wk[:], ctb[:], start=True, stop=True).then_inc(*k_full.up())
                elif kind == "sel":
                    if n == 0:
                        pe.wait_ge(*parts_ready.at(b, 2))
                        v_ready.before(pe, b)
                    bank = 5 + n % 2
                    pe.wait_ge(*ring_done.free(b, n + 1))
                    if n < 8:
                        for part in range(3):
                            m = mm(P[:, bank, :], selq[:, n, part, :], qp[:, part, :], start=part == 0, stop=part == 2)
                    else:
                        for j, h in enumerate(range((n - 8) * KPER, min(H, (n - 7) * KPER))):
                            for part in range(3):
                                m = mm(P[:, bank, j * LK:(j + 1) * LK], selk[:, h, part, :], kp[:, part, :],
                                       start=part == 0, stop=part == 2)
                    m.then_inc(*ring_full.up())
                elif kind == "scores":
                    qt, kt = divmod(n, 2)
                    if n == 0:
                        pe.wait_ge(*ring_done.at(b, NSEL))
                        sub_done.before(pe, b)
                    else:
                        pe.wait_ge(*sub_done.at(b, n))
                    k_b, q_b = seq(ks, b), seq(qs, b)
                    for h in range(H):
                        m = mm(P[0:KT, h // 4, (h % 4) * 128:(h % 4) * 128 + 128],
                               k_b[:, h * LK + kt * KT:h * LK + (kt + 1) * KT],
                               q_b[:, (h // 2) * T + qt * 128:(h // 2) * T + (qt + 1) * 128], start=True, stop=True)
                    m.then_inc(*st_full.up())
                elif kind == "values":
                    pe.wait_ge(*p_ready.at(b, 2 * n + 2))
                    if n == 0:
                        pe.wait_ge(*v_ready.at(b, 2))
                    pe.wait_ge(*on_ready.free(b, n + 1))
                    for g in range(4):
                        for kt in range(2):
                            for j in range(4):
                                h = 4 * g + j
                                m = mm(P[32 * j:32 * j + 32, 4, g * 128:(g + 1) * 128], va[:, kt, 32 * h:32 * h + 32],
                                       ex[:, 2 * n + kt, h, :], start=kt == 0, stop=kt == 1)
                    m.then_inc(*o_full.up())
                elif kind == "out":
                    pe.wait_ge(*on_ready.at(b, QT))
                    for g in range(4):
                        m = mm(P[:, 7, :], wo[:, g, :], on[:, g, :], start=g == 0, stop=g == 3)
                    m.then_inc(*out_full.up())

            run(nc.tensor, one_step)

        @block.scalar
        def _(act):
            nc.scalar.copy(G["scr"][:, 0:1], G["eps"][:, 0:1]).then_inc(ring_done.sem, 2)
            act.wait_ge(ring_done.sem, 2)
            nc.scalar.copy(G["scr"][:, 0:1], G["eps"][:, 0:1]).then_inc(on_ready.sem, 1)

            def one_step(b, kind, n):
                if kind == "v":
                    act.wait_ge(*v_full.at(b, n + 1))
                    nc.scalar.copy(va[:, n, :], P[0:KT, 5 + n, :]).then_inc(*v_ready.up())
                elif kind == "q":
                    act.wait_ge(*q_full.at(b, 1))
                    nc.scalar.mul(qf[:], P[:, 7, :], 8.0 ** -0.5).then_inc(*qf_ready.up())
                    act.wait_ge(*qf_ready.at(b, 1))
                    nc.scalar.copy(qp[:, 0, :], qf[:]).then_inc(*qf_ready.up())
                elif kind == "k":
                    act.wait_ge(*k_full.at(b, 1))
                    nc.scalar.copy(kf[:], P[:, 7, 0:LK]).then_inc(*kf_ready.up())
                    nc.scalar.copy(kp[:, 0, :], P[:, 7, 0:LK]).then_inc(*kf_ready.up())
                elif kind == "sel":
                    act.wait_ge(*ring_full.at(b, n + 1))
                    if n < 8:
                        m = nc.scalar.copy(seq(qs, b)[:, n * T:(n + 1) * T], P[:, 5 + n % 2, :])
                    else:
                        h0, w = (n - 8) * KPER, min(H, (n - 7) * KPER) - (n - 8) * KPER
                        m = nc.scalar.copy(seq(ks, b)[:, h0 * LK:(h0 + w) * LK], P[:, 5 + n % 2, 0:w * LK])
                    m.then_inc(*ring_done.up())
                elif kind == "unit":
                    act.wait_ge(*sub_done.at(b, n + 1))
                    nc.scalar.activation(ex[:, n, :, :], ex[:, n, :, :], ACT.Exp).then_inc(*exp_done.up())
                elif kind == "values":
                    act.wait_ge(*o_full.at(b, n + 1))
                    nc.scalar.copy(on[:, :, n * 128:(n + 1) * 128], P[:, 4, :].rearrange("p (g q) -> p g q", q=128))\
                        .then_inc(*on_ready.up())

            run(nc.scalar, one_step)

        @block.vector
        def _(dve):
            nc.vector.memset(mx[:, 0:1], 0.0).then_inc(x_done.sem, 1)
            dve.wait_ge(x_done.sem, 1)
            scores = P[0:KT, 0:4, :].rearrange("p b (j q) -> p (b j) q", q=128)

            def one_step(b, kind, n):
                if kind == "unit":
                    dve.wait_ge(*st_full.at(b, n + 1))
                    if n:
                        dve.wait_ge(*sub_done.at(b, n))
                    else:
                        sub_done.before(dve, b)
                    link(dve, nc.vector.tensor_reduce(mx[:], scores.rearrange("p h q -> p q h"), AX.X, ALU.max), mx_step, b)
                    dve.wait_ge(*o_full.free(b, n // 2 + 1))
                    nc.vector.tensor_tensor(ex[:, n, :, :], scores, mx[:].unsqueeze(1).to_broadcast([KT, H, 128]),
                                            ALU.subtract).then_inc(*sub_done.up())
                elif kind == "total":
                    dve.wait_ge(*exp_done.at(b, n + 1))
                    link(dve, nc.vector.tensor_reduce(sm[:, n, :], ex[:, n, :, :].rearrange("p h q -> p q h"), AX.X, ALU.add), sm_step, b)
                    nc.vector.reciprocal(sm[:, n, :], sm[:, n, :]).then_inc(*sum_ready.up())
                elif kind == "out":
                    dve.wait_ge(*out_full.at(b, 1))
                    x = seq(G["X"], b)
                    nc.vector.tensor_tensor(x, x, P[:, 7, :], ALU.add).then_inc(*x_done.up())

            run(nc.vector, one_step)
    ph.done()


def phase_output(nc, G, D, norm):
    ph = Phase(nc, "out")
    P, sb = G["P"], ph.sb
    ROUND = 1.5 * 2.0 ** 23
    ld = ph.count("ld")
    rhs, rt, rs, ri, rqT, rq = (sb("rhs", [128, C]), sb("rt", [128, C]), sb("rs", [128, 1]), sb("ri", [128, 1]),
                                sb("rqT", [128, C], BF16), sb("rq", [128, C], BF16))
    diag, rsb = sb("diag", [128, 128]), sb("rsb", [128, 128])
    zb, xb = sb("zb", [128, T]), sb("xb", [128, T])
    amax, sc, inv = sb("amax", [128, QT]), sb("sc", [128, QT]), sb("inv", [128, QT])
    qz, qb, qt_ = sb("qz", [128, QT, 128]), sb("qb", [128, QT, 128], BF16), sb("qt", [128, T], BF16)
    o = sb("o", [128, NB * QT, C])
    pre, pre_pe, pstep = ph.count("pre"), ph.count("pre_pe"), ph.count("pstep")
    step = ph.count("step", 7)
    b_ready, z_full, q_ready, qt_full, qt_done = (ph.count(n, k, a) for n, k, a in (
        ("b_ready", 2, 0), ("z_full", 1, 0), ("q_ready", 1, 0), ("qt_full", 1, 0), ("qt_done", 1, 0)))
    y_full, o_ready, stored = ph.count("y_full", 1, 1), ph.count("o_ready", 1), ph.count("stored", 16)
    loads = [(rhs[:], D["L3f_rhs"])]
    qview = P[:, 1, 0:256].bitcast(BF16)
    wide = [128, QT, 128]
    norm((ld, loads))
    with nc.Block() as block:
        @block.sync
        def _(sp):
            with nc.sync.Fori(0, NB) as b:
                sp.wait_ge(*o_ready.at(b, 1))
                sp.dma_start(D["out"][:, bass.ds(b * QT, QT), :], o[:, bass.ds(b * QT, QT), :]).then_inc(*stored.up(16))
            sp.wait_ge(stored.sem, 16 * NB)

        @block.gpsimd
        def _(pool):
            with nc.gpsimd.Fori(0, NB) as b:
                pool.wait_ge(*y_full.free(b, 1))
                nc.gpsimd.tensor_copy(zb[:], seq(G["Z"], b)).then_inc(*b_ready.up())
                nc.gpsimd.tensor_copy(xb[:], seq(G["X"], b)).then_inc(*b_ready.up())

        @block.tensor
        def _(pe):
            mm = nc.tensor.matmul
            pe.wait_ge(*ld.at(0, 16 * len(loads)))
            nc.tensor.transpose(P[:, 0, 0:128], rhs[:], G["ident"][:]).then_inc(*pre_pe.up())
            pe.wait_ge(*pre.at(0, 1))
            nc.tensor.transpose(qview[:, 0:128], rqT[:], G["identb"][:])
            mm(P[:, 2, 0:128], G["mean"][:], diag[:], start=True, stop=True).then_inc(*pre_pe.up())
            mm(P[0:32, 7, 0:32], G["identb"][0:32, 0:32], G["identb"][0:32, 0:32], start=True, stop=True).then_inc(y_full.sem, 1)
            pe.wait_ge(*pre.at(0, 2))
            with nc.tensor.Fori(0, NB) as b:
                pe.wait_ge(*b_ready.at(b, 1))
                for t in range(QT):
                    m = nc.tensor.transpose(P[:, 0, t * 128:(t + 1) * 128], zb[:, t * 128:(t + 1) * 128], G["ident"][:])
                m.then_inc(*z_full.up())
                pe.wait_ge(*q_ready.at(b, 1))
                for t in range(QT):
                    m = nc.tensor.transpose(qview[:, t * 128:(t + 1) * 128], qb[:, t, :], G["identb"][:])
                m.then_inc(*qt_full.up())
                pe.wait_ge(*qt_done.at(b, 1))
                pe.wait_ge(*b_ready.at(b, 2))
                for t in range(QT):
                    mm(P[:, 2, t * 128:(t + 1) * 128], qt_[:, t * 128:(t + 1) * 128], rq[:], start=True, stop=True)
                for t in range(QT):
                    m = nc.tensor.transpose(P[:, 3, t * 128:(t + 1) * 128], xb[:, t * 128:(t + 1) * 128], G["ident"][:])
                m.then_inc(*y_full.up())

        @block.scalar
        def _(act):
            with nc.scalar.Fori(0, NB) as b:
                act.wait_ge(*qt_full.at(b, 1))
                nc.scalar.copy(qt_[:], qview).then_inc(*qt_done.up())

        @block.vector
        def _(dve):
            def plink(ins):
                link(dve, ins, pstep)
            dve.wait_ge(*pre_pe.at(0, 1))
            plink(nc.vector.tensor_reduce(rs[:], P[:, 0, 0:128], AX.X, ALU.max, apply_absolute_value=True))
            plink(nc.vector.tensor_scalar(rs[:], rs[:], 1e-12, 1.0 / 127.0, ALU.max, ALU.mult))
            plink(nc.vector.reciprocal(ri[:], rs[:]))
            plink(nc.vector.tensor_scalar(rt[:], P[:, 0, 0:128], ri[:, 0:1], None, ALU.mult))
            plink(nc.vector.tensor_scalar(rt[:], rt[:], ROUND, ROUND, ALU.add, ALU.subtract))
            plink(nc.vector.tensor_scalar(diag[:], G["ident"][:], rs[:, 0:1], 128.0, ALU.mult, ALU.mult))
            nc.vector.tensor_scalar(rqT[:], rt[:], 127.0, -127.0, ALU.min, ALU.max).then_inc(*pre.up())
            dve.wait_ge(*pre_pe.at(0, 2))
            plink(nc.vector.tensor_copy(rq[:], qview[:, 0:128]))
            nc.vector.tensor_copy(rsb[:], P[:, 2, 0:128]).then_inc(*pre.up())
            dve.wait_ge(*pre.at(0, 2))
            with nc.vector.Fori(0, NB) as b:
                dve.wait_ge(*z_full.at(b, 1))
                zt = P[:, 0, :].rearrange("p (t c) -> p t c", c=128)
                link(dve, nc.vector.tensor_reduce(amax[:], zt, AX.X, ALU.max, apply_absolute_value=True), step, b)
                link(dve, nc.vector.tensor_scalar(sc[:], amax[:], 1e-12, 1.0 / 127.0, ALU.max, ALU.mult), step, b)
                link(dve, nc.vector.reciprocal(inv[:], sc[:]), step, b)
                link(dve, nc.vector.tensor_tensor(qz[:], zt, inv[:].unsqueeze(2).to_broadcast(wide), ALU.mult), step, b)
                link(dve, nc.vector.tensor_scalar(qz[:], qz[:], ROUND, ROUND, ALU.add, ALU.subtract), step, b)
                nc.vector.tensor_scalar(qb[:], qz[:], 127.0, -127.0, ALU.min, ALU.max).then_inc(*q_ready.up())
                dve.wait_ge(*y_full.at(b, 1))
                y = P[:, 2, :].rearrange("p (t c) -> p t c", c=128)
                link(dve, nc.vector.tensor_tensor(qz[:], y, sc[:].unsqueeze(2).to_broadcast(wide), ALU.mult), step, b)
                link(dve, nc.vector.tensor_tensor(qz[:], qz[:], rsb[:].unsqueeze(1).to_broadcast(wide), ALU.mult), step, b)
                nc.vector.tensor_tensor(o[:, bass.ds(b * QT, QT), :], qz[:], P[:, 3, :].rearrange("p (t c) -> p t c", c=128),
                                        ALU.add).then_inc(*o_ready.up())
    ph.done()


def build(nc, D):
    ctx = ExitStack()
    with ctx:
        def sb(name, shape, dt=F32):
            return ctx.enter_context(nc.sbuf_tensor(name, shape, dt))
        G = {"X": sb("X", [128, NB, T]), "Y": sb("Y", [128, NB, T]), "Z": sb("Z", [128, NB, T]),
             "CT": sb("CT", [128, NB, LK]), "ident": sb("ident", [128, 128]), "identb": sb("identb", [128, 128], BF16),
             "mean": sb("mean", [128, 128]), "eps": sb("eps", [128, 2]), "zero": sb("zero", [128, 1]), "scr": sb("scr", [128, 2]),
             "P": ctx.enter_context(nc.psum_tensor("P", [128, 8, 512], F32))}
        phase_input(nc, G, D)
        X, Y, Z = G["X"], G["Y"], G["Z"]
        phase_latent(nc, G, D, "L0x", lambda fetch: phase_norm(nc, G, "n0x", X, Y, fetch=fetch))
        phase_norm(nc, G, "n0f", X, Y)
        phase_conv_attention(nc, G, D, lambda fetch: phase_norm(nc, G, "n0a", Y, Z, gain=D["L0_ln1_w"], bias=D["L0_ln1_b"], fetch=fetch))
        phase_experts(nc, G, D, "L0m", lambda fetch: phase_norm(nc, G, "n0m", Y, Z, gain=D["L0_ln2_w"], bias=D["L0_ln2_b"], fetch=fetch))
        phase_cross(nc, G, D, "L1x", lambda fetch: phase_norm(nc, G, "n1x", X, Y, fetch=fetch))
        phase_tree(nc, G, D, lambda fetch: phase_norm(nc, G, "n1f", X, Y, fetch=fetch))
        phase_cross(nc, G, D, "L2x", lambda fetch: phase_norm(nc, G, "n2x", X, Y, fetch=fetch))
        phase_norm(nc, G, "n2f", X, Y)
        phase_latent(nc, G, D, "L2f", lambda fetch: phase_norm(nc, G, "n2a", Y, Z, center=False, gain=D["L2_w_ln1"], fetch=fetch))
        phase_experts(nc, G, D, "L2m", lambda fetch: phase_norm(nc, G, "n2m", Y, Z, center=False, gain=D["L2_w_ln2"], fetch=fetch))
        phase_over_heads(nc, G, D, lambda fetch: phase_norm(nc, G, "n3x", X, Y, fetch=fetch))
        phase_output(nc, G, D, lambda fetch: phase_norm(nc, G, "n3f", X, Z, fetch=fetch))


def lay_out(i):
    f32, bf = np.float32, mybir.dt.np(BF16)
    d = {}
    tok = lambda a: np.ascontiguousarray(a.reshape(-1, 128, a.shape[-1]).transpose(1, 0, 2))
    col = lambda a: np.ascontiguousarray(a.reshape(-1, 1))
    d["x"] = tok(i["x"])
    d["ctx"] = np.ascontiguousarray(i["ctx_1024"].reshape(NB * 2, KT, C).transpose(1, 0, 2))
    d["ident"] = np.eye(128, dtype=f32)
    d["identb"] = np.eye(128).astype(bf)
    d["mean"] = np.full((128, 128), 1 / 128, f32)
    d["eps"] = np.full((128, 2), EPS, f32)

    qpart, kpart = (0, 0, 1, 0, 2, 1), (0, 1, 0, 2, 0, 1)
    selq, selk = np.zeros((128, 8, 3, 128), f32), np.zeros((128, H, 3, 128), f32)
    selm = np.zeros((128, H, 128), f32)
    seld = np.zeros((128, 4), f32)
    selr = np.zeros((128, 4, 4, 32), f32)
    for h in range(H):
        for c in range(6):
            for e in range(8):
                row = 64 * (h % 2) + 8 * c + e
                selq[8 * h + e, h // 2, qpart[c], row] = 1
                selk[8 * h + e, h, kpart[c], row] = 1
        for p in range(3):
            selm[16 * p + h, h, :] = 1
            selr[16 * p + h, h // 4, h % 4, :] = 1
    for j in range(4):
        seld[32 * j + 8, j] = 1
    d["selq"], d["selk"], d["selm"] = selq.astype(bf), selk.astype(bf), selm.astype(bf)
    d["selr"] = selr.reshape(128, 4, 128).astype(bf)
    d["seld"] = seld

    def spread_cols(w):
        n, e = w.shape[0], w.shape[1] // H
        out = np.zeros((n, H, 32), w.dtype)
        out[:, :, :e] = w.reshape(n, H, e)
        return out.reshape(n, H * 32)

    def spread_rows(w):
        return np.ascontiguousarray(spread_cols(w.T).T.reshape(4, 128, C).transpose(1, 0, 2))

    def values_bias(b):
        out = spread_cols(b.reshape(1, -1)).reshape(H, 32)
        out[:, 8] = 1
        return np.ascontiguousarray(np.broadcast_to(out.reshape(1, -1), (KT, 512)))

    def block_diagonal(w):
        out = np.zeros((H, 8, H, 8), w.dtype)
        for h in range(H):
            out[h, :, h, :] = w[h]
        return out.reshape(C, C)

    p = "L1_xattn_"
    d["L1x_wq"], d["L1x_wk"] = (np.ascontiguousarray(i[p + w].T) for w in ("w_q", "w_k"))
    d["L1x_wv"], d["L1x_wo"] = spread_cols(i[p + "w_v"].T), spread_rows(np.ascontiguousarray(i[p + "w_o"].T))
    d["L1x_bq"], d["L1x_bk"], d["L1x_bo"] = (col(i[p + b]) for b in ("b_q", "b_k", "b_o"))
    d["L1x_bv"] = values_bias(i[p + "b_v"])

    d["zero"] = np.zeros((128, 1), f32)
    k, q = np.arange(128)[:, None], np.arange(128)[None, :]
    d["mask_k"] = np.where(k > q, -BIG, 0).astype(f32).astype(bf)
    d["mask_q"] = np.ascontiguousarray(d["mask_k"].T)

    def rope(n, half, base, pos_exp):
        inv = (1.0 / np.float32(base) ** pos_exp.astype(f32)).astype(f32)
        ang = (np.arange(n, dtype=f32)[None, :] * inv[:, None]).astype(f32)
        return np.cos(ang).astype(f32), np.sin(ang).astype(f32)

    cos, sin = rope(T, 4, 10000.0, np.arange(0, 8, 2) / 8)
    cos8, sin8 = np.tile(cos, (32, 1)), np.tile(np.concatenate([-sin, sin]), (16, 1))
    s8 = f32(8.0) ** f32(-0.5)
    d["L0f_cq"], d["L0f_sq"], d["L0f_ck"], d["L0f_sk"] = cos8 * s8, sin8 * s8, cos8, sin8
    p = "L0_ffn_"
    d["L0f_conv"] = np.ascontiguousarray(i[p + "conv_w"][:, 0, :])
    wq, wk, wv = np.split(i[p + "attn_w"], 3, axis=1)
    swap = np.arange(C).reshape(16, 2, 4)[:, ::-1].reshape(-1)
    d["L0f_wq"], d["L0f_wqr"], d["L0f_wk"], d["L0f_wkr"] = wq, wq[:, swap], wk, wk[:, swap]
    d["L0f_wv"], d["L0f_wo"] = spread_cols(wv), spread_rows(i[p + "proj_w"])
    d["L0f_bv"] = np.ascontiguousarray(np.broadcast_to(values_bias(np.zeros(C, f32))[0:1], (128, 512)))
    for n in ("ln1_w", "ln1_b", "ln2_w", "ln2_b"):
        d["L0_" + n] = col(i[p + n])

    def padded(a, shape, at=(0, 0)):
        out = np.zeros(shape, a.dtype)
        out[tuple(slice(o, o + n) for o, n in zip(at, a.shape))] = a
        return out

    p = "L0_xattn_"
    wa, wb = np.zeros((128, H, 128), f32), np.zeros((128, 8, 128), f32)
    qr = i[p + "w_q_rope"].reshape(48, H, 64)
    wa[:48, :, :64] = qr
    wb[:48] = qr.reshape(48, H, 2, 32)[:, :, ::-1].reshape(48, 8, 128)
    d["L0x_wa"], d["L0x_wb"] = wa, wb
    d["L0x_wqd"] = padded(i[p + "w_q_down"], (128, 128))
    d["L0x_wqT"] = i[p + "w_q_up"].reshape(48, H, 64).transpose(2, 1, 0)
    d["L0x_wkT"] = i[p + "w_k_up"].reshape(32, H, 64).transpose(2, 1, 0)
    d["L0x_wvT"] = i[p + "w_v_up"].reshape(32, H, 64).transpose(2, 1, 0)
    d["L0x_woh"] = i[p + "w_out"].reshape(H, 64, C).transpose(1, 0, 2)
    wka = padded(i[p + "w_k_rope"], (128, 128))
    wka[:32, 64:96] = np.eye(32)
    d["L0x_wka"] = wka
    d["L0x_wkb"] = padded(i[p + "w_k_rope"].reshape(32, 2, 32)[:, ::-1].reshape(32, 64), (128, 128))
    d["L0x_wlat"] = padded(i[p + "w_kv_comp"], (128, 128))
    cos, sin = rope(T, 32, 10000.0, np.arange(32) / 32)
    s128 = f32(1.0) / np.sqrt(128).astype(f32)
    rc, rs = np.tile(cos, (2, 1)), np.concatenate([-sin, sin])
    one = np.ones((32, T), f32)
    d["L0x_cq"] = padded(np.concatenate([rc, one]) * s128, (128, T))
    d["L0x_sq"] = np.tile(rs, (2, 1)) * s128
    d["L0x_ck"] = padded(np.concatenate([rc, one])[:, :LK], (128, LK))
    d["L0x_sk"] = padded(rs[:, :LK], (128, LK))
    seg = i["itok_BxS_0_511"]
    d["segc"] = np.ascontiguousarray(seg.reshape(NB * QT, 128).T)
    d["keyrow"] = np.ascontiguousarray(np.broadcast_to(np.arange(1, LK + 1, dtype=f32), (128, LK)))

    p = "L2_ffn_"
    wq = i[p + "Wq"].reshape(C, H, 64)
    flip = np.arange(32).reshape(16, 2)[:, ::-1].reshape(-1)
    wa = np.zeros((128, H, 128), f32)
    wa[:, :, :32] = wq[:, :, 32:]
    d["L2f_wa"], d["L2f_wb"] = wa, wq[:, :, 32:][:, :, flip].reshape(C, 4, 128)
    d["L2f_wqT"] = wq[:, :, :32].transpose(2, 1, 0)
    kvb = i[p + "Wkvb"].reshape(16, H, 32).transpose(2, 1, 0)
    d["L2f_wkT"] = kvb
    d["L2f_wvT"] = padded(kvb, (32, H, 32), (0, 0, 0))
    d["L2f_woh"] = i[p + "Wo"].reshape(H, 64, C)[:, :32].transpose(1, 0, 2)
    kva = i[p + "Wkva"]
    d["L2f_wka"] = padded(np.concatenate([kva[:, 16:], kva[:, :16]], 1), (128, 128))
    d["L2f_wkb"] = padded(kva[:, 16:][:, flip], (128, 128))
    d["L2f_wlat"] = kva[:, :16]
    cos, sin = rope(T, 16, 100000.0, np.arange(0, 32, 2) / 32)
    rc = np.repeat(cos, 2, axis=0)
    rs = np.stack([-sin, sin], 1).reshape(32, T)
    one = np.ones((16, T), f32)
    d["L2f_cq"] = padded(np.concatenate([rc, one]) * f32(0.125), (128, T))
    d["L2f_sq"] = np.tile(rs, (4, 1)) * f32(0.125)
    d["L2f_ck"] = padded(np.concatenate([rc, one]), (128, T))
    d["L2f_sk"] = padded(rs, (128, T))
    d["L2_w_ln1"], d["L2_w_ln2"] = col(i[p + "w_ln1"]), col(i[p + "w_ln2"])

    p = "L2_xattn_"
    d["L2x_wq"], d["L2x_wk"] = (block_diagonal(i[p + w]) for w in ("Wq", "Wk"))
    d["L2x_wv"], d["L2x_wo"] = spread_cols(block_diagonal(i[p + "Wv"])), spread_rows(i[p + "Wo"])
    d["L2x_bq"], d["L2x_bk"], d["L2x_bo"] = (col(i[p + b]) for b in ("bq", "bk", "bo"))
    d["L2x_bv"] = values_bias(i[p + "bv"].reshape(-1))

    p = "L0_ffn_"
    d["L0m_router"] = i[p + "router_w"]
    d["L0m_w1"] = i[p + "expert_wv"].transpose(1, 0, 2)
    d["L0m_w2"] = i[p + "expert_proj"].reshape(4, 4, 128, C).transpose(2, 0, 1, 3)
    p = "L2_ffn_"
    d["L2m_router"] = i[p + "Wgate"]
    w1, w2 = np.zeros((128, 5, 2, 2, 64), f32), np.zeros((2, 64, 5, C), f32)
    for e in range(8):
        w1[:, e // 2, 0, e % 2], w1[:, e // 2, 1, e % 2] = i[p + "Wg"][e], i[p + "Wu"][e]
        w2[e % 2, :, e // 2] = i[p + "Wd"][e]
    w1[:, 4, 0, 0], w1[:, 4, 1, 0], w2[0, :, 4] = i[p + "sWg"][0], i[p + "sWu"][0], i[p + "sWd"][0]
    d["L2m_w1"], d["L2m_w2"] = w1.reshape(128, 5, 2, 128), w2.reshape(128, 5, C)
    d["L2m_ebias"] = np.broadcast_to(i[p + "expert_bias"], (128, NB * QT, 8))
    for n, e in (("L0m", 4), ("L2m", 8)):
        d[n + "_prio"] = np.broadcast_to(np.arange(e, 0, -1, dtype=f32), (128, NB * QT, e))
        sel = np.zeros((128, 4, 128), f32)
        sel[:3 * e] = np.tile(np.repeat(np.eye(e, dtype=f32), 128 if e == 4 else 64, axis=1).reshape(e, 4, 128), (3, 1, 1))
        d[n + "_sel"] = sel.astype(bf)

    p = "L1_ffn_"
    d["L1f_wq"], d["L1f_rt"], d["L1f_lvT"], d["L1f_woT"] = (
        i[p + "Wq"], i[p + "routers"].T, i[p + "leaf_values"].T, i[p + "Wout_w"].T)
    d["L1f_bias"] = col(i[p + "Wout_b"])
    p = "L3_xattn_"
    d["L3x_wq"], d["L3x_wk"] = i[p + "Wq"].T, i[p + "Wk"].T
    d["L3x_wv"], d["L3x_wo"] = spread_cols(i[p + "Wv"].T), spread_rows(i[p + "Wo"].T)
    d["L3f_rhs"] = i["L3_ffn_rhs"]
    return d


def kernel(**inputs):
    import concourse.bacc as bacc
    from concourse.bass_utils import run_bass_kernel_spmd

    nc = bacc.Bacc("TRN2", target_bir_lowering=False, num_devices=1)
    arrays = {"in_" + k: np.ascontiguousarray(v) for k, v in lay_out({k: np.asarray(v) for k, v in inputs.items()}).items()}
    D = {k[3:]: nc.dram_tensor(k, a.shape, mybir.dt.from_np(a.dtype), kind="ExternalInput").ap() for k, a in arrays.items()}
    D["out"] = nc.dram_tensor("out_0", (128, NB * QT, C), F32, kind="ExternalOutput").ap()
    build(nc, D)
    r = run_bass_kernel_spmd(nc, [arrays], core_ids=[0])
    return np.ascontiguousarray(r.results[0]["out_0"].transpose(1, 0, 2)).reshape(NB, T, C)
```
